# Optimizing a Trainium2 kernel written in Bass

```python
import numpy as np
import jax
import jax.numpy as jnp

def _softmax(x, axis=-1):
    return jax.nn.softmax(x, axis=axis)

def _gelu(x):
    return jax.nn.gelu(x, approximate=True)

def _silu(x):
    return jax.nn.silu(x)

def _sigmoid(x):
    return jax.nn.sigmoid(x)

def _layernorm(x, axis=-1, eps=1e-05):
    m = jnp.mean(x, axis=axis, keepdims=True)
    v = jnp.var(x, axis=axis, keepdims=True)
    return (x - m) / jnp.sqrt(v + eps)

def _scatter_add(tgt, idx, src, axis=0):
    return tgt.at[idx].add(src)

def _segment_sum(src, seg, n):
    return jax.ops.segment_sum(src, seg, n)
kernel_name = 'mk_flamingo_gated_d2_seqx_r8_8e7300'

def setup_inputs(seed: int=0):
    np.random.seed(seed)
    _w = jnp.asarray

    def _rec_inputs():
        import jax
        import jax.numpy as jnp
        _rk = jax.random.key(seed)
        x = 7.22e-05 + 1 * jax.random.normal(jax.random.fold_in(_rk, 1), (64, 64, 128), jnp.float32)
        _lenS = 64 - jax.random.randint(jax.random.fold_in(_rk, 7), (64,), 0, max(1, 64 // 4) + 1, jnp.int32)
        _lenS2 = 64 - jax.random.randint(jax.random.fold_in(_rk, 8), (64,), 0, max(1, 64 // 4) + 1, jnp.int32)
        _ctx_1024P = jax.random.normal(jax.random.fold_in(_rk, 11), (64, 16, 128), jnp.float32)
        _ctx_1024c = jax.random.dirichlet(jax.random.fold_in(_rk, 511), 0.3 * jnp.ones((16,), jnp.float32), (64, 64))
        _ctx_1024t = jnp.einsum('bsk,bkd->bsd', _ctx_1024c, _ctx_1024P)
        _ctx_1024t = _ctx_1024t * jax.lax.rsqrt(jnp.mean(jnp.square(_ctx_1024t)) + 1e-12) * 0.953939
        ctx_1024 = 4.13588e-05 + 0.999923 * (_ctx_1024t + 0.3 * jax.random.normal(jax.random.fold_in(_rk, 611), (64, 64, 128), jnp.float32))
        _g = jax.random.normal(jax.random.fold_in(_rk, 9001), (2, 2), jnp.float32)
        _g = jnp.sign(_g) * jnp.maximum(jnp.abs(_g), 1.0) + (_g == 0) * 1.0
        g_xattn = _g[0]
        g_ffn = _g[1]
        return (x, ctx_1024, g_xattn, g_ffn)
    x, ctx_1024, g_xattn, g_ffn = _rec_inputs()

    def _L0_xattn_setup():
        import math
        import jax, jax.numpy as jnp
        import numpy as np
        EMB_DIM = 128
        CFG_N_HEADS = 16
        N_HEADS = CFG_N_HEADS if CFG_N_HEADS >= EMB_DIM else 1
        key = jax.random.key(seed)
        ks = jax.random.split(key, 11)
        B, T, C = (4, 256, EMB_DIM)
        s = 1.0 / math.sqrt(C)
        return {'q': jax.random.normal(ks[0], (B, T, C), jnp.float32), 'k': jax.random.normal(ks[1], (B, T, C), jnp.float32), 'v': jax.random.normal(ks[2], (B, T, C), jnp.float32), 'Wq': jax.random.normal(ks[3], (C, C), jnp.float32) * s, 'bq': jax.random.normal(ks[4], (C,), jnp.float32) * s, 'Wk': jax.random.normal(ks[5], (C, C), jnp.float32) * s, 'bk': jax.random.normal(ks[6], (C,), jnp.float32) * s, 'Wv': jax.random.normal(ks[7], (C, C), jnp.float32) * s, 'bv': jax.random.normal(ks[8], (C,), jnp.float32) * s, 'Wff': jax.random.normal(ks[9], (C, C), jnp.float32) * s, 'bff': jax.random.normal(ks[10], (C,), jnp.float32) * s}
    _L0_xattn_all = _L0_xattn_setup()
    _L0_xattn_in = {k: v for k, v in _L0_xattn_all.items() if k in ('Wq', 'bq', 'Wk', 'bk', 'Wv', 'bv', 'Wff', 'bff')}
    del _L0_xattn_all

    def _L0_ffn_setup():
        import jax, jax.numpy as jnp
        import numpy as np
        D_MODEL = 128
        D1, D2 = (32, 32)
        F1, F2 = (64, 64)
        E = 64
        TOP_K = 2

        def kmoe(x_flat, W_router, A, B, scale, bias, d_in1, d_in2, d_out1, d_out2, top_k):
            logits = x_flat @ W_router.T
            vals, idx = jax.lax.top_k(logits, top_k)
            probs = jax.nn.softmax(vals, axis=-1)
            xs = x_flat.reshape(-1, d_in1, d_in2)
            Ag = A[idx]
            Bg = B[idx]
            Y = jnp.einsum('nkoi,nij,nkpj->nkop', Ag, xs, Bg)
            out = jnp.einsum('nkop,nk->nop', Y, probs).reshape(-1, d_out1 * d_out2)
            return out * scale + bias
        key = jax.random.key(seed)
        ks = jax.random.split(key, 12)
        s = 0.02
        return {'x': jax.random.normal(ks[0], (4, 256, D_MODEL), dtype=jnp.float32), 'W_up': jax.random.normal(ks[1], (E, D1 * D2), dtype=jnp.float32) * s, 'A_up': jax.random.normal(ks[2], (E, F1, D1), dtype=jnp.float32) * s, 'B_up': jax.random.normal(ks[3], (E, F2, D2), dtype=jnp.float32) * s, 'scale_up': jnp.ones((1,), dtype=jnp.float32), 'bias_up': jnp.zeros((F1 * F2,), dtype=jnp.float32), 'W_down': jax.random.normal(ks[4], (E, F1 * F2), dtype=jnp.float32) * s, 'A_down': jax.random.normal(ks[5], (E, D1, F1), dtype=jnp.float32) * s, 'B_down': jax.random.normal(ks[6], (E, D2, F2), dtype=jnp.float32) * s, 'scale_down': jnp.ones((1,), dtype=jnp.float32), 'bias_down': jnp.zeros((D1 * D2,), dtype=jnp.float32)}
    _L0_ffn_all = _L0_ffn_setup()
    _L0_ffn_in = {k: v for k, v in _L0_ffn_all.items() if k in ('W_up', 'A_up', 'B_up', 'scale_up', 'bias_up', 'W_down', 'A_down', 'B_down', 'scale_down', 'bias_down')}
    del _L0_ffn_all

    def _L1_xattn_setup():
        import jax, jax.numpy as jnp
        import numpy as np
        EMBED_DIM = 128
        BATCH = 4
        SEQ = 256
        key = jax.random.key(seed)
        ks = jax.random.split(key, 9)
        shape = (BATCH, SEQ, EMBED_DIM)
        lim = 1.0 / np.sqrt(EMBED_DIM)
        return {'query': jax.random.normal(ks[0], shape, dtype=jnp.float32), 'key': jax.random.normal(ks[1], shape, dtype=jnp.float32), 'value': jax.random.normal(ks[2], shape, dtype=jnp.float32), 'Wq': jax.random.uniform(ks[3], (EMBED_DIM, EMBED_DIM), jnp.float32, -lim, lim), 'bq': jax.random.uniform(ks[4], (EMBED_DIM,), jnp.float32, -lim, lim), 'Wk': jax.random.uniform(ks[5], (EMBED_DIM, EMBED_DIM), jnp.float32, -lim, lim), 'bk': jax.random.uniform(ks[6], (EMBED_DIM,), jnp.float32, -lim, lim), 'Wv': jax.random.uniform(ks[7], (EMBED_DIM, EMBED_DIM), jnp.float32, -lim, lim), 'bv': jax.random.uniform(ks[8], (EMBED_DIM,), jnp.float32, -lim, lim)}
    _L1_xattn_all = _L1_xattn_setup()
    _L1_xattn_in = {k: v for k, v in _L1_xattn_all.items() if k in ('Wq', 'bq', 'Wk', 'bk', 'Wv', 'bv')}
    del _L1_xattn_all

    def _L1_ffn_setup():
        import jax, jax.numpy as jnp
        import numpy as np
        TOP_K = 2
        key = jax.random.key(seed)
        ks = jax.random.split(key, 7)
        B_, S, D, F, E, R = (2, 256, 128, 512, 4, 4)
        x = jax.random.normal(ks[0], (B_, S, D), dtype=jnp.float32)
        Wg = jax.random.normal(ks[1], (E, D), dtype=jnp.float32) * (1.0 / np.sqrt(D))
        bg = jnp.zeros((E,), dtype=jnp.float32)
        Wi = jax.random.normal(ks[2], (F, D), dtype=jnp.float32) * (1.0 / np.sqrt(D))
        Wo = jax.random.normal(ks[3], (D, F), dtype=jnp.float32) * (1.0 / np.sqrt(F))
        A = jax.random.normal(ks[4], (E, R, D), dtype=jnp.float32) * (1.0 / np.sqrt(D))
        Bm = jax.random.normal(ks[5], (E, F, R), dtype=jnp.float32) * 0.01
        return {'x': x, 'Wg': Wg, 'bg': bg, 'Wi': Wi, 'Wo': Wo, 'A': A, 'B': Bm}
    _L1_ffn_all = _L1_ffn_setup()
    _L1_ffn_in = {k: v for k, v in _L1_ffn_all.items() if k in ('Wg', 'bg', 'Wi', 'Wo', 'A', 'B')}
    del _L1_ffn_all
    return {'x': x, 'ctx_1024': ctx_1024, 'g_xattn': g_xattn, 'g_ffn': g_ffn, 'L0_xattn_Wq': _L0_xattn_in['Wq'], 'L0_xattn_bq': _L0_xattn_in['bq'], 'L0_xattn_Wk': _L0_xattn_in['Wk'], 'L0_xattn_bk': _L0_xattn_in['bk'], 'L0_xattn_Wv': _L0_xattn_in['Wv'], 'L0_xattn_bv': _L0_xattn_in['bv'], 'L0_xattn_Wff': _L0_xattn_in['Wff'], 'L0_xattn_bff': _L0_xattn_in['bff'], 'L0_ffn_W_up': _L0_ffn_in['W_up'], 'L0_ffn_A_up': _L0_ffn_in['A_up'], 'L0_ffn_B_up': _L0_ffn_in['B_up'], 'L0_ffn_scale_up': _L0_ffn_in['scale_up'], 'L0_ffn_bias_up': _L0_ffn_in['bias_up'], 'L0_ffn_W_down': _L0_ffn_in['W_down'], 'L0_ffn_A_down': _L0_ffn_in['A_down'], 'L0_ffn_B_down': _L0_ffn_in['B_down'], 'L0_ffn_scale_down': _L0_ffn_in['scale_down'], 'L0_ffn_bias_down': _L0_ffn_in['bias_down'], 'L1_xattn_Wq': _L1_xattn_in['Wq'], 'L1_xattn_bq': _L1_xattn_in['bq'], 'L1_xattn_Wk': _L1_xattn_in['Wk'], 'L1_xattn_bk': _L1_xattn_in['bk'], 'L1_xattn_Wv': _L1_xattn_in['Wv'], 'L1_xattn_bv': _L1_xattn_in['bv'], 'L1_ffn_Wg': _L1_ffn_in['Wg'], 'L1_ffn_bg': _L1_ffn_in['bg'], 'L1_ffn_Wi': _L1_ffn_in['Wi'], 'L1_ffn_Wo': _L1_ffn_in['Wo'], 'L1_ffn_A': _L1_ffn_in['A'], 'L1_ffn_B': _L1_ffn_in['B']}

def reference(x, ctx_1024, g_xattn, g_ffn, L0_xattn_Wq, L0_xattn_bq, L0_xattn_Wk, L0_xattn_bk, L0_xattn_Wv, L0_xattn_bv, L0_xattn_Wff, L0_xattn_bff, L0_ffn_W_up, L0_ffn_A_up, L0_ffn_B_up, L0_ffn_scale_up, L0_ffn_bias_up, L0_ffn_W_down, L0_ffn_A_down, L0_ffn_B_down, L0_ffn_scale_down, L0_ffn_bias_down, L1_xattn_Wq, L1_xattn_bq, L1_xattn_Wk, L1_xattn_bk, L1_xattn_Wv, L1_xattn_bv, L1_ffn_Wg, L1_ffn_bg, L1_ffn_Wi, L1_ffn_Wo, L1_ffn_A, L1_ffn_B):
    import jax
    import jax.numpy as jnp

    def _L0_xattn_ref(q, k, v, Wq, bq, Wk, bk, Wv, bv, Wff, bff):
        import math
        import jax, jax.numpy as jnp
        import numpy as np
        EMB_DIM = 128
        CFG_N_HEADS = 16
        N_HEADS = CFG_N_HEADS if CFG_N_HEADS >= EMB_DIM else 1
        B, T, C = q.shape
        H = N_HEADS
        D = C // H
        qp = (q @ Wq.T + bq).reshape(B, T, H, D).transpose(0, 2, 1, 3)
        kp = (k @ Wk.T + bk).reshape(B, T, H, D).transpose(0, 2, 1, 3)
        vp = (v @ Wv.T + bv).reshape(B, T, H, D).transpose(0, 2, 1, 3)
        scale = 1.0 / math.sqrt(D)
        scores = jnp.einsum('bhqd,bhkd->bhqk', qp, kp) * scale
        causal = jnp.tril(jnp.ones((T, T), dtype=bool))
        scores = jnp.where(causal[None, None, :, :], scores, -jnp.inf)
        attn = jax.nn.softmax(scores, axis=-1)
        out = jnp.einsum('bhqk,bhkd->bhqd', attn, vp)
        out = out.transpose(0, 2, 1, 3).reshape(B, T, C)
        return out @ Wff.T + bff

    def _L0_ffn_ref(x, W_up, A_up, B_up, scale_up, bias_up, W_down, A_down, B_down, scale_down, bias_down):
        import jax, jax.numpy as jnp
        import numpy as np
        D_MODEL = 128
        D1, D2 = (32, 32)
        F1, F2 = (64, 64)
        E = 64
        TOP_K = 2

        def kmoe(x_flat, W_router, A, B, scale, bias, d_in1, d_in2, d_out1, d_out2, top_k):
            logits = x_flat @ W_router.T
            vals, idx = jax.lax.top_k(logits, top_k)
            probs = jax.nn.softmax(vals, axis=-1)
            xs = x_flat.reshape(-1, d_in1, d_in2)
            Ag = A[idx]
            Bg = B[idx]
            Y = jnp.einsum('nkoi,nij,nkpj->nkop', Ag, xs, Bg)
            out = jnp.einsum('nkop,nk->nop', Y, probs).reshape(-1, d_out1 * d_out2)
            return out * scale + bias
        orig_shape = x.shape
        x_flat = x.reshape(-1, D1 * D2)
        h = kmoe(x_flat, W_up, A_up, B_up, scale_up, bias_up, D1, D2, F1, F2, TOP_K)
        h = jax.nn.gelu(h, approximate=False)
        y = kmoe(h, W_down, A_down, B_down, scale_down, bias_down, F1, F2, D1, D2, TOP_K)
        return y.reshape(*orig_shape[:-1], D_MODEL)

    def _L1_xattn_ref(query, key, value, Wq, bq, Wk, bk, Wv, bv):
        import jax, jax.numpy as jnp
        import numpy as np
        EMBED_DIM = 128
        BATCH = 4
        SEQ = 256
        q = jnp.einsum('bsd,ed->bse', query, Wq) + bq
        k = jnp.einsum('bsd,ed->bse', key, Wk) + bk
        v = jnp.einsum('bsd,ed->bse', value, Wv) + bv
        inv_scale = jnp.asarray(EMBED_DIM ** 0.5, dtype=q.dtype)
        scores = jnp.einsum('bqd,bkd->bqk', q, k) / inv_scale
        attn = jax.nn.softmax(scores, axis=-1)
        return jnp.einsum('bqk,bkd->bqd', attn, v)

    def _L1_ffn_ref(x, Wg, bg, Wi, Wo, A, B):
        import jax, jax.numpy as jnp
        import numpy as np
        TOP_K = 2
        E = Wg.shape[0]
        logits = jnp.einsum('bsd,ed->bse', x, Wg) + bg
        scores = jax.nn.softmax(logits, axis=-1)
        topv, topi = jax.lax.top_k(scores, TOP_K)
        w = jnp.sum(jax.nn.one_hot(topi, E, dtype=x.dtype) * topv[..., None], axis=-2)
        base = jnp.einsum('bsd,fd->bsf', x, Wi)
        lora_low = jnp.einsum('bsd,erd->bser', x, A)
        lora = jnp.einsum('bser,efr->bsef', lora_low, B)
        h = jax.nn.relu(base[:, :, None, :] + lora)
        expert_out = jnp.einsum('bsef,df->bsed', h, Wo)
        out = jnp.einsum('bse,bsed->bsd', w, expert_out)
        return out
    x = x + jnp.tanh(g_xattn[0]) * _L0_xattn_ref(_layernorm(x, axis=-1), ctx_1024, ctx_1024, L0_xattn_Wq, L0_xattn_bq, L0_xattn_Wk, L0_xattn_bk, L0_xattn_Wv, L0_xattn_bv, L0_xattn_Wff, L0_xattn_bff)
    x = x + jnp.tanh(g_ffn[0]) * _L0_ffn_ref(_layernorm(x, axis=-1), L0_ffn_W_up, L0_ffn_A_up, L0_ffn_B_up, L0_ffn_scale_up, L0_ffn_bias_up, L0_ffn_W_down, L0_ffn_A_down, L0_ffn_B_down, L0_ffn_scale_down, L0_ffn_bias_down)
    x = x + jnp.tanh(g_xattn[1]) * _L1_xattn_ref(_layernorm(x, axis=-1), ctx_1024, ctx_1024, L1_xattn_Wq, L1_xattn_bq, L1_xattn_Wk, L1_xattn_bk, L1_xattn_Wv, L1_xattn_bv)
    x = x + jnp.tanh(g_ffn[1]) * _L1_ffn_ref(_layernorm(x, axis=-1), L1_ffn_Wg, L1_ffn_bg, L1_ffn_Wi, L1_ffn_Wo, L1_ffn_A, L1_ffn_B)
    return x

_drawn_inputs = setup_inputs


def setup_inputs(seed=0):
    import zlib

    import numpy as np

    out = dict(_drawn_inputs(seed))
    spreads = {'g_ffn': (-1.0, 0.549),
     'L0_ffn_bias_up': (0.0, 0.8),
     'L0_ffn_bias_down': (0.0, 0.1),
     'L1_ffn_bg': (0.0, 0.8)}
    factors = {'L0_xattn_bq': 3.465,
     'L0_xattn_bk': 8.0,
     'L0_ffn_W_up': 8.0,
     'L0_ffn_A_up': 8.0,
     'L0_ffn_B_up': 8.0,
     'L0_ffn_W_down': 8.0,
     'L0_ffn_A_down': 8.0,
     'L0_ffn_B_down': 8.0,
     'L1_xattn_bq': 8.0,
     'L1_xattn_bk': 8.0,
     'L1_ffn_A': 8.0,
     'L1_ffn_B': 8.0}
    for name, (base, spread) in spreads.items():
        noise = np.random.default_rng([zlib.crc32(name.encode()), seed]).standard_normal(out[name].shape)
        drawn = base * np.exp(spread * noise) if base else spread * noise
        out[name] = jnp.asarray(drawn.astype(out[name].dtype))
    for name, factor in factors.items():
        out[name] = (out[name] * factor).astype(out[name].dtype)
    return out
```

```python
from contextlib import ExitStack

import concourse.bass as bass
from concourse import mybir

F32 = mybir.dt.float32
BF16 = mybir.dt.bfloat16
U32 = mybir.dt.uint32
I32 = mybir.dt.int32
ALU = mybir.AluOpType
ACT = mybir.ActivationFunctionType
AX_X = mybir.AxisListType.X

ROWS, D = 4096, 128
TILES = ROWS // 128
CHUNK = 4
W = CHUNK * D
CHUNKS = TILES // CHUNK
EXPERTS = 64
EPS = 1e-5
NEWTON = 3
SCALE = float(D) ** -0.5
HIDDEN, FC = 512, 4
LORA_E, LORA_R = 4, 4
LR = LORA_E * LORA_R
PROJ = LORA_E + LR


def spread(ap, axis, n):
    u = ap.unsqueeze(axis)
    shape = list(u.shape)
    shape[axis] = n
    return u.broadcast_to(shape)


def flamingo_kernel(nc, x_in, ctx_in, consts, gates, rows, cols, attn_w, w_up_router, w_down_router,
                    a_up, b_up, a_down, b_down, bias_up, bias_down, wi_t, wo_t, wg_a, lora_b, out):
    with ExitStack() as ctx:
        def sb(name, n, dt=F32, p=128):
            return ctx.enter_context(nc.sbuf_tensor(name, [p, n], dt))

        def sem(name):
            return ctx.enter_context(nc.semaphore(name))

        banks = ctx.enter_context(nc.psum_tensor("banks", [128, 8, 512], F32))

        x_res = sb("x_res", TILES * D)
        region_h = sb("region_h", 16384)
        region_a = sb("region_a", 16384)
        region_t = sb("region_t", 4096)
        region_x = sb("region_x", 4096)
        region_r = sb("region_r", 4096)
        const = sb("const", 472)
        gate = sb("gate", 6)
        tgate = sb("tgate", 4)
        row_c = sb("row_c", 260)
        col_c = sb("col_c", 5)
        w_att = sb("w_att", 7 * 128)
        w_vff = sb("w_vff", 128)
        bias_x = sb("bias_x", 2 * 128)
        shared = sb("shared", 1024)
        prob_up = sb("prob_up", 256)
        bup = sb("bup", 64)
        bdn = sb("bdn", 32)
        ident_b = sb("ident_b", 128, BF16)
        stat = sb("stat", CHUNK * 6)
        mv = sb("mv", CHUNK * 2)
        rstd = sb("rstd", 4 * CHUNK)
        shift = sb("shift", 4 * CHUNK)
        mx = sb("mx", CHUNK)
        newton = sb("newton", 2 * CHUNK)
        negm = sb("negm", 2 * CHUNK)
        rsum = sb("rsum", 2 * CHUNK)
        rinv = sb("rinv", CHUNK)
        v8 = sb("v8", 32)
        ix8 = sb("ix8", 32, U32)
        idx = sb("idx", 8)
        gap = sb("gap", 4)
        egap = sb("egap", 4)
        den = sb("den", 4)
        pr = sb("pr", 8)
        down_scale = sb("down_scale", 1)

        var, half = newton[:, 0:CHUNK], newton[:, CHUNK:2 * CHUNK]
        ident = const[:, 0:128]
        masks = [const[:, 128:256], const[:, 256:384]]
        iota = const[:, 384:448]
        tri = const[:, 448:464]
        slot_id = const[:, 464:466]
        sel = const[0:96, 466:469]
        wq = [w_att[:, 0:128], w_att[:, 512:640]]
        wk = [w_att[:, 128:256], w_att[:, 640:768]]
        wff_t, wv0 = w_att[:, 256:384], w_att[:, 384:512]
        wout = [w_vff[:, :], w_att[:, 768:896]]
        y_t = lambda t: w_att[:, (t % 2) * 128:(t % 2) * 128 + 128]
        y_r = lambda t: w_att[:, 256 + (t % 2) * 128:256 + (t % 2) * 128 + 128]
        bq = [col_c[:, 0:1], col_c[:, 3:4]]
        bk = [col_c[:, 1:2], col_c[:, 4:5]]
        bv0 = col_c[:, 2:3]

        def step_buf(region, at, n, k):
            return region[:, at + (k % n) * W:at + (k % n) * W + W]

        def ctx_ring(L, k):
            return step_buf(region_h, 4096, 4, k) if L == 0 else step_buf(region_t, 2048, 4, k)

        A = region_a
        ctxT_s = lambda k: step_buf(A, 0, 2, k)
        ln_s = lambda k: step_buf(A, 1024, 2, k)
        lnT_s = lambda k: step_buf(A, 2048, 2, k)
        kT_s = lambda k: step_buf(A, 3072, 2, k)
        qT_s = lambda k: step_buf(A, 4096, 2, k)
        sm_s = lambda k: step_buf(A, 5120, 2, k)
        prob_s = lambda k: step_buf(A, 6144, 2, k)
        pT_s = lambda k: step_buf(A, 7168, 2, k)
        uT_s = lambda k: step_buf(A, 8192, 2, k)
        vff_tmp = A[:, 9216:9472]
        mln_s = lambda k: step_buf(A, 12288, 2, k)
        logT_up = A[0:64, 13312:13824]
        lg_up = A[:, 13824:14080]
        oh_up = A[:, 14592:15104].bitcast(BF16)
        prb_up = A[:, 14336:14592]
        logT_dn = A[:, 8192:8448]
        lg_dn = A[:, 8448:8704]
        oh_dn = A[:, 8704:8960].bitcast(BF16)
        prb_dn = A[:, 8960:9472]

        lnT_all = region_h[:, 0:4096]
        raw_up = region_h[:, 8192:12288]
        h_all = region_h
        g_b, g_a = region_h, region_a
        wu = shared[:, 0:512]
        oh_up_T = shared[:, 512:1024].bitcast(BF16)
        oh_a_T = shared[:, 0:256].bitcast(BF16)
        oh_b_T = shared[:, 256:512].bitcast(BF16)
        prob_dn = shared[:, 512:1024]
        up_hm = [region_t[:, 0:1024].bitcast(BF16), region_t[:, 1024:2048].bitcast(BF16)]
        up_lo = [region_t[:, 2048:3072].bitcast(BF16), region_t[:, 3072:4096].bitcast(BF16)]
        xT = region_x
        x_bd = lambda t: region_r[:, (t % 2) * 1024:(t % 2) * 1024 + 1024]
        t_bd = lambda t: region_r[:, 2048 + (t % 2) * 1024:2048 + (t % 2) * 1024 + 1024]
        u_bd = lambda t: region_t[:, (t % 2) * 1024:(t % 2) * 1024 + 1024]
        raw_dn = region_t
        dn_part = [region_x.bitcast(BF16), region_a[:, 12288:16384].bitcast(BF16),
                   region_r.bitcast(BF16)]
        wd_bd = region_a[:, 0:8192]
        a_bd = region_a[:, 0:8192]
        b_nat = region_a[:, 8192:12288]

        H = region_h
        f_ln = lambda k: step_buf(H, 0, 2, k)
        f_lnT = lambda k: step_buf(H, 13824, 3, k)
        h1_s = H[:, 2048:4096]
        h2_s = H[:, 4096:6144]
        lora_T = lambda k: H[0:96, 6144 + (k % 2) * 512:6656 + (k % 2) * 512].bitcast(BF16)
        wi_s = H[:, 8192:8704]
        wo_s = H[:, 8704:9216]
        wga_s = H[:, 9216:9236]
        lb_raw = H[0:96, 9728:10240]
        lb_hi = H[0:96, 10240:10496].bitcast(BF16)
        lb_mid = H[0:96, 10496:10752].bitcast(BF16)
        lb_part = H[0:96, 10752:11008].bitcast(BF16)
        proj = lambda k: H[:, 11008 + (k % 2) * 80:11008 + (k % 2) * 80 + 80]
        T0 = 11264
        r_max = H[:, T0:T0 + 4]
        r_sh = H[:, T0 + 16:T0 + 32]
        r_exp = H[:, T0 + 32:T0 + 48]
        r_gt = H[:, T0 + 64:T0 + 128]
        r_eq = H[:, T0 + 128:T0 + 192]
        r_rank = H[:, T0 + 192:T0 + 208]
        r_mask = H[:, T0 + 256:T0 + 288]
        r_pick = H[:, T0 + 288:T0 + 320]
        r_sum = H[:, T0 + 320:T0 + 324]
        r_inv = H[:, T0 + 328:T0 + 332]
        r_w = lambda k: H[:, T0 + 328 + 8 * (k % 3 + 1):T0 + 336 + 8 * (k % 3 + 1)]
        r_wr = H[:, T0 + 360:T0 + 368]
        l_low = H[:, T0 + 384:T0 + 512]
        l_rest = H[:, T0 + 512:T0 + 640]
        l_parts = H[:, T0 + 640:T0 + 1024].bitcast(BF16)
        o_sum = lambda k: step_buf(H, 12800, 2, k)

        consts_in, weights_in, small_in = sem("consts_in"), sem("weights_in"), sem("small_in")
        up_raw_in, down_raw_in, router_in = sem("up_raw_in"), sem("down_raw_in"), sem("router_in")
        lora_in, wd_in = sem("lora_in"), sem("wd_in")
        x_in_sem = [sem(f"x_in_{k}") for k in range(CHUNKS)]
        ctx_in_sem = [[sem(f"ctx{L}_in_{i}") for i in range(4)] for L in range(2)]
        names = ("stats ln xb ctxT_pe lnT_pe ctxT lnT k_pe q_pe k q s_pe s_ev sm prob pt_pe pt u_pe u "
                 "o_pe x").split()
        att = [{n: sem(f"att{L}_{n}") for n in names} for L in range(2)]
        gates_ready, ident_b_ready = sem("gates_ready"), sem("ident_b_ready")
        vff_pe, vff_ready, bv_ready, bias_ready = (sem("vff_pe"), sem("vff_ready"), sem("bv_ready"),
                                                   sem("bias_ready"))
        tables_up = sem("tables_up")
        m_stats, m_ln, m_lnT_pe, m_lnT, m_xt = (sem("m_stats"), sem("m_ln"), sem("m_lnT_pe"),
                                                sem("m_lnT"), sem("m_xt"))
        ru = {n: sem(f"ru_{n}") for n in "log_pe log lgT_pe gap egap oh oh_pe ohT_a ohT_d prb pb_pe pb".split()}
        rd = {n: sem(f"rd_{n}") for n in "log_pe log lgT_pe gap egap oh oh_pe ohT_a ohT_d prb pb_pe pb".split()}
        g_pe, g_act, g_dve = sem("g_pe"), sem("g_act"), sem("g_dve")
        xbd_ready, s1_pe, tbd_ready, s2_pe, hb_ready, h_ready = (
            sem("xbd_ready"), sem("s1_pe"), sem("tbd_ready"), sem("s2_pe"), sem("hb_ready"), sem("h_ready"))
        wd_zero, split_act, split_dve, split_pool, split_zero = (
            sem("wd_zero"), sem("split_act"), sem("split_dve"), sem("split_pool"), sem("split_zero"))
        abd_zero = sem("abd_zero")
        da_pe, da_act, da_dve, db_pe, db_act, db_dve = (sem("da_pe"), sem("da_act"), sem("da_dve"),
                                                        sem("db_pe"), sem("db_act"), sem("db_dve"))
        d1_pe, ubd_ready, d2_pe = sem("d1_pe"), sem("ubd_ready"), sem("d2_pe")
        y_ev, y_rows, x2 = sem("y_ev"), sem("y_rows"), sem("x2")
        fnames = ("hi mid rest stats ln lnT_pe lnT proj_pe proj low parts lora_pe lora exp_in exp lb z1_pe z2_pe h1 h2 "
                  "o_pe y").split()
        ff = {n: sem(f"ff_{n}") for n in fnames}
        stored = sem("stored")
        act_step, dve_step, pool_step = sem("act_step"), sem("dve_step"), sem("pool_step")

        block = ctx.enter_context(nc.Block())

        def steps(lag):
            return range(CHUNKS + lag)

        def here(k):
            return 0 <= k < CHUNKS

        def linker(eng, step_sem):
            count = [0]

            def link(ins):
                count[0] += 1
                ins.then_inc(step_sem, 1)
                eng.wait_ge(step_sem, count[0])
            return link

        @block.sync
        def _(sp):
            sp.dma_start(x_res[:, 0:W].rearrange("p (t d) -> p t d", t=CHUNK),
                         x_in[0:CHUNK].rearrange("t p d -> p t d")).then_inc(x_in_sem[0], 16)
            sp.dma_start(const[:, :], consts).then_inc(consts_in, 16)
            sp.dma_start(ctx_ring(0, 0).rearrange("p (t d) -> p t d", t=CHUNK),
                         ctx_in[0:CHUNK].rearrange("t p d -> p t d")).then_inc(ctx_in_sem[0][0], 16)
            sp.dma_start(w_att[:, :], attn_w).then_inc(weights_in, 16)
            sp.dma_start(gate[:, :], gates.broadcast_to([128, 6])).then_inc(small_in, 16)
            sp.dma_start(row_c[:, :], rows.broadcast_to([128, 260])).then_inc(small_in, 16)
            sp.dma_start(col_c[:, :], cols).then_inc(small_in, 16)
            for k in range(1, CHUNKS):
                sp.dma_start(x_res[:, k * W:(k + 1) * W].rearrange("p (t d) -> p t d", t=CHUNK),
                             x_in[k * CHUNK:(k + 1) * CHUNK].rearrange("t p d -> p t d")).then_inc(x_in_sem[k], 16)
                if k >= 4:
                    sp.wait_ge(att[0]["u_pe"], k - 3)
                sp.dma_start(ctx_ring(0, k).rearrange("p (t d) -> p t d", t=CHUNK),
                             ctx_in[k * CHUNK:(k + 1) * CHUNK].rearrange("t p d -> p t d")
                             ).then_inc(ctx_in_sem[0][k % 4], 16)
                if k == 2:
                    for tb, table in enumerate((b_up, a_up)):
                        for half in range(2):
                            sp.dma_start(raw_up[64 * half:64 * half + 64, tb * 2048:tb * 2048 + 2048],
                                         table).then_inc(up_raw_in, 16)
                if k == 3:
                    sp.dma_start(wu, w_up_router).then_inc(router_in, 16)
                    for half in range(2):
                        sp.dma_start(bup[64 * half:64 * half + 64, :], bias_up).then_inc(router_in, 16)
                    for g in range(4):
                        sp.dma_start(bdn[32 * g:32 * g + 32, :], bias_down).then_inc(router_in, 16)
            sp.wait_ge(g_pe, 32)
            for tb, table in enumerate((a_down, b_down)):
                for half in range(2):
                    sp.dma_start(raw_dn[64 * half:64 * half + 64, tb * 2048:tb * 2048 + 2048],
                                 table).then_inc(down_raw_in, 16)
            sp.wait_ge(s2_pe, TILES // 2)
            for half in range(2):
                sp.dma_start(wd_bd[64 * half:64 * half + 64, :].rearrange("p (j x e) -> p j x e", j=64, x=2)[:, :, half, :],
                             w_down_router).then_inc(wd_in, 16)
            sp.wait_ge(split_act, 6)
            sp.wait_ge(split_dve, 2)
            sp.wait_ge(split_pool, 2)
            for k in range(CHUNKS):
                if k >= 4:
                    sp.wait_ge(att[1]["u_pe"], k - 3)
                sp.dma_start(ctx_ring(1, k).rearrange("p (t d) -> p t d", t=CHUNK),
                             ctx_in[k * CHUNK:(k + 1) * CHUNK].rearrange("t p d -> p t d")
                             ).then_inc(ctx_in_sem[1][k % 4], 16)
                if k == 3:
                    sp.wait_ge(d1_pe, TILES)
                    sp.dma_start(wi_s, wi_t).then_inc(lora_in, 16)
                    sp.dma_start(wo_s, wo_t).then_inc(lora_in, 16)
                    sp.dma_start(wga_s, wg_a).then_inc(lora_in, 16)
                    for i in range(6):
                        sp.dma_start(lb_raw[i * LR:(i + 1) * LR, :], lora_b).then_inc(lora_in, 16)
            for k in range(CHUNKS):
                sp.wait_ge(ff["y"], k + 1)
                sp.dma_start(out[k * CHUNK:(k + 1) * CHUNK].rearrange("t p d -> p t d"),
                             x_res[:, k * W:(k + 1) * W].rearrange("p (t d) -> p t d", t=CHUNK)
                             ).then_inc(stored, 16)
            sp.wait_ge(stored, 16 * CHUNKS)

        @block.gpsimd
        def _(pool):
            link = linker(pool, pool_step)

            def attention(L, extra):
                S = att[L]
                for k in range(CHUNKS):
                    if k == 0:
                        pool.wait_ge(bias_ready, 2)
                    pool.wait_ge(S["ln"], k + 1)
                    xk = x_res[:, k * W:(k + 1) * W].rearrange("p (t d) -> p t d", t=CHUNK)
                    pool.tensor_tensor(xk, xk, spread(bias_x[:, L * 128:(L + 1) * 128], 1, CHUNK),
                                       ALU.add).then_inc(S["xb"], 1)
                    pool.wait_ge(S["xb"], k + 1)
                    for _ in range(3):
                        if extra:
                            extra.pop(0)()

            def split_steps(tb):
                raw = raw_up[:, tb * 2048:(tb + 1) * 2048]
                hm, lo = up_hm[tb], up_lo[tb]

                def first():
                    if tb == 0:
                        pool.wait_ge(up_raw_in, 64)
                    link(pool.tensor_copy(hm, raw))
                return [first,
                        lambda: link(pool.tensor_tensor(raw, raw, hm, ALU.subtract)),
                        lambda: link(pool.tensor_copy(hm[64:128, :], raw[64:128, :])),
                        lambda: link(pool.tensor_copy(lo[0:64, :], raw[0:64, :])),
                        lambda: link(pool.tensor_tensor(raw[0:64, :], raw[0:64, :], lo[0:64, :], ALU.subtract)),
                        lambda: link(pool.tensor_copy(lo[0:64, :], raw[0:64, :])),
                        lambda: link(pool.memset(lo[64:128, :], 0.0))]

            work = split_steps(0) + split_steps(1)
            work.append(lambda: link(pool.memset(region_r[:, :], 0.0)))
            work.append(lambda: pool.nop().then_inc(tables_up, 1))
            attention(0, work)
            while work:
                work.pop(0)()
            wd_off = wd_bd.rearrange("p (j x e) -> p j x e", j=64, x=2)
            pool.wait_ge(s2_pe, TILES // 2)
            link(pool.memset(wd_off[0:64, :, 1, :], 0.0))
            pool.memset(wd_off[64:128, :, 0, :], 0.0).then_inc(wd_zero, 1)
            pool.wait_ge(wd_zero, 1)
            pool.wait_ge(xbd_ready, TILES)
            pool.wait_ge(s2_pe, TILES)
            for part in range(3):
                v = dn_part[part].rearrange("p (m x i) -> p m x i", m=64, x=2)
                link(pool.memset(v[0:64, :, 1, :], 0.0))
                pool.memset(v[64:128, :, 0, :], 0.0).then_inc(split_zero, 1)
                pool.wait_ge(split_zero, part + 1)
            raw = raw_dn[64:128, :].rearrange("p (m i) -> p m i", m=64)
            for part in range(2):
                pool.wait_ge(split_act, 2 * part + 2)
                v = dn_part[part].rearrange("p (m x i) -> p m x i", m=64, x=2)[64:128, :, 1, :]
                pool.tensor_tensor(raw, raw, v, ALU.subtract).then_inc(split_pool, 1)
                pool.wait_ge(split_pool, part + 1)
            pool.wait_ge(rd["log_pe"], 1)
            v = a_bd.rearrange("p (m x i) -> p m x i", m=64, x=2)
            link(pool.memset(v[0:64, :, 1, :], 0.0))
            pool.memset(v[64:128, :, 0, :], 0.0).then_inc(abd_zero, 1)
            pool.wait_ge(abd_zero, 1)
            pool.wait_ge(split_act, 6)
            pool.memset(region_t[:, 0:2048], 0.0).then_inc(abd_zero, 1)

            for t in range(TILES):
                pool.wait_ge(y_rows, t + 1)
                xt = x_res[:, t * 128:(t + 1) * 128]
                pool.tensor_tensor(xt, xt, y_r(t), ALU.add).then_inc(x2, 1)

            attention(1, [])

            rest, low = l_rest, l_low
            hi, mid = (l_parts.rearrange("p (m six c) -> p m six c", m=2 * CHUNK, six=6)[:, :, i, :] for i in (0, 1))
            m16 = lambda ap: ap.rearrange("p (m c) -> p m c", c=LR)
            for k in range(CHUNKS):
                pool.wait_ge(ff["hi"], k + 1)
                if k >= 1:
                    pool.wait_ge(ff["parts"], k)
                pool.tensor_tensor(m16(rest), m16(low), hi, ALU.subtract).then_inc(ff["rest"], 1)
                pool.wait_ge(ff["mid"], k + 1)
                pool.tensor_tensor(m16(rest), m16(rest), mid, ALU.subtract).then_inc(ff["rest"], 1)
                pool.wait_ge(ff["rest"], 2 * k + 2)

        @block.scalar
        def _(act):
            link = linker(act, act_step)

            def copy(dst, src):
                return act.activation(dst, src, ACT.Copy)

            act.wait_ge(small_in, 48)
            act.activation(tgate[:, :], gate[:, 0:4], ACT.Tanh).then_inc(gates_ready, 1)

            def normalise(dst, k, lane, stats_sem, done_sem):
                act.wait_ge(stats_sem, k + 1)
                for i in range(CHUNK):
                    j = CHUNK * (2 * lane + k % 2) + i
                    ins = act.activation(dst[:, i * D:(i + 1) * D], x_res[:, k * W + i * D:k * W + (i + 1) * D],
                                         ACT.Identity, bias=shift[:, j:j + 1], scale=rstd[:, j:j + 1])
                ins.then_inc(done_sem, 1)

            def attention(L):
                S = att[L]
                normalise(ln_s(0), 0, 0, S["stats"], S["ln"])
                for j in steps(5 if L == 0 else 3):
                    k = j - 5
                    if L == 0 and here(k):
                        act.wait_ge(m_lnT_pe, k + 1)
                        copy(lnT_all[:, k * W:(k + 1) * W], banks[:, 0, :]).then_inc(m_lnT, 1)
                    k = j - 3
                    if here(k):
                        act.wait_ge(S["pt_pe"], k + 1)
                        if k >= 2:
                            act.wait_ge(S["u_pe"], k - 1)
                        copy(pT_s(k), banks[:, 5, :]).then_inc(S["pt"], 1)
                    k = j
                    if here(k):
                        act.wait_ge(S["ctxT_pe"], k + 1)
                        if k >= 2:
                            act.wait_ge(S["k_pe"], k - 1)
                        copy(ctxT_s(k), banks[:, 0, :]).then_inc(S["ctxT"], 1)
                    k = j - 2
                    if here(k):
                        act.wait_ge(S["sm"], k + 1)
                        if k >= 2:
                            act.wait_ge(S["pt_pe"], k - 1)
                            act.wait_ge(S["x"], k - 1)
                        for i in range(CHUNK):
                            j2 = (k % 2) * CHUNK + i
                            ins = act.activation(prob_s(k)[:, i * D:(i + 1) * D], sm_s(k)[:, i * D:(i + 1) * D],
                                                 ACT.Exp, bias=negm[:, j2:j2 + 1], scale=SCALE,
                                                 accum_out=rsum[:, j2:j2 + 1])
                        ins.then_inc(S["prob"], 1)
                    k = j - 1
                    if here(k):
                        act.wait_ge(S["k_pe"], k + 1)
                        if k >= 2:
                            act.wait_ge(S["s_pe"], k - 1)
                        act.activation(kT_s(k), banks[:, 2, :], ACT.Identity, bias=bk[L]).then_inc(S["k"], 1)
                    k = j + 1
                    if here(k):
                        if k >= 2:
                            act.wait_ge(S["lnT_pe"], k - 1)
                        normalise(ln_s(k), k, 0, S["stats"], S["ln"])
                    k = j - 4
                    if L == 0 and here(k):
                        if k >= 2:
                            act.wait_ge(m_lnT_pe, k - 1)
                            act.wait_ge(m_xt, k - 1)
                        normalise(mln_s(k), k, 1, m_stats, m_ln)

            attention(0)

            act.wait_ge(ru["log_pe"], 1)
            copy(logT_up.rearrange("p (q t n) -> p t q n", q=4, n=4),
                 banks[0:64, 2, :].rearrange("p (t q n) -> p t q n", q=4, n=4)).then_inc(ru["log"], 1)
            act.wait_ge(ru["gap"], 1)
            act.activation(egap[:, :], gap[:, :], ACT.Exp).then_inc(ru["egap"], 1)
            act.wait_ge(ru["oh_pe"], 1)
            copy(oh_up_T[:, 0:512].rearrange("p (s P x) -> p s x P", s=2, x=2),
                 banks[:, 4, :].rearrange("p (s x P) -> p s x P", s=2, x=2)).then_inc(ru["ohT_a"], 1)
            for u in range(0, 32, 2):
                act.wait_ge(g_pe, u + 1)
                dst = (g_b if u < 16 else g_a)[:, :].rearrange("p (m c) -> p c m", c=64)
                copy(dst[:, 4 * (u % 16):4 * (u % 16) + 4, :],
                     banks[:, 2 * (u % 4):2 * (u % 4) + 2, :].rearrange("p b (c m) -> p (b c) m", c=2)
                     ).then_inc(g_act, 1)
            act.wait_ge(m_xt, CHUNKS)
            act.wait_ge(tables_up, 1)
            for j in range(TILES + 2):
                t = j
                if t < TILES:
                    if t >= 2:
                        act.wait_ge(s1_pe, t - 1)
                    dst = x_bd(t).rearrange("p (n x g i) -> p n x g i", n=4, x=2, g=4)
                    src = xT[:, t * 128:(t + 1) * 128].rearrange("p (n i) -> p n i", n=4)
                    for g in range(4):
                        for x in range(2):
                            q = (g // 2) * 2 + x
                            ins = copy(dst[32 * g:32 * g + 32, :, x, g, :], src[32 * q:32 * q + 32, :, :])
                    ins.then_inc(xbd_ready, 1)
                t = j - 2
                if t >= 0:
                    act.wait_ge(hb_ready, t + 1)
                    ht = h_all[:, t * 512:(t + 1) * 512]
                    act.activation(ht, ht, ACT.Gelu).then_inc(h_ready, 1)
            act.wait_ge(down_raw_in, 64)
            for part in range(3):
                act.wait_ge(xbd_ready, TILES) if part == 0 else act.wait_ge(s2_pe, TILES)
                for x in range(2):
                    if part:
                        act.wait_ge(split_dve if x == 0 else split_pool, part)
                    raw = raw_dn[64 * x:64 * x + 64, :].rearrange("p (m i) -> p m i", m=64)
                    v = dn_part[part].rearrange("p (m x i) -> p m x i", m=64, x=2)
                    copy(v[64 * x:64 * x + 64, :, x, :], raw).then_inc(split_act, 1)
            act.wait_ge(rd["log_pe"], 1)
            copy(logT_dn, banks[:, 6, 0:256]).then_inc(rd["log"], 1)
            act.wait_ge(rd["gap"], 1)
            act.activation(egap[:, :], gap[:, :], ACT.Exp).then_inc(rd["egap"], 1)
            act.wait_ge(rd["oh_pe"], 1)
            copy(oh_a_T.rearrange("p (s P k) -> p k s P", s=2, k=2),
                 banks[:, 0, :].rearrange("p (k s P) -> p k s P", k=2, s=2)).then_inc(rd["ohT_a"], 1)
            act.wait_ge(abd_zero, 1)
            for k in range(4):
                for v in range(8):
                    act.wait_ge(da_pe, 8 * k + v + 1)
                    dst = a_bd.rearrange("p (m x s o) -> p o s m x", m=64, x=2, s=2)
                    src = banks[:, v % 4, :].rearrange("p (o s m) -> p o s m", o=4, s=2)
                    copy(dst[0:64, 4 * v:4 * v + 4, :, :, 0], src[0:64]).then_inc(da_act, 1)
                for v in range(0, 8, 2):
                    act.wait_ge(db_pe, 8 * k + v + 1)
                    dst = b_nat.rearrange("p (m s o) -> p o s m", m=64, s=2)
                    src = banks[:, v % 4, :].rearrange("p (o s m) -> p o s m", o=4, s=2)
                    copy(dst[:, 4 * v:4 * v + 4, :, :], src).then_inc(db_act, 1)

            attention(1)

            for j in steps(2):
                k = j
                if here(k):
                    if k >= 2:
                        act.wait_ge(ff["lnT_pe"], k - 1)
                    normalise(f_ln(k), k, 1, ff["stats"], ff["ln"])
                    act.wait_ge(ff["lnT_pe"], k + 1)
                    if k >= 3:
                        act.wait_ge(ff["z2_pe"], FC * (k - 2))
                    copy(f_lnT(k), banks[:, 0, :]).then_inc(ff["lnT"], 1)
                k = j - 2
                if here(k):
                    for fc in range(FC):
                        act.wait_ge(ff["z1_pe"], FC * k + fc + 1)
                        if k >= 1 and fc == 0:
                            act.wait_ge(ff["o_pe"], k)
                        act.activation(h1_s[:, fc * W:(fc + 1) * W], banks[:, 2 + (FC * k + fc) % 3, :],
                                       ACT.Relu).then_inc(ff["h1"], 1)
                k = j - 1
                if here(k):
                    act.wait_ge(ff["lora_pe"], k + 1)
                    if k >= 2:
                        act.wait_ge(ff["z2_pe"], FC * (k - 1))
                    copy(lora_T(k), banks[0:96, 1, :].bitcast(BF16)).then_inc(ff["lora"], 1)
                k = j
                if here(k):
                    act.wait_ge(ff["exp_in"], k + 1)
                    act.activation(r_exp, r_sh, ACT.Exp).then_inc(ff["exp"], 1)
                    low = l_low.rearrange("p (m c) -> p m c", c=LR)
                    rest = l_rest.rearrange("p (m c) -> p m c", c=LR)
                    parts = l_parts.rearrange("p (m six c) -> p m six c", m=2 * CHUNK, six=6)
                    act.wait_ge(ff["low"], k + 1)
                    if k >= 1:
                        act.wait_ge(ff["lora_pe"], k)
                    copy(parts[:, :, 0, :], low).then_inc(ff["hi"], 1)
                    copy(parts[:, :, 2, :], low)
                    copy(parts[:, :, 4, :], low)
                    act.wait_ge(ff["rest"], 2 * k + 1)
                    copy(parts[:, :, 1, :], rest)
                    copy(parts[:, :, 3, :], rest).then_inc(ff["mid"], 1)
                    act.wait_ge(ff["rest"], 2 * k + 2)
                    copy(parts[:, :, 5, :], rest).then_inc(ff["parts"], 1)

        @block.vector
        def _(dve):
            link = linker(dve, dve_step)

            statistics_sems = []

            def statistics(k, lane, done):
                if statistics_sems:
                    dve.wait_ge(*statistics_sems[-1])
                for i in range(CHUNK):
                    ins = dve.bn_stats(stat[:, 6 * i:6 * i + 6], x_res[:, k * W + i * D:k * W + (i + 1) * D])
                link(ins)
                for i in range(CHUNK):
                    ins = dve.bn_aggr(mv[:, 2 * i:2 * i + 2], stat[:, 6 * i:6 * i + 6])
                link(ins)
                m4 = mv[:, :].rearrange("p (t c) -> p t c", c=2)
                at = CHUNK * (2 * lane + k % 2)
                y = rstd[:, at:at + CHUNK]
                link(dve.tensor_scalar(var, m4[:, :, 1], EPS, None, ALU.add))
                link(dve.tensor_scalar(half.bitcast(I32), var.bitcast(I32), 1, None, ALU.arith_shift_right))
                link(dve.tensor_scalar(y.bitcast(I32), half.bitcast(I32), -1.0, float(0x5F3759DF),
                                       ALU.mult, ALU.add))
                for i in range(NEWTON):
                    link(dve.scalar_tensor_tensor(half, y, -0.5, y, ALU.mult, ALU.mult))
                    link(dve.tensor_tensor(half, half, var, ALU.mult))
                    link(dve.scalar_tensor_tensor(y, half, 1.5, y, ALU.add, ALU.mult))
                dve.scalar_tensor_tensor(shift[:, at:at + CHUNK], m4[:, :, 0], -1.0, y, ALU.mult,
                                         ALU.mult).then_inc(done, 1)
                statistics_sems.append((done, k + 1))

            def attention(L):
                S = att[L]

                def stats(k):
                    if L == 0:
                        dve.wait_ge(x_in_sem[k], 16)
                    else:
                        dve.wait_ge(x2, CHUNK * (k + 1))
                    if k >= 2:
                        dve.wait_ge(S["ln"], k - 1)
                    statistics(k, 0, S["stats"])

                stats(0)
                for j in steps(5 if L == 0 else 3):
                    k = j - 5
                    if L == 0 and here(k):
                        dve.wait_ge(m_ln, k + 1)
                        for i in range(CHUNK):
                            t = k * CHUNK + i
                            ins = dve.transpose(
                                xT[:, t * 128:(t + 1) * 128].rearrange("p (n b r) -> p b n r", n=4, b=4),
                                mln_s(k)[:, i * 128:(i + 1) * 128])
                        ins.then_inc(m_xt, 1)
                    k = j - 2
                    if here(k):
                        dve.wait_ge(S["s_pe"], k + 1)
                        if k >= 2:
                            dve.wait_ge(S["prob"], k - 1)
                        dve.tensor_tensor(sm_s(k).rearrange("p (t m) -> p t m", t=CHUNK),
                                          banks[:, 4, :].rearrange("p (t m) -> p t m", t=CHUNK),
                                          spread(masks[L], 1, CHUNK), ALU.add).then_inc(S["s_ev"], 1)
                        dve.wait_ge(S["s_ev"], k + 1)
                        if k >= 1:
                            dve.wait_ge(S["sm"], k)
                        link(dve.tensor_reduce(mx[:, :], sm_s(k).rearrange("p (t m) -> p t m", t=CHUNK),
                                               AX_X, ALU.max))
                        dve.tensor_scalar(negm[:, CHUNK * (k % 2):CHUNK * (k % 2 + 1)], mx[:, :], -SCALE, None,
                                          ALU.mult).then_inc(S["sm"], 1)
                    k = j
                    if here(k):
                        dve.wait_ge(S["lnT_pe"], k + 1)
                        if k >= 2:
                            dve.wait_ge(S["q_pe"], k - 1)
                        dve.tensor_copy(lnT_s(k), banks[:, 1, :]).then_inc(S["lnT"], 1)
                    k = j - 3
                    if here(k):
                        dve.wait_ge(S["u_pe"], k + 1)
                        if k >= 2:
                            dve.wait_ge(S["o_pe"], k - 1)
                        dve.tensor_copy(uT_s(k), banks[:, 6, :]).then_inc(S["u"], 1)
                    k = j - 1
                    if here(k):
                        dve.wait_ge(S["q_pe"], k + 1)
                        if k >= 2:
                            dve.wait_ge(S["s_pe"], k - 1)
                        dve.tensor_scalar(qT_s(k), banks[:, 3, :], bq[L], None, ALU.add).then_inc(S["q"], 1)
                    if here(j + 1):
                        stats(j + 1)
                    if L == 0 and j == 0:
                        dve.wait_ge(gates_ready, 1)
                        dve.wait_ge(vff_pe, 1)
                        link(dve.tensor_tensor(bias_x[:, 0:128], banks[:, 7, 128:256], row_c[:, 0:128], ALU.add))
                        dve.tensor_copy(w_vff[:, :], banks[:, 7, 0:128]).then_inc(vff_ready, 1)
                        dve.tensor_scalar(bias_x[:, 0:128], bias_x[:, 0:128], tgate[:, 0:1], None,
                                          ALU.mult).then_inc(bias_ready, 1)
                        dve.tensor_scalar(bias_x[:, 128:256], row_c[:, 128:256], tgate[:, 1:2], None,
                                          ALU.mult).then_inc(bias_ready, 1)
                    k = j - 3
                    if here(k):
                        dve.wait_ge(S["prob"], k + 1)
                        if k >= 1:
                            dve.wait_ge(S["x"], k)
                        link(dve.reciprocal(rinv[:, :], rsum[:, CHUNK * (k % 2):CHUNK * (k % 2 + 1)]))
                        link(dve.tensor_scalar(rinv[:, :], rinv[:, :], tgate[:, L:L + 1], None, ALU.mult))
                        dve.wait_ge(S["o_pe"], k + 1)
                        dve.wait_ge(S["xb"], k + 1)
                        for i in range(CHUNK):
                            xt = x_res[:, k * W + i * D:k * W + (i + 1) * D]
                            ins = dve.scalar_tensor_tensor(xt, banks[:, 7, i * D:(i + 1) * D], rinv[:, i:i + 1],
                                                           xt, ALU.mult, ALU.add)
                        ins.then_inc(S["x"], 1)
                        if L == 0:
                            dve.wait_ge(S["x"], k + 1)
                            if k >= 2:
                                dve.wait_ge(m_ln, k - 1)
                            statistics(k, 1, m_stats)

            dve.wait_ge(small_in, 48)
            dve.tensor_copy(vff_tmp[:, 0:128], spread(bv0[:, 0], 1, 128)).then_inc(bv_ready, 1)
            dve.wait_ge(consts_in, 16)
            dve.tensor_copy(ident_b[:, :], ident).then_inc(ident_b_ready, 1)
            attention(0)

            def route(S, lg, log_bank, oh, copies):
                dve.wait_ge(S["lgT_pe"], 1)
                link(dve.tensor_copy(lg, banks[:, log_bank, 0:256]))
                for q in range(4):
                    ins = dve.max(v8[:, 8 * q:8 * q + 8], lg[:, 64 * q:64 * q + 64])
                link(ins)
                for q in range(4):
                    ins = dve.max_index(ix8[:, 8 * q:8 * q + 8], v8[:, 8 * q:8 * q + 8], lg[:, 64 * q:64 * q + 64])
                v = v8[:, :].rearrange("p (q k) -> p q k", k=8)
                dve.tensor_tensor(gap[:, :], v[:, :, 1], v[:, :, 0], ALU.subtract).then_inc(S["gap"], 1)
                dve.wait_ge(S["gap"], 1)
                link(dve.tensor_copy(idx[:, :].rearrange("p (q s) -> p q s", s=2),
                                     ix8[:, :].rearrange("p (q k) -> p q k", k=8)[:, :, 0:2]))
                for i in range(copies):
                    ins = dve.tensor_tensor(oh.rearrange("p (m i e) -> p m i e", i=copies, e=64)[:, :, i, :],
                                            spread(iota, 1, 8), spread(idx[:, :], 2, 64), ALU.is_equal)
                ins.then_inc(S["oh"], 1)
                dve.wait_ge(S["egap"], 1)
                link(dve.tensor_scalar(den[:, :], egap[:, :], 1.0, None, ALU.add))
                p2 = pr[:, :].rearrange("p (q s) -> p q s", s=2)
                link(dve.reciprocal(p2[:, :, 0], den[:, :]))
                link(dve.tensor_tensor(p2[:, :, 1], p2[:, :, 0], egap[:, :], ALU.mult))

            route(ru, lg_up, 3, oh_up, 2)
            prq = pr[:, :].rearrange("p (k x s) -> p k x s", k=2, x=2)
            for x in range(2):
                ins = dve.tensor_copy(prb_up[:, x * 128:(x + 1) * 128].rearrange("p (k s i) -> p k s i", k=2, s=2),
                                      spread(prq[:, :, x, :], 3, 32))
            ins.then_inc(ru["prb"], 1)
            dve.wait_ge(ru["oh_pe"], 1)
            dve.tensor_copy(oh_up_T[:, 512:1024].rearrange("p (s P x) -> p s x P", s=2, x=2),
                            banks[:, 5, :].rearrange("p (s x P) -> p s x P", s=2, x=2)).then_inc(ru["ohT_d"], 1)
            dve.wait_ge(ru["pb_pe"], 1)
            dve.tensor_copy(prob_up[:, :].rearrange("p (P x) -> p x P", x=2),
                            banks[:, 6, 0:256].rearrange("p (x P) -> p x P", x=2)).then_inc(ru["pb"], 1)
            for u in range(1, 32, 2):
                dve.wait_ge(g_pe, u + 1)
                dst = (g_b if u < 16 else g_a)[:, :].rearrange("p (m c) -> p c m", c=64)
                dve.tensor_copy(dst[:, 4 * (u % 16):4 * (u % 16) + 4, :],
                                banks[:, 2 * (u % 4):2 * (u % 4) + 2, :].rearrange("p b (c m) -> p (b c) m", c=2)
                                ).then_inc(g_dve, 1)

            dve.wait_ge(ru["pb"], 1)
            dve.wait_ge(router_in, 16 * 7)
            for j in range(TILES + 1):
                t = j
                if t < TILES:
                    dve.wait_ge(s1_pe, t + 1)
                    if t >= 2:
                        dve.wait_ge(s2_pe, t - 1)
                    for k in range(2):
                        part = slice(64 * k, 64 * k + 64)
                        ins = dve.tensor_tensor(
                            t_bd(t).rearrange("p (m k c) -> p m k c", m=8, k=2)[part, :, k, :],
                            banks[part, t % 3, :].rearrange("p (m c) -> p m c", m=8),
                            spread(prob_up[part, t * 8:(t + 1) * 8], 2, 64), ALU.mult)
                    ins.then_inc(tbd_ready, 1)
                t = j - 1
                if t >= 0:
                    dve.wait_ge(s2_pe, t + 1)
                    dve.scalar_tensor_tensor(
                        h_all[:, t * 512:(t + 1) * 512].rearrange("p (m c) -> p m c", c=64),
                        banks[:, 3 + t % 3, :].rearrange("p (m c) -> p m c", c=64), gate[:, 4:5],
                        spread(bup[:, :], 1, 8), ALU.mult, ALU.add).then_inc(hb_ready, 1)

            raw = raw_dn[0:64, :].rearrange("p (m i) -> p m i", m=64)
            for part in range(2):
                dve.wait_ge(split_act, 2 * part + 1)
                v = dn_part[part].rearrange("p (m x i) -> p m x i", m=64, x=2)[0:64, :, 0, :]
                dve.tensor_tensor(raw, raw, v, ALU.subtract).then_inc(split_dve, 1)

            route(rd, lg_dn, 7, oh_dn, 1)
            dve.tensor_copy(prb_dn.rearrange("p (m c) -> p m c", c=64), spread(pr[:, :], 2, 64)).then_inc(rd["prb"], 1)
            dve.wait_ge(rd["oh_pe"], 2)
            dve.tensor_copy(oh_b_T.rearrange("p (s m q) -> p q s m", s=2, q=4),
                            banks[:, 1, :].rearrange("p (q s m) -> p q s m", q=4, s=2)).then_inc(rd["ohT_d"], 1)
            dve.wait_ge(rd["pb_pe"], 1)
            dve.tensor_copy(prob_dn.rearrange("p (m g) -> p g m", g=8),
                            banks[:, 2, :].rearrange("p (g m) -> p g m", g=8)).then_inc(rd["pb"], 1)
            dve.tensor_tensor(down_scale[:, :], gate[:, 5:6], tgate[:, 2:3], ALU.mult)
            link(dve.tensor_scalar(bdn[:, :], bdn[:, :], tgate[:, 2:3], None, ALU.mult))
            dve.wait_ge(abd_zero, 2)
            dve.wait_ge(rd["pb"], 1)
            for k in range(4):
                for v in range(8):
                    dve.wait_ge(da_pe, 8 * k + v + 1)
                    dst = a_bd.rearrange("p (m x s o) -> p o s m x", m=64, x=2, s=2)
                    src = banks[:, v % 4, :].rearrange("p (o s m) -> p o s m", o=4, s=2)
                    dve.tensor_copy(dst[64:128, 4 * v:4 * v + 4, :, :, 1], src[64:128]).then_inc(da_dve, 1)
                for v in range(1, 8, 2):
                    dve.wait_ge(db_pe, 8 * k + v + 1)
                    dst = b_nat.rearrange("p (m s o) -> p o s m", m=64, s=2)
                    src = banks[:, v % 4, :].rearrange("p (o s m) -> p o s m", o=4, s=2)
                    dve.tensor_copy(dst[:, 4 * v:4 * v + 4, :, :], src).then_inc(db_dve, 1)
                for j in range(9):
                    t = 8 * k + j
                    if j < 8:
                        dve.wait_ge(d1_pe, t + 1)
                        if t >= 2:
                            dve.wait_ge(d2_pe, t - 1)
                        for c in range(2):
                            part = slice(64 * c, 64 * c + 64)
                            ins = dve.tensor_tensor(
                                u_bd(t).rearrange("p (m c o) -> p m c o", m=16, c=2)[part, :, c, :],
                                banks[part, 4 + t % 2, :].rearrange("p (m o) -> p m o", m=16),
                                spread(prob_dn[part, t * 16:(t + 1) * 16], 2, 32), ALU.mult)
                        ins.then_inc(ubd_ready, 1)
                    t = 8 * k + j - 1
                    if j >= 1:
                        dve.wait_ge(d2_pe, t + 1)
                        if t >= 2:
                            dve.wait_ge(y_rows, t - 1)
                        bias = spread(bdn[:, :].rearrange("p (r b) -> p r b", b=4), 1, 4)
                        dve.scalar_tensor_tensor(
                            y_t(t).rearrange("p (b n r) -> p n r b", b=4, n=4),
                            banks[:, 6 + t % 2, 0:128].rearrange("p (n r b) -> p n r b", n=4, b=4), down_scale[:, :],
                            bias, ALU.mult, ALU.add).then_inc(y_ev, 1)
                        dve.wait_ge(y_ev, t + 1)
                        if t >= 2:
                            dve.wait_ge(x2, t - 1)
                        dve.transpose(y_r(t), y_t(t)).then_inc(y_rows, 1)

            attention(1)

            dve.wait_ge(lora_in, 16 * 9)
            link(dve.tensor_copy(lb_hi, lb_raw))
            link(dve.tensor_tensor(lb_raw, lb_raw, lb_hi, ALU.subtract))
            link(dve.tensor_copy(lb_mid, lb_raw))
            link(dve.tensor_tensor(lb_raw, lb_raw, lb_mid, ALU.subtract))
            link(dve.tensor_scalar(lb_part, lb_raw, sel[:, 2:3], None, ALU.mult))
            link(dve.scalar_tensor_tensor(lb_part, lb_mid, sel[:, 1:2], lb_part, ALU.mult, ALU.add))
            dve.scalar_tensor_tensor(lb_part, lb_hi, sel[:, 0:1], lb_part, ALU.mult, ALU.add).then_inc(ff["lb"], 1)

            def f_stats(k):
                dve.wait_ge(att[1]["x"], k + 1)
                if k >= 2:
                    dve.wait_ge(ff["ln"], k - 1)
                statistics(k, 1, ff["stats"])

            f_stats(0)
            for j in steps(2):
                k = j - 2
                if here(k):
                    for fc in range(FC):
                        dve.wait_ge(ff["z2_pe"], FC * k + fc + 1)
                        if k >= 1 and fc == 0:
                            dve.wait_ge(ff["o_pe"], k)
                        dve.tensor_scalar(h2_s[:, fc * W:(fc + 1) * W], banks[:, 2 + (FC * k + fc) % 3, :],
                                          0.0, None, ALU.max).then_inc(ff["h2"], 1)
                if here(j + 1):
                    f_stats(j + 1)
                k = j
                if here(k):
                    dve.wait_ge(ff["proj_pe"], k + 1)
                    pk = proj(k).rearrange("p (t c) -> p t c", c=PROJ)
                    pp = banks[:, 7, 0:CHUNK * PROJ].rearrange("p (t c) -> p t c", c=PROJ)
                    dve.tensor_tensor(pk[:, :, 0:LORA_E], pp[:, :, 0:LORA_E],
                                      spread(row_c[:, 256:260], 1, CHUNK), ALU.add)
                    dve.tensor_copy(pk[:, :, LORA_E:PROJ], pp[:, :, LORA_E:PROJ]).then_inc(ff["proj"], 1)
                    dve.wait_ge(ff["proj"], k + 1)
                    lg = pk[:, :, 0:LORA_E]
                    low = pk[:, :, LORA_E:PROJ].rearrange("p t (e r) -> p t e r", e=LORA_E)
                    e3 = lambda ap: ap.rearrange("p (t e) -> p t e", e=LORA_E)
                    pair = lambda ap: ap.rearrange("p (t e f) -> p t e f", e=LORA_E, f=LORA_E)
                    link(dve.tensor_reduce(r_max, lg, AX_X, ALU.max))
                    dve.tensor_tensor(e3(r_sh), lg, spread(r_max, 2, LORA_E), ALU.subtract).then_inc(ff["exp_in"], 1)
                    other, own = spread(lg, 2, LORA_E), spread(lg, 3, LORA_E)
                    dve.tensor_tensor(pair(r_gt), other, own, ALU.is_gt)
                    link(dve.tensor_tensor(pair(r_eq), other, own, ALU.is_equal))
                    link(dve.tensor_tensor(pair(r_eq), pair(r_eq),
                                           spread(tri.rearrange("p (e f) -> p e f", f=LORA_E), 1, CHUNK), ALU.mult))
                    link(dve.tensor_tensor(r_gt, r_gt, r_eq, ALU.add))
                    link(dve.tensor_reduce(e3(r_rank), pair(r_gt), AX_X, ALU.add))
                    mask = r_mask.rearrange("p (t s e) -> p t s e", s=2, e=LORA_E)
                    link(dve.tensor_tensor(mask, spread(e3(r_rank), 2, 2),
                                           spread(spread(slot_id, 1, CHUNK), 3, LORA_E), ALU.is_equal))
                    if k >= 1:
                        dve.wait_ge(ff["parts"], k)
                    lo4 = l_low.rearrange("p (v t e r) -> p v t e r", v=2, t=CHUNK, e=LORA_E)
                    for s in range(2):
                        ins = dve.tensor_tensor(lo4[:, s], low, spread(mask[:, :, s, :], 3, LORA_R), ALU.mult)
                    link(ins)
                    dve.tensor_tensor(l_low[:, 64:128], l_low[:, 64:128], l_low[:, 0:64],
                                      ALU.subtract).then_inc(ff["low"], 1)
                    dve.wait_ge(ff["exp"], k + 1)
                    dve.tensor_reduce(r_sum, e3(r_exp), AX_X, ALU.add)
                    link(dve.tensor_tensor(r_pick.rearrange("p (t s e) -> p t s e", s=2, e=LORA_E), mask,
                                           spread(e3(r_exp), 2, 2), ALU.mult))
                    dve.reciprocal(r_inv, r_sum)
                    link(dve.tensor_reduce(r_wr.rearrange("p (t s) -> p t s", s=2),
                                           r_pick.rearrange("p (t s e) -> p t s e", s=2, e=LORA_E), AX_X, ALU.add))
                    link(dve.tensor_scalar(r_inv, r_inv, tgate[:, 3:4], None, ALU.mult))
                    link(dve.tensor_tensor(r_w(k).rearrange("p (t s) -> p t s", s=2),
                                           r_wr.rearrange("p (t s) -> p t s", s=2), spread(r_inv, 2, 2), ALU.mult))
                k = j - 2
                if here(k):
                    dve.wait_ge(ff["o_pe"], k + 1)
                    for s in range(2):
                        for i in range(CHUNK):
                            xt = x_res[:, k * W + i * D:k * W + (i + 1) * D]
                            ins = dve.scalar_tensor_tensor(xt, banks[:, 5 + s, i * D:(i + 1) * D],
                                                           r_w(k)[:, 2 * i + s:2 * i + s + 1], xt,
                                                           ALU.mult, ALU.add)
                        if s == 0:
                            link(ins)
                    ins.then_inc(ff["y"], 1)

        @block.tensor
        def _(pe):
            def tiles4(fn):
                for i in range(CHUNK):
                    ins = fn(slice(i * D, (i + 1) * D))
                return ins

            def transpose4(bank, src):
                return tiles4(lambda c: pe.transpose(banks[:, bank, c], src[:, c], ident))

            def attention(L):
                S = att[L]
                for j in steps(4 if L == 0 else 3):
                    k = j - 2
                    if here(k):
                        pe.wait_ge(S["k"], k + 1)
                        pe.wait_ge(S["q"], k + 1)
                        if k >= 1:
                            pe.wait_ge(S["s_ev"], k)
                        tiles4(lambda c: pe.matmul(banks[:, 4, c], qT_s(k)[:, c], kT_s(k)[:, c],
                                                   start=True, stop=True)).then_inc(S["s_pe"], 1)
                    k = j - 3
                    if here(k):
                        pe.wait_ge(S["prob"], k + 1)
                        if k >= 1:
                            pe.wait_ge(S["pt"], k)
                        transpose4(5, prob_s(k)).then_inc(S["pt_pe"], 1)
                    k = j
                    if here(k):
                        pe.wait_ge(ctx_in_sem[L][k % 4], 16 * (k // 4 + 1))
                        if k == 0:
                            pe.wait_ge(consts_in, 16)
                        if k >= 1:
                            pe.wait_ge(S["ctxT"], k)
                        if L == 0 and here(k - 5):
                            pe.wait_ge(m_lnT, k - 4)
                        transpose4(0, ctx_ring(L, k)).then_inc(S["ctxT_pe"], 1)
                        pe.wait_ge(S["ln"], k + 1)
                        if k >= 1:
                            pe.wait_ge(S["lnT"], k)
                        transpose4(1, ln_s(k)).then_inc(S["lnT_pe"], 1)
                    if L == 0 and j == 0:
                        pe.wait_ge(weights_in, 16)
                        pe.wait_ge(bv_ready, 1)
                        pe.matmul(banks[:, 7, 0:128], wv0, wff_t, start=True, stop=True)
                        pe.matmul(banks[:, 7, 128:256], vff_tmp[:, 0:128], wff_t, start=True,
                                  stop=True).then_inc(vff_pe, 1)
                    k = j - 3
                    if here(k):
                        pe.wait_ge(S["pt"], k + 1)
                        if k >= 1:
                            pe.wait_ge(S["u"], k)
                        tiles4(lambda c: pe.matmul(banks[:, 6, c], ctx_ring(L, k)[:, c], pT_s(k)[:, c],
                                                   start=True, stop=True)).then_inc(S["u_pe"], 1)
                    k = j - 1
                    if here(k):
                        pe.wait_ge(S["ctxT"], k + 1)
                        if k >= 1:
                            pe.wait_ge(S["k"], k)
                        pe.matmul(banks[:, 2, :], wk[L], ctxT_s(k), start=True, stop=True).then_inc(S["k_pe"], 1)
                        pe.wait_ge(S["lnT"], k + 1)
                        if k >= 1:
                            pe.wait_ge(S["q"], k)
                        pe.matmul(banks[:, 3, :], wq[L], lnT_s(k), start=True, stop=True).then_inc(S["q_pe"], 1)
                    k = j - 3
                    if here(k):
                        pe.wait_ge(S["u"], k + 1)
                        if L == 0 and k == 0:
                            pe.wait_ge(vff_ready, 1)
                            pe.wait_ge(bias_ready, 2)
                        if k >= 1:
                            pe.wait_ge(S["x"], k)
                        tiles4(lambda c: pe.matmul(banks[:, 7, c], uT_s(k)[:, c], wout[L],
                                                   start=True, stop=True)).then_inc(S["o_pe"], 1)
                    k = j - 4
                    if L == 0 and here(k):
                        pe.wait_ge(m_ln, k + 1)
                        pe.wait_ge(S["ctxT"], min(j + 1, CHUNKS))
                        if k >= 1:
                            pe.wait_ge(m_lnT, k)
                        transpose4(0, mln_s(k)).then_inc(m_lnT_pe, 1)

            attention(0)

            pe.wait_ge(m_lnT, CHUNKS)
            pe.wait_ge(router_in, 16 * 7)
            tok = lnT_all.rearrange("p (n r) -> p n r", r=8)
            for r in range(8):
                ins = pe.matmul(banks[0:64, 2, :], wu[:, r * 64:(r + 1) * 64], tok[:, :, r],
                                start=(r == 0), stop=(r == 7))
            ins.then_inc(ru["log_pe"], 1)
            pe.wait_ge(ru["log"], 1)
            for q in range(4):
                ins = pe.transpose(banks[:, 3, q * 64:(q + 1) * 64], logT_up[:, q * 128:(q + 1) * 128], ident[0:64, 0:64])
            ins.then_inc(ru["lgT_pe"], 1)
            pe.wait_ge(ru["oh"], 1)
            pe.wait_ge(ident_b_ready, 1)
            oh = oh_up.rearrange("p (k x s e) -> p k x s e", k=2, x=2, s=2)
            for k in range(2):
                for s in range(2):
                    for x in range(2):
                        c = (s * 2 + x) * 128
                        ins = pe.matmul(banks[:, 4 + k, c:c + 128], oh[:, k, x, s, :],
                                        ident_b[:, :], start=True, stop=True)
            ins.then_inc(ru["oh_pe"], 1)
            pe.wait_ge(ru["prb"], 1)
            for x in range(2):
                ins = pe.matmul(banks[:, 6, x * 128:(x + 1) * 128], prb_up[:, x * 128:(x + 1) * 128], ident,
                                start=True, stop=True)
            ins.then_inc(ru["pb_pe"], 1)
            pe.wait_ge(ru["ohT_a"], 1)
            pe.wait_ge(ru["ohT_d"], 1)
            pe.wait_ge(ru["pb"], 1)
            pe.wait_ge(tables_up, 1)
            for u in range(32):
                if u >= 4:
                    pe.wait_ge(g_act if u % 2 == 0 else g_dve, (u - 4) // 2 + 1)
                tb = u // 16
                for ci in range(4):
                    col = 4 * (u % 16) + ci
                    for g in range(4):
                        o = banks[32 * g:32 * g + 32, 2 * (u % 4) + ci // 2, (ci % 2) * 256:(ci % 2) * 256 + 256]
                        rhs = oh_up_T[:, g * 256:(g + 1) * 256]
                        pe.matmul(o, up_hm[tb][:, col * 32:(col + 1) * 32], rhs, start=True, stop=False)
                        ins = pe.matmul(o, up_lo[tb][:, col * 32:(col + 1) * 32], rhs, start=False, stop=True)
                ins.then_inc(g_pe, 1)
            pe.wait_ge(g_act, 16)
            pe.wait_ge(g_dve, 16)
            for j in range(TILES + 1):
                t = j
                if t < TILES:
                    pe.wait_ge(xbd_ready, t + 1)
                    if t >= 3:
                        pe.wait_ge(tbd_ready, t - 2)
                    for k in range(2):
                        for m in range(8):
                            ins = pe.matmul(banks[64 * k:64 * k + 64, t % 3, m * 64:(m + 1) * 64],
                                            x_bd(t)[:, m * 128 + k * 64:m * 128 + k * 64 + 64],
                                            g_b[:, t * 512 + m * 64:t * 512 + (m + 1) * 64], start=True, stop=True)
                    ins.then_inc(s1_pe, 1)
                t = j - 1
                if t >= 0:
                    pe.wait_ge(tbd_ready, t + 1)
                    if t >= 3:
                        pe.wait_ge(hb_ready, t - 2)
                    for m in range(8):
                        n, x = m // 2, m % 2
                        ins = pe.matmul(banks[64 * x:64 * x + 64, 3 + t % 3, n * 128:(n + 1) * 128],
                                        g_a[:, t * 512 + m * 64:t * 512 + (m + 1) * 64],
                                        t_bd(t)[:, m * 128:(m + 1) * 128], start=True, stop=True)
                    ins.then_inc(s2_pe, 1)

            pe.wait_ge(h_ready, TILES)
            pe.wait_ge(wd_in, 32)
            pe.wait_ge(wd_zero, 1)
            hp = h_all[:, :].rearrange("p (m c) -> p m c", c=64)
            for c in range(64):
                ins = pe.matmul(banks[:, 6, 0:256], wd_bd[:, c * 128:(c + 1) * 128], hp[:, :, c],
                                start=(c == 0), stop=(c == 63))
            ins.then_inc(rd["log_pe"], 1)
            pe.wait_ge(rd["log"], 1)
            lt2 = logT_dn.rearrange("p (P k) -> p P k", k=2)
            for k in range(2):
                ins = pe.transpose(banks[:, 7, k * 128:(k + 1) * 128], lt2[:, :, k], ident)
            ins.then_inc(rd["lgT_pe"], 1)
            pe.wait_ge(rd["oh"], 1)
            oh = oh_dn.rearrange("p (k x s e) -> p k x s e", k=2, x=2, s=2)
            for k in range(2):
                for s in range(2):
                    for x in range(2):
                        c = (k * 2 + s) * 128
                        ins = pe.matmul(banks[64 * x:64 * x + 64, 0, c:c + 128], oh[:, k, x, s, :], ident_b[:, :],
                                        start=True, stop=True)
            ins.then_inc(rd["oh_pe"], 1)
            ohq = oh_dn.rearrange("p (m e) -> p m e", e=64)
            par = lambda ap, c: ap.rearrange("p (m c) -> p m c", c=2)[:, :, c]
            for m in range(8):
                for c in range(2):
                    ins = pe.matmul(banks[64 * c:64 * c + 64, 1, m * 64:(m + 1) * 64], ohq[:, m, :],
                                    par(ident_b[:, :], c), start=True, stop=True)
            ins.then_inc(rd["oh_pe"], 1)
            pe.wait_ge(rd["prb"], 1)
            for m in range(8):
                for c in range(2):
                    ins = pe.matmul(banks[64 * c:64 * c + 64, 2, m * 64:(m + 1) * 64],
                                    prb_dn[:, m * 64:(m + 1) * 64], par(ident, c), start=True, stop=True)
            ins.then_inc(rd["pb_pe"], 1)
            pe.wait_ge(rd["ohT_a"], 1)
            pe.wait_ge(rd["ohT_d"], 1)
            pe.wait_ge(rd["pb"], 1)
            pe.wait_ge(split_act, 6)
            pe.wait_ge(split_zero, 3)
            pe.wait_ge(abd_zero, 2)
            part = [v.rearrange("p (tb o c) -> p tb o c", tb=2, o=32) for v in dn_part]
            for k in range(4):
                for tb in range(2):
                    ohT = (oh_a_T if tb == 0 else oh_b_T).rearrange("p (s m) -> p s m", s=2)[:, :, 64 * k:64 * k + 64]
                    for v in range(8):
                        if tb == 1 or (v >= 4):
                            if tb == 1 and v >= 4:
                                n = 4 * k + (v - 4) // 2 + 1
                                pe.wait_ge(db_act if v % 2 == 0 else db_dve, n)
                            else:
                                n = 8 * k + (v - 4) % 8 + 1
                                pe.wait_ge(da_act, n)
                                pe.wait_ge(da_dve, n)
                        elif k >= 1:
                            pe.wait_ge(db_act if v % 2 == 0 else db_dve, 4 * (k - 1) + (v + 4) // 2 + 1)
                        for oi in range(4):
                            for i in range(3):
                                ins = pe.matmul(banks[:, v % 4, oi * 128:(oi + 1) * 128],
                                                part[i][:, tb, 4 * v + oi, :], ohT, start=(i == 0), stop=(i == 2))
                        ins.then_inc(da_pe if tb == 0 else db_pe, 1)
                pe.wait_ge(da_act, 8 * k + 8)
                pe.wait_ge(da_dve, 8 * k + 8)
                for j in range(9):
                    t = 8 * k + j
                    if j < 8:
                        if t >= 2:
                            pe.wait_ge(ubd_ready, t - 1)
                        for n4h in range(2):
                            for k2 in range(2):
                                for c in range(2):
                                    m = (n4h * 2 + c) * 2 + k2
                                    o = (n4h * 2 + k2) * 128
                                    ins = pe.matmul(banks[64 * c:64 * c + 64, 4 + t % 2, o:o + 128],
                                                    h_all[:, t * 512 + m * 64:t * 512 + (m + 1) * 64],
                                                    a_bd[:, (j * 8 + m) * 128:(j * 8 + m + 1) * 128],
                                                    start=True, stop=True)
                        ins.then_inc(d1_pe, 1)
                    t = 8 * k + j - 1
                    if j >= 1:
                        if j == 1:
                            pe.wait_ge(db_act, 4 * k + 4)
                            pe.wait_ge(db_dve, 4 * k + 4)
                        pe.wait_ge(ubd_ready, t + 1)
                        if t >= 2:
                            pe.wait_ge(y_ev, t - 1)
                        for n4h in range(2):
                            for q in range(4):
                                for s in range(2):
                                    m = n4h * 4 + q
                                    ins = pe.matmul(banks[32 * q:32 * q + 32, 6 + t % 2, n4h * 64:(n4h + 1) * 64],
                                                    b_nat[:, (((j - 1) * 8 + m) * 2 + s) * 32:(((j - 1) * 8 + m) * 2 + s + 1) * 32],
                                                    u_bd(t)[:, (m * 2 + s) * 64:(m * 2 + s + 1) * 64],
                                                    start=(s == 0), stop=(s == 1))
                        ins.then_inc(d2_pe, 1)

            attention(1)

            pe.wait_ge(lora_in, 16 * 9)
            pe.wait_ge(ff["lb"], 1)
            for j in steps(2):
                k = j
                if here(k):
                    pe.wait_ge(ff["ln"], k + 1)
                    if k >= 1:
                        pe.wait_ge(ff["lnT"], k)
                    transpose4(0, f_ln(k)).then_inc(ff["lnT_pe"], 1)
                k = j - 2
                if here(k):
                    pe.wait_ge(ff["lora"], k + 1)
                    lv = lora_T(k).rearrange("p (v m) -> p v m", v=2)

                    def slot0(fc):
                        n = FC * k + fc
                        f = slice(fc * 128, (fc + 1) * 128)
                        if n >= 3:
                            pe.wait_ge(ff["h2"], n - 2)
                        pe.matmul(banks[:, 2 + n % 3, :], wi_s[:, f], f_lnT(k), start=True, stop=False)
                        pe.matmul(banks[:, 2 + n % 3, :], lb_part[:, f], lv[:, 0, :], start=False, stop=True,
                                  ).then_inc(ff["z1_pe"], 1)

                    def slot1(fc):
                        n = FC * k + fc
                        f = slice(fc * 128, (fc + 1) * 128)
                        pe.wait_ge(ff["h1"], n + 1)
                        pe.matmul(banks[:, 2 + n % 3, :], lb_part[:, f], lv[:, 1, :], start=False, stop=True,
                                  skip_group_check=True).then_inc(ff["z2_pe"], 1)

                    slot0(0)
                    slot0(1)
                    slot1(0)
                    slot0(2)
                    slot1(1)
                    slot0(3)
                    slot1(2)
                    slot1(3)
                k = j
                if here(k):
                    pe.wait_ge(ff["lnT"], k + 1)
                    if k >= 1:
                        pe.wait_ge(ff["proj"], k)
                    for i in range(CHUNK):
                        ins = pe.matmul(banks[:, 7, i * PROJ:(i + 1) * PROJ], f_lnT(k)[:, i * D:(i + 1) * D],
                                        wga_s, start=True, stop=True)
                    ins.then_inc(ff["proj_pe"], 1)
                k = j - 1
                if here(k):
                    pe.wait_ge(ff["parts"], k + 1)
                    if k >= 1:
                        pe.wait_ge(ff["lora"], k)
                    lp = l_parts.rearrange("p (m c) -> p m c", m=2 * CHUNK)
                    lb = banks[0:96, 1, :].bitcast(BF16).rearrange("p (m c) -> p m c", m=2 * CHUNK)
                    for m in range(2 * CHUNK):
                        ins = pe.transpose(lb[:, m, :], lp[:, m, :], ident_b[:, :])
                    ins.then_inc(ff["lora_pe"], 1)
                k = j - 2
                if here(k):
                    if k >= 1:
                        pe.wait_ge(ff["y"], k)
                    for s in range(2):
                        hs = h1_s if s == 0 else h2_s
                        pe.wait_ge(ff["h1"] if s == 0 else ff["h2"], FC * (k + 1))
                        for i in range(CHUNK):
                            for fc in range(FC):
                                ins = pe.matmul(banks[:, 5 + s, i * D:(i + 1) * D],
                                                hs[:, fc * W + i * D:fc * W + (i + 1) * D],
                                                wo_s[:, fc * 128:(fc + 1) * 128], start=(fc == 0), stop=(fc == FC - 1))
                    ins.then_inc(ff["o_pe"], 1)


def kernel(**inputs):
    import numpy as np
    import concourse.bacc as bacc
    from concourse import mybir as _mybir
    from concourse.bass_utils import run_bass_kernel_spmd

    v = {k: np.asarray(a) for k, a in inputs.items()}
    f32 = np.float32
    r = np.arange(128)
    same = (r[:, None] // 64) == (r[None, :] // 64)
    e4 = np.arange(4)
    consts = np.zeros((128, 472), f32)
    consts[:, 0:128] = np.eye(128, dtype=f32)
    consts[:, 128:256] = np.where(same & (r[None, :] <= r[:, None]), 0.0, -1e30)
    consts[:, 256:384] = np.where(same, 0.0, -1e30)
    consts[:, 384:448] = np.arange(64)
    consts[:, 448:464] = (e4[None, :] < e4[:, None]).reshape(-1)
    consts[:, 464:466] = np.arange(2)
    place = r[:96] // 16
    for c, places in enumerate(((0, 1, 5), (2, 3), (4,))):
        consts[:96, 466 + c] = np.isin(place, places)

    def t(name):
        return v[name].T

    arrays = {
        "x": v["x"].reshape(TILES, 128, D),
        "ctx": v["ctx_1024"].reshape(TILES, 128, D),
        "consts": consts,
        "gates": np.concatenate([v["g_xattn"], v["g_ffn"], v["L0_ffn_scale_up"], v["L0_ffn_scale_down"]])[None, :],
        "rows": np.concatenate([v["L0_xattn_bff"], v["L1_xattn_bv"], v["L1_ffn_bg"]])[None, :],
        "cols": np.stack([v["L0_xattn_bq"], v["L0_xattn_bk"], v["L0_xattn_bv"], v["L1_xattn_bq"],
                          v["L1_xattn_bk"]], axis=1),
        "attn_w": np.concatenate([t("L0_xattn_Wq"), t("L0_xattn_Wk"), t("L0_xattn_Wff"), v["L0_xattn_Wv"],
                                  t("L1_xattn_Wq"), t("L1_xattn_Wk"), t("L1_xattn_Wv")], axis=1),
        "w_up_router": v["L0_ffn_W_up"].reshape(64, 8, 128).transpose(2, 1, 0).reshape(128, 512),
        "w_down_router": v["L0_ffn_W_down"].reshape(64, 64, 64).transpose(1, 2, 0),
        "a_up": v["L0_ffn_A_up"].reshape(64, 64, 8, 4).transpose(0, 1, 3, 2).reshape(64, 2048),
        "b_up": v["L0_ffn_B_up"].reshape(64, 2048),
        "a_down": v["L0_ffn_A_down"].reshape(64, 2048),
        "b_down": v["L0_ffn_B_down"].reshape(64, 2048),
        "bias_up": v["L0_ffn_bias_up"].reshape(64, 64),
        "bias_down": v["L0_ffn_bias_down"].reshape(32, 32).T,
        "wi_t": t("L1_ffn_Wi"),
        "wo_t": v["L1_ffn_Wo"].T.reshape(FC, 128, D).transpose(1, 0, 2).reshape(128, FC * D),
        "wg_a": np.concatenate([t("L1_ffn_Wg"), v["L1_ffn_A"].reshape(LR, D).T], axis=1),
        "lora_b": v["L1_ffn_B"].transpose(0, 2, 1).reshape(LR, HIDDEN),
    }
    nc = bacc.Bacc("TRN2", target_bir_lowering=False, num_devices=1)
    feed, args = {}, []
    for name, a in arrays.items():
        a = np.ascontiguousarray(a)
        feed[f"in_{name}"] = a
        args.append(nc.dram_tensor(f"in_{name}", a.shape, _mybir.dt.from_np(a.dtype), kind="ExternalInput").ap())
    res = nc.dram_tensor("out_x", (TILES, 128, D), _mybir.dt.float32, kind="ExternalOutput").ap()
    flamingo_kernel(nc, *args, res)
    got = run_bass_kernel_spmd(nc, [feed], core_ids=[0])
    return got.results[0]["out_x"].reshape(64, 64, D)
```

```python
from contextlib import ExitStack

import concourse.bass as bass
from concourse import mybir

F32 = mybir.dt.float32
BF16 = mybir.dt.bfloat16
U32 = mybir.dt.uint32
I32 = mybir.dt.int32
ALU = mybir.AluOpType
ACT = mybir.ActivationFunctionType
AX_X = mybir.AxisListType.X

ROWS, D = 4096, 128
TILES = ROWS // 128
CHUNK = 4
W = CHUNK * D
CHUNKS = TILES // CHUNK
EXPERTS = 64
EPS = 1e-5
NEWTON = 3
SCALE = float(D) ** -0.5
HIDDEN, FC = 512, 4
LORA_E, LORA_R = 4, 4
LR = LORA_E * LORA_R
PROJ = LORA_E + LR


def spread(ap, axis, n):
    u = ap.unsqueeze(axis)
    shape = list(u.shape)
    shape[axis] = n
    return u.broadcast_to(shape)


def flamingo_kernel(nc, x_in, ctx_in, consts, gates, rows, cols, attn_w, w_up_router, w_down_router,
                    a_up, b_up, a_down, b_down, bias_up, bias_down, wi_t, wo_t, wg_a, lora_b, out):
    with ExitStack() as ctx:
        def sb(name, n, dt=F32, p=128):
            return ctx.enter_context(nc.sbuf_tensor(name, [p, n], dt))

        def sem(name):
            return ctx.enter_context(nc.semaphore(name))

        banks = ctx.enter_context(nc.psum_tensor("banks", [128, 8, 512], F32))

        x_res = sb("x_res", TILES * D)
        region_h = sb("region_h", 16384)
        region_a = sb("region_a", 16384)
        region_t = sb("region_t", 4096)
        region_x = sb("region_x", 4096)
        region_r = sb("region_r", 4096)
        const = sb("const", 472)
        gate = sb("gate", 6)
        tgate = sb("tgate", 4)
        row_c = sb("row_c", 260)
        col_c = sb("col_c", 5)
        w_att = sb("w_att", 7 * 128)
        w_vff = sb("w_vff", 128)
        bias_x = sb("bias_x", 2 * 128)
        shared = sb("shared", 1024)
        prob = sb("prob", 512)
        bup = sb("bup", 64)
        bdn = sb("bdn", 32)
        ident_b = sb("ident_b", 128, BF16)
        stat = sb("stat", CHUNK * 6)
        mv = sb("mv", 2 * CHUNK * 2)
        rstd = sb("rstd", 4 * CHUNK)
        shift = sb("shift", 4 * CHUNK)
        mx = sb("mx", CHUNK)
        newton = sb("newton", 2 * CHUNK)
        negm = sb("negm", 2 * CHUNK)
        rsum = sb("rsum", 2 * CHUNK)
        rinv = sb("rinv", CHUNK)
        v8 = sb("v8", 32)
        ix8 = sb("ix8", 32, U32)
        idx = sb("idx", 8)
        gap = sb("gap", 4)
        egap = sb("egap", 4)
        den = sb("den", 4)
        pr = sb("pr", 8)
        down_scale = sb("down_scale", 1)

        var, half = newton[:, 0:CHUNK], newton[:, CHUNK:2 * CHUNK]
        ident = const[:, 0:128]
        masks = [const[:, 128:256], const[:, 256:384]]
        iota = const[:, 384:448]
        tri = const[:, 448:464]
        slot_id = const[:, 464:466]
        sel = const[0:96, 466:469]
        wq = [w_att[:, 0:128], w_att[:, 512:640]]
        wk = [w_att[:, 128:256], w_att[:, 640:768]]
        wff_t, wv0 = w_att[:, 256:384], w_att[:, 384:512]
        wout = [w_vff[:, :], w_att[:, 768:896]]
        y_t = lambda t: w_att[:, (t % 2) * 128:(t % 2) * 128 + 128]
        y_r = lambda t: w_att[:, 256 + (t % 2) * 128:256 + (t % 2) * 128 + 128]
        bq = [col_c[:, 0:1], col_c[:, 3:4]]
        bk = [col_c[:, 1:2], col_c[:, 4:5]]
        bv0 = col_c[:, 2:3]

        def step_buf(region, at, n, k):
            return region[:, at + (k % n) * W:at + (k % n) * W + W]

        def ctx_ring(L, k):
            return step_buf(region_h, 4096, 4, k) if L == 0 else step_buf(region_t, 2048, 4, k)

        A = region_a
        ctxT_s = lambda k: step_buf(A, 0, 2, k)
        ln_s = lambda k: step_buf(A, 1024, 2, k)
        lnT_s = lambda k: step_buf(A, 2048, 2, k)
        kT_s = lambda k: step_buf(A, 3072, 2, k)
        qT_s = lambda k: step_buf(A, 4096, 2, k)
        sm_s = lambda k: step_buf(A, 5120, 2, k)
        prob_s = lambda k: step_buf(A, 6144, 2, k)
        pT_s = lambda k: step_buf(A, 7168, 2, k)
        uT_s = lambda k: step_buf(A, 8192, 2, k)
        vff_tmp = A[:, 9216:9472]
        mln_s = lambda k: step_buf(A, 12288, 2, k)
        logT_up = A[0:64, 13312:13824]
        lg_up = A[:, 13824:14080]
        oh_up = A[:, 14592:15104].bitcast(BF16)
        prb_up = A[:, 14336:14592]
        logT_dn = A[:, 4096:4352]
        lg_dn = A[:, 4352:4608]
        oh_dn = A[:, 4608:5120].bitcast(BF16)
        prb_dn = A[:, 5120:5632]

        lnT_all = region_h[:, 0:4096]
        raw_up = region_h[:, 8192:12288]
        h_all = region_h
        g_b, g_a = region_h, region_a
        wu = shared[:, 0:512]
        oh_up_T = shared[:, 512:1024].bitcast(BF16)
        oh_a_T = shared[:, 0:512].bitcast(BF16)
        oh_b_T = shared[:, 512:1024].bitcast(BF16)
        up_hm = [region_t[:, 0:1024].bitcast(BF16), region_t[:, 1024:2048].bitcast(BF16)]
        up_lo = [region_t[:, 2048:3072].bitcast(BF16), region_t[:, 3072:4096].bitcast(BF16)]
        xT = region_x
        x_bd = lambda t: region_r[:, (t % 2) * 1024:(t % 2) * 1024 + 1024]
        t_bd = lambda t: region_r[:, 2048 + (t % 2) * 1024:2048 + (t % 2) * 1024 + 1024]
        u_bd = lambda t: region_r[:, (t % 2) * 1024:(t % 2) * 1024 + 1024]
        raw_dn = region_t
        dn_hm = [region_x[:, 0:1024].bitcast(BF16), region_x[:, 1024:2048].bitcast(BF16)]
        dn_lo = [region_x[:, 2048:3072].bitcast(BF16), region_x[:, 3072:4096].bitcast(BF16)]
        wd_bd = region_a[:, 0:8192]
        a_bd = region_a[:, 8192:16384]
        b_nat = region_a[:, 0:4096]

        H = region_h
        f_ln = lambda k: step_buf(H, 0, 2, k)
        f_lnT = lambda k: step_buf(H, 13824, 3, k)
        h1_s = H[:, 2048:4096]
        h2_s = H[:, 4096:6144]
        lora_T = lambda k: H[0:96, 6144 + (k % 2) * 512:6656 + (k % 2) * 512].bitcast(BF16)
        wi_s = H[:, 8192:8704]
        wo_s = H[:, 8704:9216]
        wga_s = H[:, 9216:9236]
        lb_raw = H[0:96, 9728:10240]
        lb_hi = H[0:96, 10240:10496].bitcast(BF16)
        lb_mid = H[0:96, 10496:10752].bitcast(BF16)
        lb_part = H[0:96, 10752:11008].bitcast(BF16)
        proj = lambda k: H[:, 11008 + (k % 2) * 80:11008 + (k % 2) * 80 + 80]
        T0 = 11264
        r_max = H[:, T0:T0 + 4]
        r_sh = H[:, T0 + 16:T0 + 32]
        r_exp = H[:, T0 + 32:T0 + 48]
        r_gt = H[:, T0 + 64:T0 + 128]
        r_eq = H[:, T0 + 128:T0 + 192]
        r_rank = H[:, T0 + 192:T0 + 208]
        r_mask = H[:, T0 + 256:T0 + 288]
        r_pick = H[:, T0 + 288:T0 + 304]
        r_sum = H[:, T0 + 320:T0 + 324]
        r_inv = H[:, T0 + 328:T0 + 332]
        r_wr = H[:, T0 + 336:T0 + 344]
        r_ratio = H[:, T0 + 344:T0 + 348]
        r_w0 = lambda k: H[:, T0 + 352 + 4 * (k % 3):T0 + 356 + 4 * (k % 3)]
        l_low = H[:, T0 + 384:T0 + 512]
        l_rest = H[:, T0 + 512:T0 + 640]
        l_parts = H[:, T0 + 640:T0 + 1024].bitcast(BF16)
        h_s = lambda k: A[:, 10240 + (k % 2) * 2048:12288 + (k % 2) * 2048]
        ratio_T = H[:, 12800:13312]

        consts_in, weights_in, small_in = sem("consts_in"), sem("weights_in"), sem("small_in")
        up_raw_in, down_raw_in, router_in = sem("up_raw_in"), sem("down_raw_in"), sem("router_in")
        lora_in, wd_in = sem("lora_in"), sem("wd_in")
        x_in_sem = [sem(f"x_in_{k}") for k in range(CHUNKS)]
        ctx_in_sem = [sem(f"ctx_in_{i}") for i in range(4)]
        names = ("stats ln xb ctxT_pe lnT_pe ctxT lnT k_pe q_pe k q s_pe s_ev sm prob pt_pe pt u_pe u "
                 "o_pe x").split()
        att = [{n: sem(f"att{L}_{n}") for n in names} for L in range(2)]
        gates_ready, ident_b_ready = sem("gates_ready"), sem("ident_b_ready")
        vff_pe, vff_ready, bv_ready, bias_ready = (sem("vff_pe"), sem("vff_ready"), sem("bv_ready"),
                                                   sem("bias_ready"))
        tables_up = sem("tables_up")
        m_stats, m_ln, m_lnT_pe, m_lnT, m_xt = (sem("m_stats"), sem("m_ln"), sem("m_lnT_pe"),
                                                sem("m_lnT"), sem("m_xt"))
        ru = {n: sem(f"ru_{n}") for n in "log_pe log lgT_pe gap egap oh oh_pe ohT_a ohT_d prb pb_pe pb".split()}
        rd = {n: sem(f"rd_{n}") for n in "log_pe log lgT_pe gap egap oh oh_pe ohT_a ohT_d prb pb_pe pb".split()}
        g_pe, g_act, g_dve = sem("g_pe"), sem("g_act"), sem("g_dve")
        xbd_ready, s1_pe, tbd_ready, s2_pe, hb_ready, h_ready = (
            sem("xbd_ready"), sem("s1_pe"), sem("tbd_ready"), sem("s2_pe"), sem("hb_ready"), sem("h_ready"))
        wd_zero, split_act, split_dve, split_pool, split_zero = (
            sem("wd_zero"), sem("split_act"), sem("split_dve"), sem("split_pool"), sem("split_zero"))
        mv_ready = sem("mv_ready")
        abd_zero = sem("abd_zero")
        da_pe, da_act, da_dve, db_pe, db_act, db_dve = (sem("da_pe"), sem("da_act"), sem("da_dve"),
                                                        sem("db_pe"), sem("db_act"), sem("db_dve"))
        d1_pe, ubd_ready, d2_pe = sem("d1_pe"), sem("ubd_ready"), sem("d2_pe")
        y_ev, y_rows, x2 = sem("y_ev"), sem("y_rows"), sem("x2")
        fnames = ("hi mid rest stats ln lnT_pe lnT proj_pe proj low parts lora_pe lora exp_in exp lb z1_pe z2_pe h1 h2 "
                  "o_pe y ratio_w ratio_pe ratio h").split()
        ff = {n: sem(f"ff_{n}") for n in fnames}
        stored = sem("stored")
        dve_step, pool_step = sem("dve_step"), sem("pool_step")

        block = ctx.enter_context(nc.Block())

        def steps(lag):
            return range(CHUNKS + lag)

        def here(k):
            return 0 <= k < CHUNKS

        SPLIT = 8

        def split_cast(act, n, raw, hm, lo, first):
            tb, stage = ((0, 0), (1, 0), (0, 1), (0, 2), (1, 1), (1, 2), (0, 3), (1, 3))[n]
            src = raw[:, tb * 2048:(tb + 1) * 2048]
            rest = split_pool if first else split_dve
            if stage == 1:
                act.wait_ge(rest, tb + 1)
            if stage == 3:
                act.wait_ge(rest, tb + 3)
            dst, part = ((hm[tb], slice(0, 128)), (hm[tb], slice(64, 128)), (lo[tb], slice(0, 64)),
                         (lo[tb], slice(0, 64)))[stage]
            act.activation(dst[part, :], src[part, :], ACT.Copy).then_inc(split_act, 1)

        def split_rest(eng, n, raw, hm, lo, first):
            tb, part = n % 2, slice(0, 128) if n < 2 else slice(0, 64)
            src = raw[part, tb * 2048:(tb + 1) * 2048]
            eng.wait_ge(split_act, (1, 2, 4, 6)[n] + (0 if first else SPLIT))
            eng.tensor_tensor(src, src, (hm if n < 2 else lo)[tb][part, :], ALU.subtract
                              ).then_inc(split_pool if first else split_dve, 1)

        def linker(eng, step_sem):
            count = [0]

            def link(ins):
                count[0] += 1
                ins.then_inc(step_sem, 1)
                eng.wait_ge(step_sem, count[0])
            return link

        @block.sync
        def _(sp):
            sp.dma_start(x_res[:, 0:W].rearrange("p (t d) -> p t d", t=CHUNK),
                         x_in[0:CHUNK].rearrange("t p d -> p t d")).then_inc(x_in_sem[0], 16)
            sp.dma_start(const[:, :], consts).then_inc(consts_in, 16)
            sp.dma_start(ctx_ring(0, 0).rearrange("p (t d) -> p t d", t=CHUNK),
                         ctx_in[0:CHUNK].rearrange("t p d -> p t d")).then_inc(ctx_in_sem[0], 16)
            sp.dma_start(w_att[:, :], attn_w).then_inc(weights_in, 16)
            sp.dma_start(gate[:, :], gates.broadcast_to([128, 6])).then_inc(small_in, 16)
            sp.dma_start(row_c[:, :], rows.broadcast_to([128, 260])).then_inc(small_in, 16)
            sp.dma_start(col_c[:, :], cols).then_inc(small_in, 16)
            for k in range(1, CHUNKS):
                for i in range(k, k + 1) if k < 4 else range(4, CHUNKS) if k == 4 else ():
                    sp.dma_start(x_res[:, i * W:(i + 1) * W].rearrange("p (t d) -> p t d", t=CHUNK),
                                 x_in[i * CHUNK:(i + 1) * CHUNK].rearrange("t p d -> p t d")
                                 ).then_inc(x_in_sem[i], 16)
                if k >= 4:
                    sp.wait_ge(att[0]["u_pe"], k - 3)
                sp.dma_start(ctx_ring(0, k).rearrange("p (t d) -> p t d", t=CHUNK),
                             ctx_in[k * CHUNK:(k + 1) * CHUNK].rearrange("t p d -> p t d")
                             ).then_inc(ctx_in_sem[k % 4], 16)
                if k == 2:
                    for tb, table in enumerate((b_up, a_up)):
                        for half in range(2):
                            sp.dma_start(raw_up[64 * half:64 * half + 64, tb * 2048:tb * 2048 + 2048],
                                         table).then_inc(up_raw_in, 16)
                if k == 3:
                    sp.dma_start(wu, w_up_router).then_inc(router_in, 16)
                    for half in range(2):
                        sp.dma_start(bup[64 * half:64 * half + 64, :], bias_up).then_inc(router_in, 16)
                    for g in range(4):
                        sp.dma_start(bdn[32 * g:32 * g + 32, :], bias_down).then_inc(router_in, 16)
            sp.wait_ge(g_pe, 32)
            for tb, table in enumerate((a_down, b_down)):
                for half in range(2):
                    sp.dma_start(raw_dn[64 * half:64 * half + 64, tb * 2048:tb * 2048 + 2048],
                                 table).then_inc(down_raw_in, 16)
            sp.wait_ge(s2_pe, TILES // 2)
            for half in range(2):
                sp.dma_start(wd_bd[64 * half:64 * half + 64, :].rearrange("p (j x e) -> p j x e", j=64, x=2)[:, :, half, :],
                             w_down_router).then_inc(wd_in, 16)
            sp.wait_ge(split_act, 2 * SPLIT)
            for k in range(CHUNKS):
                if k >= 4:
                    sp.wait_ge(att[1]["u_pe"], k - 3)
                sp.dma_start(ctx_ring(1, k).rearrange("p (t d) -> p t d", t=CHUNK),
                             ctx_in[k * CHUNK:(k + 1) * CHUNK].rearrange("t p d -> p t d")
                             ).then_inc(ctx_in_sem[k % 4], 16)
                if k == 3:
                    sp.wait_ge(d1_pe, TILES)
                    sp.dma_start(wi_s, wi_t).then_inc(lora_in, 16)
                    sp.dma_start(wo_s, wo_t).then_inc(lora_in, 16)
                    sp.dma_start(wga_s, wg_a).then_inc(lora_in, 16)
                    for i in range(6):
                        sp.dma_start(lb_raw[i * LR:(i + 1) * LR, :], lora_b).then_inc(lora_in, 16)
            for k in range(CHUNKS):
                sp.wait_ge(ff["y"], k + 1)
                sp.dma_start(out[k * CHUNK:(k + 1) * CHUNK].rearrange("t p d -> p t d"),
                             x_res[:, k * W:(k + 1) * W].rearrange("p (t d) -> p t d", t=CHUNK)
                             ).then_inc(stored, 16)
            sp.wait_ge(stored, 16 * CHUNKS)

        @block.gpsimd
        def _(pool):
            link = linker(pool, pool_step)

            chains = [0]

            def rstd_chain(k, lane, S_stats, ln_sem):
                m4 = mv[:, 8 * (chains[0] % 2):8 * (chains[0] % 2) + 8].rearrange("p (t c) -> p t c", c=2)
                chains[0] += 1
                pool.wait_ge(mv_ready, chains[0])
                if k >= 2:
                    pool.wait_ge(ln_sem, k - 1)
                at = CHUNK * (2 * lane + k % 2)
                y = rstd[:, at:at + CHUNK]
                link(pool.tensor_scalar(var, m4[:, :, 1], EPS, None, ALU.add))
                link(pool.tensor_scalar(y.bitcast(I32), var.bitcast(I32), -0.5, float(0x5F3759DF),
                                        ALU.mult, ALU.add))
                for i in range(NEWTON):
                    link(pool.tensor_tensor(half, y, y, ALU.mult))
                    link(pool.tensor_tensor(half, half, var, ALU.mult))
                    link(pool.tensor_scalar(half, half, -0.5, 1.5, ALU.mult, ALU.add))
                    link(pool.tensor_tensor(y, half, y, ALU.mult))
                link(pool.tensor_tensor(half, m4[:, :, 0], y, ALU.mult))
                pool.tensor_scalar(shift[:, at:at + CHUNK], half, -1.0, None, ALU.mult).then_inc(S_stats, 1)
                pool.wait_ge(S_stats, k + 1)

            def attention(L):
                S = att[L]
                rstd_chain(0, 0, S["stats"], S["ln"])
                rstd_chain(1, 0, S["stats"], S["ln"])
                pool.wait_ge(bias_ready, 2)
                for j in steps(3):
                    if here(j + 2):
                        rstd_chain(j + 2, 0, S["stats"], S["ln"])
                    k = j
                    if here(k):
                        pool.wait_ge(S["ln"], k + 1)
                        xk = x_res[:, k * W:(k + 1) * W].rearrange("p (t d) -> p t d", t=CHUNK)
                        pool.tensor_tensor(xk, xk, spread(bias_x[:, L * 128:(L + 1) * 128], 1, CHUNK),
                                           ALU.add).then_inc(S["xb"], 1)
                        pool.wait_ge(S["xb"], k + 1)
                    k = j - 3
                    if here(k) and L == 0:
                        rstd_chain(k, 1, m_stats, m_ln)
                    elif here(k) and k < 2:
                        rstd_chain(k, 1, ff["stats"], ff["ln"])
                    if L == 0 and j >= 3 and j < 7:
                        split_rest(pool, j - 3, raw_up, up_hm, up_lo, True)
                        pool.wait_ge(split_pool, j - 2)
                        if j == 3:
                            for tb in range(2):
                                link(pool.memset(up_lo[tb][64:128, :], 0.0))
                            link(pool.memset(region_r[:, :], 0.0))
                            pool.nop().then_inc(tables_up, 1)

            attention(0)
            wd_off = wd_bd.rearrange("p (j x e) -> p j x e", j=64, x=2)
            pool.wait_ge(s2_pe, TILES // 2)
            link(pool.memset(wd_off[0:64, :, 1, :], 0.0))
            pool.memset(wd_off[64:128, :, 0, :], 0.0).then_inc(wd_zero, 1)
            pool.wait_ge(wd_zero, 1)
            pool.wait_ge(xbd_ready, TILES)
            pool.wait_ge(s2_pe, TILES)
            for tb in range(2):
                link(pool.memset(dn_lo[tb][64:128, :], 0.0))
            v = a_bd.rearrange("p (m x i) -> p m x i", m=64, x=2)
            link(pool.memset(v[0:64, :, 1, :], 0.0))
            pool.memset(v[64:128, :, 0, :], 0.0).then_inc(abd_zero, 1)
            pool.wait_ge(abd_zero, 1)
            pool.memset(region_r[:, 0:2048], 0.0).then_inc(abd_zero, 1)
            for t in range(TILES):
                pool.wait_ge(y_rows, t + 1)
                xt = x_res[:, t * 128:(t + 1) * 128]
                pool.tensor_tensor(xt, xt, y_r(t), ALU.add).then_inc(x2, 1)

            attention(1)

            rest, low = l_rest, l_low
            hi, mid = (l_parts.rearrange("p (m six c) -> p m six c", m=2 * CHUNK, six=6)[:, :, i, :] for i in (0, 1))
            m16 = lambda ap: ap.rearrange("p (m c) -> p m c", c=LR)
            for j in steps(2):
                k = j - 1
                if here(k):
                    pool.wait_ge(ff["hi"], k + 1)
                    if k >= 1:
                        pool.wait_ge(ff["parts"], k)
                    pool.tensor_tensor(m16(rest), m16(low), hi, ALU.subtract).then_inc(ff["rest"], 1)
                    pool.wait_ge(ff["mid"], k + 1)
                    pool.tensor_tensor(m16(rest), m16(rest), mid, ALU.subtract).then_inc(ff["rest"], 1)
                    pool.wait_ge(ff["rest"], 2 * k + 2)
                k = j - 2
                if here(k):
                    for fc in range(FC):
                        part = slice(fc * W, (fc + 1) * W)
                        pool.wait_ge(ff["h2"], FC * k + fc + 1)
                        pool.wait_ge(ff["h1"], FC * k + fc + 1)
                        if k >= 2 and fc == 0:
                            pool.wait_ge(ff["o_pe"], k - 1)
                        pool.tensor_tensor(h_s(k)[:, part], h1_s[:, part], h2_s[:, part], ALU.add).then_inc(ff["h"], 1)
                if here(j + 2):
                    rstd_chain(j + 2, 1, ff["stats"], ff["ln"])

        @block.scalar
        def _(act):
            def copy(dst, src):
                return act.activation(dst, src, ACT.Copy)

            act.wait_ge(small_in, 48)
            act.activation(tgate[:, :], gate[:, 0:4], ACT.Tanh).then_inc(gates_ready, 1)

            def normalise(dst, k, lane, stats_sem, done_sem):
                act.wait_ge(stats_sem, k + 1)
                for i in range(CHUNK):
                    j = CHUNK * (2 * lane + k % 2) + i
                    ins = act.activation(dst[:, i * D:(i + 1) * D], x_res[:, k * W + i * D:k * W + (i + 1) * D],
                                         ACT.Identity, bias=shift[:, j:j + 1], scale=rstd[:, j:j + 1])
                ins.then_inc(done_sem, 1)

            def attention(L):
                S = att[L]
                normalise(ln_s(0), 0, 0, S["stats"], S["ln"])
                for j in steps(5 if L == 0 else 3):
                    k = j - 5
                    if L == 0 and here(k):
                        act.wait_ge(m_lnT_pe, k + 1)
                        copy(lnT_all[:, k * W:(k + 1) * W], banks[:, 0, :]).then_inc(m_lnT, 1)
                    k = j - 3
                    if here(k):
                        act.wait_ge(S["pt_pe"], k + 1)
                        if k >= 2:
                            act.wait_ge(S["u_pe"], k - 1)
                        copy(pT_s(k), banks[:, 5, :]).then_inc(S["pt"], 1)
                    k = j
                    if here(k):
                        act.wait_ge(S["ctxT_pe"], k + 1)
                        if k >= 2:
                            act.wait_ge(S["k_pe"], k - 1)
                        copy(ctxT_s(k), banks[:, 0, :]).then_inc(S["ctxT"], 1)
                    k = j - 2
                    if here(k):
                        act.wait_ge(S["sm"], k + 1)
                        if k >= 2:
                            act.wait_ge(S["pt_pe"], k - 1)
                            act.wait_ge(S["x"], k - 1)
                        for i in range(CHUNK):
                            j2 = (k % 2) * CHUNK + i
                            ins = act.activation(prob_s(k)[:, i * D:(i + 1) * D], sm_s(k)[:, i * D:(i + 1) * D],
                                                 ACT.Exp, bias=negm[:, j2:j2 + 1], scale=SCALE,
                                                 accum_out=rsum[:, j2:j2 + 1])
                        ins.then_inc(S["prob"], 1)
                    k = j - 1
                    if here(k):
                        act.wait_ge(S["k_pe"], k + 1)
                        if k >= 2:
                            act.wait_ge(S["s_pe"], k - 1)
                        act.activation(kT_s(k), banks[:, 2, :], ACT.Identity, bias=bk[L]).then_inc(S["k"], 1)
                    k = j + 1
                    if here(k):
                        if k >= 2:
                            act.wait_ge(S["lnT_pe"], k - 1)
                        normalise(ln_s(k), k, 0, S["stats"], S["ln"])
                    k = j - 4
                    if L == 0 and here(k):
                        if k >= 2:
                            act.wait_ge(m_lnT_pe, k - 1)
                            act.wait_ge(m_xt, k - 1)
                        normalise(mln_s(k), k, 1, m_stats, m_ln)
                    if L == 0 and 2 <= j < 2 + SPLIT:
                        if j == 2:
                            act.wait_ge(up_raw_in, 64)
                        split_cast(act, j - 2, raw_up, up_hm, up_lo, True)

            attention(0)

            act.wait_ge(ru["log_pe"], 1)
            copy(logT_up.rearrange("p (q t n) -> p t q n", q=4, n=4),
                 banks[0:64, 2, :].rearrange("p (t q n) -> p t q n", q=4, n=4)).then_inc(ru["log"], 1)
            act.wait_ge(ru["gap"], 1)
            act.activation(egap[:, :], gap[:, :], ACT.Exp).then_inc(ru["egap"], 1)
            act.wait_ge(ru["oh_pe"], 1)
            copy(oh_up_T[:, 0:512].rearrange("p (s P x) -> p s x P", s=2, x=2),
                 banks[:, 4, :].rearrange("p (s x P) -> p s x P", s=2, x=2)).then_inc(ru["ohT_a"], 1)
            for u in range(0, 32, 2):
                act.wait_ge(g_pe, u + 1)
                dst = (g_b if u < 16 else g_a)[:, :].rearrange("p (m c) -> p c m", c=64)
                copy(dst[:, 4 * (u % 16):4 * (u % 16) + 4, :],
                     banks[:, 2 * (u % 4):2 * (u % 4) + 2, :].rearrange("p b (c m) -> p (b c) m", c=2)
                     ).then_inc(g_act, 1)
            act.wait_ge(m_xt, CHUNKS)
            act.wait_ge(tables_up, 1)
            for j in range(TILES + 2):
                t = j
                if t < TILES:
                    if t >= 2:
                        act.wait_ge(s1_pe, t - 1)
                    dst = x_bd(t).rearrange("p (n x g i) -> p n x g i", n=4, x=2, g=4)
                    src = xT[:, t * 128:(t + 1) * 128].rearrange("p (n i) -> p n i", n=4)
                    for g in range(4):
                        for x in range(2):
                            q = (g // 2) * 2 + x
                            ins = copy(dst[32 * g:32 * g + 32, :, x, g, :], src[32 * q:32 * q + 32, :, :])
                    ins.then_inc(xbd_ready, 1)
                t = j - 2
                if t >= 0:
                    act.wait_ge(hb_ready, t + 1)
                    ht = h_all[:, t * 512:(t + 1) * 512]
                    act.activation(ht, ht, ACT.Gelu).then_inc(h_ready, 1)
            act.wait_ge(down_raw_in, 64)
            act.wait_ge(xbd_ready, TILES)
            for n in range(SPLIT):
                split_cast(act, n, raw_dn, dn_hm, dn_lo, False)
            act.wait_ge(rd["log_pe"], 1)
            copy(logT_dn, banks[:, 6, 0:256]).then_inc(rd["log"], 1)
            act.wait_ge(rd["gap"], 1)
            act.activation(egap[:, :], gap[:, :], ACT.Exp).then_inc(rd["egap"], 1)
            act.wait_ge(rd["oh_pe"], 1)
            for x in range(2):
                ins = copy(oh_a_T.rearrange("p (x s P k) -> p x k s P", x=2, s=2, k=2)[:, x],
                           banks[:, x, :].rearrange("p (k s P) -> p k s P", k=2, s=2))
            ins.then_inc(rd["ohT_a"], 1)
            act.wait_ge(abd_zero, 1)
            for k in range(4):
                for v in range(8):
                    act.wait_ge(da_pe, 8 * k + v + 1)
                    dst = a_bd.rearrange("p (m x s o) -> p o s m x", m=64, x=2, s=2)
                    src = banks[:, v % 4, :].rearrange("p (o s m) -> p o s m", o=4, s=2)
                    copy(dst[0:64, 4 * v:4 * v + 4, :, :, 0], src[0:64]).then_inc(da_act, 1)
                for v in range(0, 8, 2):
                    act.wait_ge(db_pe, 8 * k + v + 1)
                    dst = b_nat.rearrange("p (m s o) -> p o s m", m=64, s=2)
                    src = banks[:, v % 4, :].rearrange("p (o s m) -> p o s m", o=4, s=2)
                    copy(dst[:, 4 * v:4 * v + 4, :, :], src).then_inc(db_act, 1)

            attention(1)

            normalise(f_ln(0), 0, 1, ff["stats"], ff["ln"])
            for j in steps(2):
                k = j
                if here(k):
                    act.wait_ge(ff["lnT_pe"], k + 1)
                    if k >= 3:
                        act.wait_ge(ff["z2_pe"], FC * (k - 2))
                    copy(f_lnT(k), banks[:, 0, :]).then_inc(ff["lnT"], 1)
                k = j - 1
                if here(k):
                    act.wait_ge(ff["exp_in"], k + 1)
                    act.activation(r_exp, r_sh, ACT.Exp).then_inc(ff["exp"], 1)
                    low = l_low.rearrange("p (m c) -> p m c", c=LR)
                    rest = l_rest.rearrange("p (m c) -> p m c", c=LR)
                    parts = l_parts.rearrange("p (m six c) -> p m six c", m=2 * CHUNK, six=6)
                    act.wait_ge(ff["low"], k + 1)
                    if k >= 1:
                        act.wait_ge(ff["lora_pe"], k)
                    copy(parts[:, :, 0, :], low).then_inc(ff["hi"], 1)
                    copy(parts[:, :, 2, :], low)
                    copy(parts[:, :, 4, :], low)
                    act.wait_ge(ff["rest"], 2 * k + 1)
                    copy(parts[:, :, 1, :], rest)
                    copy(parts[:, :, 3, :], rest).then_inc(ff["mid"], 1)
                    act.wait_ge(ff["rest"], 2 * k + 2)
                    copy(parts[:, :, 5, :], rest).then_inc(ff["parts"], 1)
                k = j - 2
                if here(k):
                    for fc in range(FC):
                        act.wait_ge(ff["z1_pe"], FC * k + fc + 1)
                        if k >= 1 and fc == 0:
                            act.wait_ge(ff["h"], FC * k)
                        act.activation(h1_s[:, fc * W:(fc + 1) * W], banks[:, 2 + (FC * k + fc) % 3, :],
                                       ACT.Relu).then_inc(ff["h1"], 1)
                k = j + 1
                if here(k):
                    if k >= 2:
                        act.wait_ge(ff["lnT_pe"], k - 1)
                    normalise(f_ln(k), k, 1, ff["stats"], ff["ln"])
                k = j - 1
                if here(k):
                    act.wait_ge(ff["lora_pe"], k + 1)
                    if k >= 2:
                        act.wait_ge(ff["z2_pe"], FC * (k - 1))
                    copy(lora_T(k), banks[0:96, 1, :].bitcast(BF16)).then_inc(ff["lora"], 1)
                    act.wait_ge(ff["ratio_pe"], k + 1)
                    if k >= 1:
                        act.wait_ge(ff["h2"], FC * k)
                    copy(ratio_T, banks[:, 6, :]).then_inc(ff["ratio"], 1)

        @block.vector
        def _(dve):
            link = linker(dve, dve_step)

            handed = [0]
            stats_of = []

            def statistics(k, done):
                n = handed[0]
                handed[0] += 1
                stats_of.append((done, k + 1))
                for i in range(CHUNK):
                    ins = dve.bn_stats(stat[:, 6 * i:6 * i + 6], x_res[:, k * W + i * D:k * W + (i + 1) * D])
                link(ins)
                if n >= 2:
                    dve.wait_ge(*stats_of[n - 2])
                for i in range(CHUNK):
                    at = 8 * (n % 2) + 2 * i
                    ins = dve.bn_aggr(mv[:, at:at + 2], stat[:, 6 * i:6 * i + 6])
                ins.then_inc(mv_ready, 1)
                dve.wait_ge(mv_ready, n + 1)

            def attention(L):
                S = att[L]

                def stats(k):
                    if L == 0:
                        dve.wait_ge(x_in_sem[k], 16)
                    else:
                        dve.wait_ge(x2, CHUNK * (k + 1))
                    statistics(k, S["stats"])

                stats(0)
                stats(1)
                for j in steps(5 if L == 0 else 3):
                    k = j - 5
                    if L == 0 and here(k):
                        dve.wait_ge(m_ln, k + 1)
                        for i in range(CHUNK):
                            t = k * CHUNK + i
                            ins = dve.transpose(
                                xT[:, t * 128:(t + 1) * 128].rearrange("p (n b r) -> p b n r", n=4, b=4),
                                mln_s(k)[:, i * 128:(i + 1) * 128])
                        ins.then_inc(m_xt, 1)
                    k = j - 2
                    if here(k):
                        dve.wait_ge(S["s_pe"], k + 1)
                        if k >= 2:
                            dve.wait_ge(S["prob"], k - 1)
                        dve.tensor_tensor(sm_s(k).rearrange("p (t m) -> p t m", t=CHUNK),
                                          banks[:, 4, :].rearrange("p (t m) -> p t m", t=CHUNK),
                                          spread(masks[L], 1, CHUNK), ALU.add).then_inc(S["s_ev"], 1)
                        dve.wait_ge(S["s_ev"], k + 1)
                        if k >= 1:
                            dve.wait_ge(S["sm"], k)
                        link(dve.tensor_reduce(mx[:, :], sm_s(k).rearrange("p (t m) -> p t m", t=CHUNK),
                                               AX_X, ALU.max))
                        dve.tensor_scalar(negm[:, CHUNK * (k % 2):CHUNK * (k % 2 + 1)], mx[:, :], -SCALE, None,
                                          ALU.mult).then_inc(S["sm"], 1)
                    k = j
                    if here(k):
                        dve.wait_ge(S["lnT_pe"], k + 1)
                        if k >= 2:
                            dve.wait_ge(S["q_pe"], k - 1)
                        dve.tensor_copy(lnT_s(k), banks[:, 1, :]).then_inc(S["lnT"], 1)
                    k = j - 3
                    if here(k):
                        dve.wait_ge(S["u_pe"], k + 1)
                        if k >= 2:
                            dve.wait_ge(S["o_pe"], k - 1)
                        dve.tensor_copy(uT_s(k), banks[:, 6, :]).then_inc(S["u"], 1)
                    k = j - 1
                    if here(k):
                        dve.wait_ge(S["q_pe"], k + 1)
                        if k >= 2:
                            dve.wait_ge(S["s_pe"], k - 1)
                        dve.tensor_scalar(qT_s(k), banks[:, 3, :], bq[L], None, ALU.add).then_inc(S["q"], 1)
                    if here(j + 2):
                        stats(j + 2)
                    if L == 0 and j == 0:
                        dve.wait_ge(gates_ready, 1)
                        dve.wait_ge(vff_pe, 1)
                        link(dve.tensor_tensor(bias_x[:, 0:128], banks[:, 7, 128:256], row_c[:, 0:128], ALU.add))
                        dve.tensor_scalar(w_vff[:, :], banks[:, 7, 0:128], tgate[:, 0:1], None, ALU.mult)
                        dve.tensor_scalar(wout[1], wout[1], tgate[:, 1:2], None, ALU.mult).then_inc(vff_ready, 1)
                        dve.tensor_scalar(bias_x[:, 0:128], bias_x[:, 0:128], tgate[:, 0:1], None,
                                          ALU.mult).then_inc(bias_ready, 1)
                        dve.tensor_scalar(bias_x[:, 128:256], row_c[:, 128:256], tgate[:, 1:2], None,
                                          ALU.mult).then_inc(bias_ready, 1)
                    k = j - 3
                    if here(k):
                        dve.wait_ge(S["prob"], k + 1)
                        if k >= 1:
                            dve.wait_ge(S["x"], k)
                        link(dve.reciprocal(rinv[:, :], rsum[:, CHUNK * (k % 2):CHUNK * (k % 2 + 1)]))
                        dve.wait_ge(S["o_pe"], k + 1)
                        dve.wait_ge(S["xb"], k + 1)
                        for i in range(CHUNK):
                            xt = x_res[:, k * W + i * D:k * W + (i + 1) * D]
                            ins = dve.scalar_tensor_tensor(xt, banks[:, 7, i * D:(i + 1) * D], rinv[:, i:i + 1],
                                                           xt, ALU.mult, ALU.add)
                        ins.then_inc(S["x"], 1)
                        if L == 0:
                            dve.wait_ge(S["x"], k + 1)
                            statistics(k, m_stats)
                        elif k < 2:
                            dve.wait_ge(S["x"], k + 1)
                            statistics(k, ff["stats"])

            dve.wait_ge(small_in, 48)
            dve.tensor_copy(vff_tmp[:, 0:128], spread(bv0[:, 0], 1, 128)).then_inc(bv_ready, 1)
            dve.wait_ge(consts_in, 16)
            dve.tensor_copy(ident_b[:, :], ident).then_inc(ident_b_ready, 1)
            attention(0)

            def route(S, lg, log_bank, oh, copies):
                dve.wait_ge(S["lgT_pe"], 1)
                link(dve.tensor_copy(lg, banks[:, log_bank, 0:256]))
                for q in range(4):
                    ins = dve.max(v8[:, 8 * q:8 * q + 8], lg[:, 64 * q:64 * q + 64])
                link(ins)
                for q in range(4):
                    ins = dve.max_index(ix8[:, 8 * q:8 * q + 8], v8[:, 8 * q:8 * q + 8], lg[:, 64 * q:64 * q + 64])
                v = v8[:, :].rearrange("p (q k) -> p q k", k=8)
                dve.tensor_tensor(gap[:, :], v[:, :, 1], v[:, :, 0], ALU.subtract).then_inc(S["gap"], 1)
                dve.wait_ge(S["gap"], 1)
                link(dve.tensor_copy(idx[:, :].rearrange("p (q s) -> p q s", s=2),
                                     ix8[:, :].rearrange("p (q k) -> p q k", k=8)[:, :, 0:2]))
                for i in range(copies):
                    ins = dve.tensor_tensor(oh.rearrange("p (m i e) -> p m i e", i=copies, e=64)[:, :, i, :],
                                            spread(iota, 1, 8), spread(idx[:, :], 2, 64), ALU.is_equal)
                ins.then_inc(S["oh"], 1)
                dve.wait_ge(S["egap"], 1)
                link(dve.tensor_scalar(den[:, :], egap[:, :], 1.0, None, ALU.add))
                p2 = pr[:, :].rearrange("p (q s) -> p q s", s=2)
                link(dve.reciprocal(p2[:, :, 0], den[:, :]))
                link(dve.tensor_tensor(p2[:, :, 1], p2[:, :, 0], egap[:, :], ALU.mult))

            route(ru, lg_up, 3, oh_up, 2)
            prq = pr[:, :].rearrange("p (k x s) -> p k x s", k=2, x=2)
            for x in range(2):
                ins = dve.tensor_copy(prb_up[:, x * 128:(x + 1) * 128].rearrange("p (k s i) -> p k s i", k=2, s=2),
                                      spread(prq[:, :, x, :], 3, 32))
            ins.then_inc(ru["prb"], 1)
            dve.wait_ge(ru["oh_pe"], 1)
            dve.tensor_copy(oh_up_T[:, 512:1024].rearrange("p (s P x) -> p s x P", s=2, x=2),
                            banks[:, 5, :].rearrange("p (s x P) -> p s x P", s=2, x=2)).then_inc(ru["ohT_d"], 1)
            dve.wait_ge(ru["pb_pe"], 1)
            dve.tensor_copy(prob[:, 0:256].rearrange("p (P x) -> p x P", x=2),
                            banks[:, 6, 0:256].rearrange("p (x P) -> p x P", x=2)).then_inc(ru["pb"], 1)
            for u in range(1, 32, 2):
                dve.wait_ge(g_pe, u + 1)
                dst = (g_b if u < 16 else g_a)[:, :].rearrange("p (m c) -> p c m", c=64)
                dve.tensor_copy(dst[:, 4 * (u % 16):4 * (u % 16) + 4, :],
                                banks[:, 2 * (u % 4):2 * (u % 4) + 2, :].rearrange("p b (c m) -> p (b c) m", c=2)
                                ).then_inc(g_dve, 1)

            dve.wait_ge(ru["pb"], 1)
            dve.wait_ge(router_in, 16 * 7)
            for j in range(TILES + 1):
                t = j
                if t < TILES:
                    dve.wait_ge(s1_pe, t + 1)
                    if t >= 2:
                        dve.wait_ge(s2_pe, t - 1)
                    for k in range(2):
                        part = slice(64 * k, 64 * k + 64)
                        ins = dve.tensor_tensor(
                            t_bd(t).rearrange("p (m k c) -> p m k c", m=8, k=2)[part, :, k, :],
                            banks[part, t % 3, :].rearrange("p (m c) -> p m c", m=8),
                            spread(prob[part, t * 8:(t + 1) * 8], 2, 64), ALU.mult)
                    ins.then_inc(tbd_ready, 1)
                t = j - 1
                if t >= 0:
                    dve.wait_ge(s2_pe, t + 1)
                    dve.scalar_tensor_tensor(
                        h_all[:, t * 512:(t + 1) * 512].rearrange("p (m c) -> p m c", c=64),
                        banks[:, 3 + t % 3, :].rearrange("p (m c) -> p m c", c=64), gate[:, 4:5],
                        spread(bup[:, :], 1, 8), ALU.mult, ALU.add).then_inc(hb_ready, 1)

            for n in range(4):
                split_rest(dve, n, raw_dn, dn_hm, dn_lo, False)

            route(rd, lg_dn, 7, oh_dn, 2)
            dve.tensor_copy(prb_dn.rearrange("p (m c) -> p m c", c=64), spread(pr[:, :], 2, 64)).then_inc(rd["prb"], 1)
            dve.wait_ge(rd["oh_pe"], 2)
            for c in range(2):
                ins = dve.tensor_copy(oh_b_T.rearrange("p (c s m q) -> p c q s m", c=2, s=2, q=4)[:, c],
                                      banks[:, 2 + c, :].rearrange("p (q s m) -> p q s m", q=4, s=2))
            ins.then_inc(rd["ohT_d"], 1)
            dve.wait_ge(rd["pb_pe"], 1)
            dve.tensor_copy(prob[:, :].rearrange("p (m g) -> p g m", g=8),
                            banks[:, 4, :].rearrange("p (g m) -> p g m", g=8)).then_inc(rd["pb"], 1)
            dve.tensor_tensor(down_scale[:, :], gate[:, 5:6], tgate[:, 2:3], ALU.mult)
            link(dve.tensor_scalar(bdn[:, :], bdn[:, :], tgate[:, 2:3], None, ALU.mult))
            dve.wait_ge(abd_zero, 2)
            dve.wait_ge(rd["pb"], 1)
            for k in range(4):
                for v in range(8):
                    dve.wait_ge(da_pe, 8 * k + v + 1)
                    dst = a_bd.rearrange("p (m x s o) -> p o s m x", m=64, x=2, s=2)
                    src = banks[:, v % 4, :].rearrange("p (o s m) -> p o s m", o=4, s=2)
                    dve.tensor_copy(dst[64:128, 4 * v:4 * v + 4, :, :, 1], src[64:128]).then_inc(da_dve, 1)
                for v in range(1, 8, 2):
                    dve.wait_ge(db_pe, 8 * k + v + 1)
                    dst = b_nat.rearrange("p (m s o) -> p o s m", m=64, s=2)
                    src = banks[:, v % 4, :].rearrange("p (o s m) -> p o s m", o=4, s=2)
                    dve.tensor_copy(dst[:, 4 * v:4 * v + 4, :, :], src).then_inc(db_dve, 1)
                for j in range(9):
                    t = 8 * k + j
                    if j < 8:
                        dve.wait_ge(d1_pe, t + 1)
                        if t >= 2:
                            dve.wait_ge(d2_pe, t - 1)
                        for c in range(2):
                            part = slice(64 * c, 64 * c + 64)
                            ins = dve.tensor_tensor(
                                u_bd(t).rearrange("p (m c o) -> p m c o", m=16, c=2)[part, :, c, :],
                                banks[part, 4 + t % 2, :].rearrange("p (m o) -> p m o", m=16),
                                spread(prob[part, t * 16:(t + 1) * 16], 2, 32), ALU.mult)
                        ins.then_inc(ubd_ready, 1)
                    t = 8 * k + j - 1
                    if j >= 1:
                        dve.wait_ge(d2_pe, t + 1)
                        if t >= 2:
                            dve.wait_ge(y_rows, t - 1)
                        bias = spread(bdn[:, :].rearrange("p (r b) -> p r b", b=4), 1, 4)
                        dve.scalar_tensor_tensor(
                            y_t(t).rearrange("p (b n r) -> p n r b", b=4, n=4),
                            banks[:, 6 + t % 2, 0:128].rearrange("p (n r b) -> p n r b", n=4, b=4), down_scale[:, :],
                            bias, ALU.mult, ALU.add).then_inc(y_ev, 1)
                        dve.wait_ge(y_ev, t + 1)
                        if t >= 2:
                            dve.wait_ge(x2, t - 1)
                        dve.transpose(y_r(t), y_t(t)).then_inc(y_rows, 1)

            attention(1)

            dve.wait_ge(lora_in, 16 * 9)
            link(dve.tensor_copy(lb_hi, lb_raw))
            link(dve.tensor_tensor(lb_raw, lb_raw, lb_hi, ALU.subtract))
            link(dve.tensor_copy(lb_mid, lb_raw))
            link(dve.tensor_tensor(lb_raw, lb_raw, lb_mid, ALU.subtract))
            link(dve.tensor_scalar(lb_part, lb_raw, sel[:, 2:3], None, ALU.mult))
            link(dve.scalar_tensor_tensor(lb_part, lb_mid, sel[:, 1:2], lb_part, ALU.mult, ALU.add))
            dve.scalar_tensor_tensor(lb_part, lb_hi, sel[:, 0:1], lb_part, ALU.mult, ALU.add).then_inc(ff["lb"], 1)

            def f_stats(k):
                dve.wait_ge(att[1]["x"], k + 1)
                statistics(k, ff["stats"])

            for j in steps(3):
                k = j - 1
                if here(k):
                    dve.wait_ge(ff["proj_pe"], k + 1)
                    pk = proj(k).rearrange("p (t c) -> p t c", c=PROJ)
                    pp = banks[:, 7, 0:CHUNK * PROJ].rearrange("p (t c) -> p t c", c=PROJ)
                    dve.tensor_tensor(pk[:, :, 0:LORA_E], pp[:, :, 0:LORA_E],
                                      spread(row_c[:, 256:260], 1, CHUNK), ALU.add)
                    dve.tensor_copy(pk[:, :, LORA_E:PROJ], pp[:, :, LORA_E:PROJ]).then_inc(ff["proj"], 1)
                    dve.wait_ge(ff["proj"], k + 1)
                    lg = pk[:, :, 0:LORA_E]
                    low = pk[:, :, LORA_E:PROJ].rearrange("p t (e r) -> p t e r", e=LORA_E)
                    e3 = lambda ap: ap.rearrange("p (t e) -> p t e", e=LORA_E)
                    pair = lambda ap: ap.rearrange("p (t e f) -> p t e f", e=LORA_E, f=LORA_E)
                    link(dve.tensor_reduce(r_max, lg, AX_X, ALU.max))
                    dve.tensor_tensor(e3(r_sh), lg, spread(r_max, 2, LORA_E), ALU.subtract).then_inc(ff["exp_in"], 1)
                    other, own = spread(lg, 2, LORA_E), spread(lg, 3, LORA_E)
                    dve.tensor_tensor(pair(r_gt), other, own, ALU.is_gt)
                    link(dve.tensor_tensor(pair(r_eq), other, own, ALU.is_equal))
                    link(dve.tensor_tensor(pair(r_eq), pair(r_eq),
                                           spread(tri.rearrange("p (e f) -> p e f", f=LORA_E), 1, CHUNK), ALU.mult))
                    link(dve.tensor_tensor(r_gt, r_gt, r_eq, ALU.add))
                    link(dve.tensor_reduce(e3(r_rank), pair(r_gt), AX_X, ALU.add))
                    mask = r_mask.rearrange("p (t s e) -> p t s e", s=2, e=LORA_E)
                    link(dve.tensor_tensor(mask, spread(e3(r_rank), 2, 2),
                                           spread(spread(slot_id, 1, CHUNK), 3, LORA_E), ALU.is_equal))
                    if k >= 1:
                        dve.wait_ge(ff["parts"], k)
                    lo4 = l_low.rearrange("p (v t e r) -> p v t e r", v=2, t=CHUNK, e=LORA_E)
                    for s in range(2):
                        ins = dve.tensor_tensor(lo4[:, s], low, spread(mask[:, :, s, :], 3, LORA_R), ALU.mult)
                    link(ins)
                    dve.tensor_tensor(l_low[:, 64:128], l_low[:, 64:128], l_low[:, 0:64],
                                      ALU.subtract).then_inc(ff["low"], 1)
                    dve.wait_ge(ff["exp"], k + 1)
                    link(dve.tensor_tensor(e3(r_pick), mask[:, :, 1, :], e3(r_exp), ALU.mult))
                    if k >= 1:
                        dve.wait_ge(ff["ratio_pe"], k)
                    dve.tensor_reduce(r_ratio, e3(r_pick), AX_X, ALU.add).then_inc(ff["ratio_w"], 1)
                    link(dve.tensor_reduce(r_sum, e3(r_exp), AX_X, ALU.add))
                    link(dve.reciprocal(r_inv, r_sum))
                    link(dve.tensor_scalar(r_w0(k), r_inv, tgate[:, 3:4], None, ALU.mult))
                k = j - 3
                if here(k):
                    dve.wait_ge(ff["o_pe"], k + 1)
                    for i in range(CHUNK):
                        xt = x_res[:, k * W + i * D:k * W + (i + 1) * D]
                        ins = dve.scalar_tensor_tensor(xt, banks[:, 5, i * D:(i + 1) * D], r_w0(k)[:, i:i + 1], xt,
                                                       ALU.mult, ALU.add)
                    ins.then_inc(ff["y"], 1)
                k = j - 2
                if here(k):
                    dve.wait_ge(ff["ratio"], k + 1)
                    for fc in range(FC):
                        dve.wait_ge(ff["z2_pe"], FC * k + fc + 1)
                        if k >= 1 and fc == 0:
                            dve.wait_ge(ff["h"], FC * k)
                        dve.scalar_tensor_tensor(h2_s[:, fc * W:(fc + 1) * W], banks[:, 2 + (FC * k + fc) % 3, :],
                                                 0.0, ratio_T, ALU.max, ALU.mult).then_inc(ff["h2"], 1)
                if here(j + 2):
                    f_stats(j + 2)

        @block.tensor
        def _(pe):
            def tiles4(fn):
                for i in range(CHUNK):
                    ins = fn(slice(i * D, (i + 1) * D))
                return ins

            def transpose4(bank, src):
                return tiles4(lambda c: pe.transpose(banks[:, bank, c], src[:, c], ident))

            def attention(L):
                S = att[L]
                for j in steps(4 if L == 0 else 3):
                    k = j - 2
                    if here(k):
                        pe.wait_ge(S["k"], k + 1)
                        pe.wait_ge(S["q"], k + 1)
                        if k >= 1:
                            pe.wait_ge(S["s_ev"], k)
                        tiles4(lambda c: pe.matmul(banks[:, 4, c], qT_s(k)[:, c], kT_s(k)[:, c],
                                                   start=True, stop=True)).then_inc(S["s_pe"], 1)
                    k = j - 3
                    if here(k):
                        pe.wait_ge(S["prob"], k + 1)
                        if k >= 1:
                            pe.wait_ge(S["pt"], k)
                        transpose4(5, prob_s(k)).then_inc(S["pt_pe"], 1)
                    k = j
                    if here(k):
                        pe.wait_ge(ctx_in_sem[k % 4], 16 * (2 * L + k // 4 + 1))
                        if k == 0:
                            pe.wait_ge(consts_in, 16)
                        if k >= 1:
                            pe.wait_ge(S["ctxT"], k)
                        if L == 0 and here(k - 5):
                            pe.wait_ge(m_lnT, k - 4)
                        transpose4(0, ctx_ring(L, k)).then_inc(S["ctxT_pe"], 1)
                        pe.wait_ge(S["ln"], k + 1)
                        if k >= 1:
                            pe.wait_ge(S["lnT"], k)
                        transpose4(1, ln_s(k)).then_inc(S["lnT_pe"], 1)
                    if L == 0 and j == 0:
                        pe.wait_ge(weights_in, 16)
                        pe.wait_ge(bv_ready, 1)
                        pe.matmul(banks[:, 7, 0:128], wv0, wff_t, start=True, stop=True)
                        pe.matmul(banks[:, 7, 128:256], vff_tmp[:, 0:128], wff_t, start=True,
                                  stop=True).then_inc(vff_pe, 1)
                    k = j - 3
                    if here(k):
                        pe.wait_ge(S["pt"], k + 1)
                        if k >= 1:
                            pe.wait_ge(S["u"], k)
                        tiles4(lambda c: pe.matmul(banks[:, 6, c], ctx_ring(L, k)[:, c], pT_s(k)[:, c],
                                                   start=True, stop=True)).then_inc(S["u_pe"], 1)
                    k = j - 1
                    if here(k):
                        pe.wait_ge(S["ctxT"], k + 1)
                        if k >= 1:
                            pe.wait_ge(S["k"], k)
                        pe.matmul(banks[:, 2, :], wk[L], ctxT_s(k), start=True, stop=True).then_inc(S["k_pe"], 1)
                        pe.wait_ge(S["lnT"], k + 1)
                        if k >= 1:
                            pe.wait_ge(S["q"], k)
                        pe.matmul(banks[:, 3, :], wq[L], lnT_s(k), start=True, stop=True).then_inc(S["q_pe"], 1)
                    k = j - 3
                    if here(k):
                        pe.wait_ge(S["u"], k + 1)
                        if L == 0 and k == 0:
                            pe.wait_ge(vff_ready, 1)
                            pe.wait_ge(bias_ready, 2)
                        if k >= 1:
                            pe.wait_ge(S["x"], k)
                        tiles4(lambda c: pe.matmul(banks[:, 7, c], uT_s(k)[:, c], wout[L],
                                                   start=True, stop=True)).then_inc(S["o_pe"], 1)
                    k = j - 4
                    if L == 0 and here(k):
                        pe.wait_ge(m_ln, k + 1)
                        pe.wait_ge(S["ctxT"], min(j + 1, CHUNKS))
                        if k >= 1:
                            pe.wait_ge(m_lnT, k)
                        transpose4(0, mln_s(k)).then_inc(m_lnT_pe, 1)

            attention(0)

            pe.wait_ge(m_lnT, CHUNKS)
            pe.wait_ge(router_in, 16 * 7)
            tok = lnT_all.rearrange("p (n r) -> p n r", r=8)
            for r in range(8):
                ins = pe.matmul(banks[0:64, 2, :], wu[:, r * 64:(r + 1) * 64], tok[:, :, r],
                                start=(r == 0), stop=(r == 7))
            ins.then_inc(ru["log_pe"], 1)
            pe.wait_ge(ru["log"], 1)
            for q in range(4):
                ins = pe.transpose(banks[:, 3, q * 64:(q + 1) * 64], logT_up[:, q * 128:(q + 1) * 128], ident[0:64, 0:64])
            ins.then_inc(ru["lgT_pe"], 1)
            pe.wait_ge(ru["oh"], 1)
            pe.wait_ge(ident_b_ready, 1)
            oh = oh_up.rearrange("p (k x s e) -> p k x s e", k=2, x=2, s=2)
            for k in range(2):
                for s in range(2):
                    for x in range(2):
                        c = (s * 2 + x) * 128
                        ins = pe.matmul(banks[:, 4 + k, c:c + 128], oh[:, k, x, s, :],
                                        ident_b[:, :], start=True, stop=True)
            ins.then_inc(ru["oh_pe"], 1)
            pe.wait_ge(ru["prb"], 1)
            for x in range(2):
                ins = pe.matmul(banks[:, 6, x * 128:(x + 1) * 128], prb_up[:, x * 128:(x + 1) * 128], ident,
                                start=True, stop=True)
            ins.then_inc(ru["pb_pe"], 1)
            pe.wait_ge(ru["ohT_a"], 1)
            pe.wait_ge(ru["ohT_d"], 1)
            pe.wait_ge(ru["pb"], 1)
            pe.wait_ge(tables_up, 1)
            for u in range(32):
                if u >= 4:
                    pe.wait_ge(g_act if u % 2 == 0 else g_dve, (u - 4) // 2 + 1)
                tb = u // 16
                for ci in range(4):
                    col = 4 * (u % 16) + ci
                    for g in range(4):
                        o = banks[32 * g:32 * g + 32, 2 * (u % 4) + ci // 2, (ci % 2) * 256:(ci % 2) * 256 + 256]
                        rhs = oh_up_T[:, g * 256:(g + 1) * 256]
                        pe.matmul(o, up_hm[tb][:, col * 32:(col + 1) * 32], rhs, start=True, stop=False)
                        ins = pe.matmul(o, up_lo[tb][:, col * 32:(col + 1) * 32], rhs, start=False, stop=True)
                ins.then_inc(g_pe, 1)
            pe.wait_ge(g_act, 16)
            pe.wait_ge(g_dve, 16)
            for j in range(TILES + 1):
                t = j
                if t < TILES:
                    pe.wait_ge(xbd_ready, t + 1)
                    if t >= 3:
                        pe.wait_ge(tbd_ready, t - 2)
                    for k in range(2):
                        for m in range(8):
                            ins = pe.matmul(banks[64 * k:64 * k + 64, t % 3, m * 64:(m + 1) * 64],
                                            x_bd(t)[:, m * 128 + k * 64:m * 128 + k * 64 + 64],
                                            g_b[:, t * 512 + m * 64:t * 512 + (m + 1) * 64], start=True, stop=True)
                    ins.then_inc(s1_pe, 1)
                t = j - 1
                if t >= 0:
                    pe.wait_ge(tbd_ready, t + 1)
                    if t >= 3:
                        pe.wait_ge(hb_ready, t - 2)
                    for m in range(8):
                        n, x = m // 2, m % 2
                        ins = pe.matmul(banks[64 * x:64 * x + 64, 3 + t % 3, n * 128:(n + 1) * 128],
                                        g_a[:, t * 512 + m * 64:t * 512 + (m + 1) * 64],
                                        t_bd(t)[:, m * 128:(m + 1) * 128], start=True, stop=True)
                    ins.then_inc(s2_pe, 1)

            pe.wait_ge(h_ready, TILES)
            pe.wait_ge(wd_in, 32)
            pe.wait_ge(wd_zero, 1)
            hp = h_all[:, :].rearrange("p (m c) -> p m c", c=64)
            for c in range(64):
                ins = pe.matmul(banks[:, 6, 0:256], wd_bd[:, c * 128:(c + 1) * 128], hp[:, :, c],
                                start=(c == 0), stop=(c == 63))
            ins.then_inc(rd["log_pe"], 1)
            pe.wait_ge(rd["log"], 1)
            lt2 = logT_dn.rearrange("p (P k) -> p P k", k=2)
            for k in range(2):
                ins = pe.transpose(banks[:, 7, k * 128:(k + 1) * 128], lt2[:, :, k], ident)
            ins.then_inc(rd["lgT_pe"], 1)
            pe.wait_ge(rd["oh"], 1)
            oh = oh_dn.rearrange("p (k x s e) -> p k x s e", k=2, x=2, s=2)
            for x in range(2):
                for k in range(2):
                    for s in range(2):
                        c = (k * 2 + s) * 128
                        ins = pe.matmul(banks[:, x, c:c + 128], oh[:, k, x, s, :], ident_b[:, :],
                                        start=True, stop=True)
            ins.then_inc(rd["oh_pe"], 1)
            ohq = oh_dn.rearrange("p (m e) -> p m e", e=128)
            par = lambda ap, c: ap.rearrange("p (m c) -> p m c", c=2)[:, :, c]
            for c in range(2):
                for m in range(8):
                    ins = pe.matmul(banks[:, 2 + c, m * 64:(m + 1) * 64], ohq[:, m, :], par(ident_b[:, :], c),
                                    start=True, stop=True)
            ins.then_inc(rd["oh_pe"], 1)
            pe.wait_ge(rd["prb"], 1)
            for m in range(8):
                for c in range(2):
                    ins = pe.matmul(banks[64 * c:64 * c + 64, 4, m * 64:(m + 1) * 64],
                                    prb_dn[:, m * 64:(m + 1) * 64], par(ident, c), start=True, stop=True)
            ins.then_inc(rd["pb_pe"], 1)
            pe.wait_ge(rd["ohT_a"], 1)
            pe.wait_ge(rd["ohT_d"], 1)
            pe.wait_ge(rd["pb"], 1)
            pe.wait_ge(split_act, 2 * SPLIT)
            pe.wait_ge(abd_zero, 2)
            for k in range(4):
                for tb in range(2):
                    ohT = (oh_a_T if tb == 0 else oh_b_T).rearrange("p (x s m) -> p x s m", x=2, s=2)[:, :, :, 64 * k:64 * k + 64]
                    for v in range(8):
                        if tb == 1 or (v >= 4):
                            if tb == 1 and v >= 4:
                                n = 4 * k + (v - 4) // 2 + 1
                                pe.wait_ge(db_act if v % 2 == 0 else db_dve, n)
                            else:
                                n = 8 * k + (v - 4) % 8 + 1
                                pe.wait_ge(da_act, n)
                                pe.wait_ge(da_dve, n)
                        elif k >= 1:
                            pe.wait_ge(db_act if v % 2 == 0 else db_dve, 4 * (k - 1) + (v + 4) // 2 + 1)
                        for oi in range(4):
                            o = 4 * v + oi
                            for i, parts in enumerate((dn_hm, dn_lo)):
                                for x in range(2):
                                    ins = pe.matmul(banks[64 * x:64 * x + 64, v % 4, oi * 128:(oi + 1) * 128],
                                                    parts[tb][:, o * 64:(o + 1) * 64], ohT[:, x],
                                                    start=(i == 0), stop=(i == 1))
                        ins.then_inc(da_pe if tb == 0 else db_pe, 1)
                pe.wait_ge(da_act, 8 * k + 8)
                pe.wait_ge(da_dve, 8 * k + 8)
                for j in range(9):
                    t = 8 * k + j
                    if j < 8:
                        if t >= 2:
                            pe.wait_ge(ubd_ready, t - 1)
                        for n4h in range(2):
                            for k2 in range(2):
                                for c in range(2):
                                    m = (n4h * 2 + c) * 2 + k2
                                    o = (n4h * 2 + k2) * 128
                                    ins = pe.matmul(banks[64 * c:64 * c + 64, 4 + t % 2, o:o + 128],
                                                    h_all[:, t * 512 + m * 64:t * 512 + (m + 1) * 64],
                                                    a_bd[:, (j * 8 + m) * 128:(j * 8 + m + 1) * 128],
                                                    start=True, stop=True)
                        ins.then_inc(d1_pe, 1)
                    t = 8 * k + j - 1
                    if j >= 1:
                        if j == 1:
                            pe.wait_ge(db_act, 4 * k + 4)
                            pe.wait_ge(db_dve, 4 * k + 4)
                        pe.wait_ge(ubd_ready, t + 1)
                        if t >= 2:
                            pe.wait_ge(y_ev, t - 1)
                        for n4h in range(2):
                            for q in range(4):
                                for s in range(2):
                                    m = n4h * 4 + q
                                    ins = pe.matmul(banks[32 * q:32 * q + 32, 6 + t % 2, n4h * 64:(n4h + 1) * 64],
                                                    b_nat[:, (((j - 1) * 8 + m) * 2 + s) * 32:(((j - 1) * 8 + m) * 2 + s + 1) * 32],
                                                    u_bd(t)[:, (m * 2 + s) * 64:(m * 2 + s + 1) * 64],
                                                    start=(s == 0), stop=(s == 1))
                        ins.then_inc(d2_pe, 1)

            attention(1)

            pe.wait_ge(lora_in, 16 * 9)
            pe.wait_ge(ff["lb"], 1)
            for j in steps(3):
                k = j
                if here(k):
                    pe.wait_ge(ff["ln"], k + 1)
                    if k >= 1:
                        pe.wait_ge(ff["lnT"], k)
                    transpose4(0, f_ln(k)).then_inc(ff["lnT_pe"], 1)
                k = j - 3
                if here(k):
                    if k >= 1:
                        pe.wait_ge(ff["y"], k)
                    for i in range(CHUNK):
                        for fc in range(FC):
                            if i == 0:
                                pe.wait_ge(ff["h"], FC * k + fc + 1)
                            ins = pe.matmul(banks[:, 5, i * D:(i + 1) * D],
                                            h_s(k)[:, fc * W + i * D:fc * W + (i + 1) * D],
                                            wo_s[:, fc * 128:(fc + 1) * 128], start=(fc == 0), stop=(fc == FC - 1))
                    ins.then_inc(ff["o_pe"], 1)
                k = j - 2
                if here(k):
                    pe.wait_ge(ff["lora"], k + 1)
                    lv = lora_T(k).rearrange("p (v m) -> p v m", v=2)

                    def slot0(fc):
                        n = FC * k + fc
                        f = slice(fc * 128, (fc + 1) * 128)
                        if n >= 3:
                            pe.wait_ge(ff["h2"], n - 2)
                        pe.matmul(banks[:, 2 + n % 3, :], wi_s[:, f], f_lnT(k), start=True, stop=False)
                        pe.matmul(banks[:, 2 + n % 3, :], lb_part[:, f], lv[:, 0, :], start=False, stop=True,
                                  ).then_inc(ff["z1_pe"], 1)

                    def slot1(fc):
                        n = FC * k + fc
                        f = slice(fc * 128, (fc + 1) * 128)
                        pe.wait_ge(ff["h1"], n + 1)
                        pe.matmul(banks[:, 2 + n % 3, :], lb_part[:, f], lv[:, 1, :], start=False, stop=True,
                                  skip_group_check=True).then_inc(ff["z2_pe"], 1)

                    slot0(0)
                    slot0(1)
                    slot1(0)
                    slot0(2)
                    slot1(1)
                    slot0(3)
                    slot1(2)
                    slot1(3)
                k = j
                if here(k):
                    pe.wait_ge(ff["lnT"], k + 1)
                    if k >= 1:
                        pe.wait_ge(ff["proj"], k)
                    for i in range(CHUNK):
                        ins = pe.matmul(banks[:, 7, i * PROJ:(i + 1) * PROJ], f_lnT(k)[:, i * D:(i + 1) * D],
                                        wga_s, start=True, stop=True)
                    ins.then_inc(ff["proj_pe"], 1)
                k = j - 1
                if here(k):
                    pe.wait_ge(ff["parts"], k + 1)
                    if k >= 1:
                        pe.wait_ge(ff["lora"], k)
                    lp = l_parts.rearrange("p (m c) -> p m c", m=2 * CHUNK)
                    lb = banks[0:96, 1, :].bitcast(BF16).rearrange("p (m c) -> p m c", m=2 * CHUNK)
                    for m in range(2 * CHUNK):
                        ins = pe.transpose(lb[:, m, :], lp[:, m, :], ident_b[:, :])
                    ins.then_inc(ff["lora_pe"], 1)
                    pe.wait_ge(ff["ratio_w"], k + 1)
                    if k >= 1:
                        pe.wait_ge(ff["ratio"], k)
                    for i in range(CHUNK):
                        ins = pe.matmul(banks[:, 6, i * D:(i + 1) * D],
                                        r_ratio[:, i:i + 1].broadcast_to([128, 128]), ident, start=True, stop=True)
                    ins.then_inc(ff["ratio_pe"], 1)


def kernel(**inputs):
    import numpy as np
    import concourse.bacc as bacc
    from concourse import mybir as _mybir
    from concourse.bass_utils import run_bass_kernel_spmd

    v = {k: np.asarray(a) for k, a in inputs.items()}
    f32 = np.float32
    r = np.arange(128)
    same = (r[:, None] // 64) == (r[None, :] // 64)
    e4 = np.arange(4)
    consts = np.zeros((128, 472), f32)
    consts[:, 0:128] = np.eye(128, dtype=f32)
    consts[:, 128:256] = np.where(same & (r[None, :] <= r[:, None]), 0.0, -1e30)
    consts[:, 256:384] = np.where(same, 0.0, -1e30)
    consts[:, 384:448] = np.arange(64)
    consts[:, 448:464] = (e4[None, :] < e4[:, None]).reshape(-1)
    consts[:, 464:466] = np.arange(2)
    place = r[:96] // 16
    for c, places in enumerate(((0, 1, 5), (2, 3), (4,))):
        consts[:96, 466 + c] = np.isin(place, places)

    def t(name):
        return v[name].T

    arrays = {
        "x": v["x"].reshape(TILES, 128, D),
        "ctx": v["ctx_1024"].reshape(TILES, 128, D),
        "consts": consts,
        "gates": np.concatenate([v["g_xattn"], v["g_ffn"], v["L0_ffn_scale_up"], v["L0_ffn_scale_down"]])[None, :],
        "rows": np.concatenate([v["L0_xattn_bff"], v["L1_xattn_bv"], v["L1_ffn_bg"]])[None, :],
        "cols": np.stack([v["L0_xattn_bq"], v["L0_xattn_bk"], v["L0_xattn_bv"], v["L1_xattn_bq"],
                          v["L1_xattn_bk"]], axis=1),
        "attn_w": np.concatenate([t("L0_xattn_Wq"), t("L0_xattn_Wk"), t("L0_xattn_Wff"), v["L0_xattn_Wv"],
                                  t("L1_xattn_Wq"), t("L1_xattn_Wk"), t("L1_xattn_Wv")], axis=1),
        "w_up_router": v["L0_ffn_W_up"].reshape(64, 8, 128).transpose(2, 1, 0).reshape(128, 512),
        "w_down_router": v["L0_ffn_W_down"].reshape(64, 64, 64).transpose(1, 2, 0),
        "a_up": v["L0_ffn_A_up"].reshape(64, 64, 8, 4).transpose(0, 1, 3, 2).reshape(64, 2048),
        "b_up": v["L0_ffn_B_up"].reshape(64, 2048),
        "a_down": v["L0_ffn_A_down"].reshape(64, 2048),
        "b_down": v["L0_ffn_B_down"].reshape(64, 2048),
        "bias_up": v["L0_ffn_bias_up"].reshape(64, 64),
        "bias_down": v["L0_ffn_bias_down"].reshape(32, 32).T,
        "wi_t": t("L1_ffn_Wi"),
        "wo_t": v["L1_ffn_Wo"].T.reshape(FC, 128, D).transpose(1, 0, 2).reshape(128, FC * D),
        "wg_a": np.concatenate([t("L1_ffn_Wg"), v["L1_ffn_A"].reshape(LR, D).T], axis=1),
        "lora_b": v["L1_ffn_B"].transpose(0, 2, 1).reshape(LR, HIDDEN),
    }
    nc = bacc.Bacc("TRN2", target_bir_lowering=False, num_devices=1)
    feed, args = {}, []
    for name, a in arrays.items():
        a = np.ascontiguousarray(a)
        feed[f"in_{name}"] = a
        args.append(nc.dram_tensor(f"in_{name}", a.shape, _mybir.dt.from_np(a.dtype), kind="ExternalInput").ap())
    res = nc.dram_tensor("out_x", (TILES, 128, D), _mybir.dt.float32, kind="ExternalOutput").ap()
    flamingo_kernel(nc, *args, res)
    got = run_bass_kernel_spmd(nc, [feed], core_ids=[0])
    return got.results[0]["out_x"].reshape(64, 64, D)
```

```python
from contextlib import ExitStack

import concourse.bass as bass
from concourse import mybir

F32 = mybir.dt.float32
BF16 = mybir.dt.bfloat16
U32 = mybir.dt.uint32
I32 = mybir.dt.int32
ALU = mybir.AluOpType
ACT = mybir.ActivationFunctionType
AX_X = mybir.AxisListType.X

ROWS, D = 4096, 128
TILES = ROWS // 128
CHUNK = 4
W = CHUNK * D
CHUNKS = TILES // CHUNK
EPS = 1e-5
NEWTON = 3
KEEP_UP, KEEP_UP2, KEEP_DOWN, KEEP_DOWN2 = 12, 8, 20, 10
KEEP_TAIL = 12
SCALE = float(D) ** -0.5
HIDDEN, FC = 512, 4
LORA_E, LORA_R = 4, 4
LR = LORA_E * LORA_R
PROJ = LORA_E + LR


def spread(ap, axis, n):
    u = ap.unsqueeze(axis)
    shape = list(u.shape)
    shape[axis] = n
    return u.broadcast_to(shape)


def flamingo_kernel(nc, x_in, ctx_in, consts, gates, rows, cols, attn_w, w_up_router, w_down_router,
                    a_up, b_up, a_down, b_down, bias_up, bias_down, wi_t, wo_t, wg_a, lora_b, out):
    with ExitStack() as ctx:
        def sb(name, n, dt=F32, p=128):
            return ctx.enter_context(nc.sbuf_tensor(name, [p, n], dt))

        def sem(name):
            return ctx.enter_context(nc.semaphore(name))

        banks = ctx.enter_context(nc.psum_tensor("banks", [128, 8, 512], F32))

        x_res = sb("x_res", TILES * D)
        region_h = sb("region_h", 16384)
        region_a = sb("region_a", 16384)
        region_t = sb("region_t", 4096)
        region_x = sb("region_x", 4096)
        region_r = sb("region_r", 4096)
        const = sb("const", 472)
        gate = sb("gate", 6)
        tgate = sb("tgate", 4)
        row_c = sb("row_c", 260)
        col_c = sb("col_c", 5)
        w_att = sb("w_att", 7 * 128)
        w_vff = sb("w_vff", 128)
        bias_x = sb("bias_x", 2 * 128)
        shared = sb("shared", 1024)
        prob = sb("prob", 512)
        bup = sb("bup", 64)
        ident_b = sb("ident_b", 128, BF16)
        stat = sb("stat", 2 * CHUNK * 6)
        mv = sb("mv", 2 * 2 * CHUNK * 2)
        rstd = sb("rstd", 6 * CHUNK)
        shift = sb("shift", 6 * CHUNK)
        mx = sb("mx", CHUNK)
        newton = sb("newton", 8 * CHUNK)
        negm = sb("negm", 2 * CHUNK)
        rsum = sb("rsum", 2 * CHUNK)
        rinv = sb("rinv", CHUNK)
        v8 = sb("v8", 32)
        ix8 = sb("ix8", 32, U32)
        idx = sb("idx", 8)
        gap = sb("gap", 4)
        egap = sb("egap", 4)
        den = sb("den", 4)
        pr = sb("pr", 8)

        ident = const[:, 0:128]
        masks = [const[:, 128:256], const[:, 256:384]]
        iota = const[:, 384:448]
        tri = const[:, 448:464]
        slot_id = const[:, 464:466]
        sel = const[0:96, 466:469]
        wq = [w_att[:, 0:128], w_att[:, 512:640]]
        wk = [w_att[:, 128:256], w_att[:, 640:768]]
        wff_t, wv0 = w_att[:, 256:384], w_att[:, 384:512]
        wout = [w_vff[:, :], w_att[:, 768:896]]
        y_r = lambda t: w_att[:, (t % 4) * 128:(t % 4) * 128 + 128]
        bq = [col_c[:, 0:1], col_c[:, 3:4]]
        bk = [col_c[:, 1:2], col_c[:, 4:5]]
        bv0 = col_c[:, 2:3]

        def step_buf(region, at, n, k):
            return region[:, at + (k % n) * W:at + (k % n) * W + W]

        def ctx_ring(L, k):
            return step_buf(region_h, 4096, 4, k) if L == 0 else step_buf(region_t, 2048, 4, k)

        A = region_a
        att_buf = lambda L, i, k: (step_buf(A, 1024 * i, 2, k) if L == 0 or i == 8 else
                                   step_buf(region_x if i < 4 else region_r, 1024 * (i % 4), 2, k))
        ctxT_s = lambda L, k: att_buf(L, 0, k)
        ln_s = lambda L, k: att_buf(L, 1, k)
        lnT_s = lambda L, k: att_buf(L, 2, k)
        kT_s = lambda L, k: att_buf(L, 3, k)
        qT_s = lambda L, k: att_buf(L, 4, k)
        sm_s = lambda L, k: att_buf(L, 5, k)
        prob_s = lambda L, k: att_buf(L, 6, k)
        pT_s = lambda L, k: att_buf(L, 7, k)
        uT_s = lambda L, k: att_buf(L, 8, k)
        vff_tmp = A[:, 9216:9472]
        mln_s = lambda k: step_buf(A, 12288, 2, k)
        logT_up = A[0:64, 13312:13824]
        lg_up = A[:, 13824:14080]
        oh_up = A[:, 14592:15104].bitcast(BF16)
        prb_up = A[:, 14336:14592]
        bias_rows = A[:, 10240:10368]
        logT_dn = A[:, 8192:8448]
        lg_dn = A[:, 8448:8704]
        oh_dn = A[:, 8704:8960].bitcast(BF16)
        prb_dn = A[:, 8960:9472]

        lnT_all = region_h[:, 0:4096]
        raw_up = region_h[:, 8192:12288]
        h_all = region_h
        g_b, g_a = region_h, region_a
        wu = shared[:, 0:512]
        oh_up_T = shared[:, 512:1024].bitcast(BF16)
        oh_a_T = shared[:, 0:256].bitcast(BF16)
        oh_b_T = shared[:, 256:512].bitcast(BF16)
        up_hm = [region_t[:, 0:1024].bitcast(BF16), region_t[:, 1024:2048].bitcast(BF16)]
        up_lo = [region_t[:, 2048:3072].bitcast(BF16), region_t[:, 3072:4096].bitcast(BF16)]
        xT = region_x
        x_bd = lambda t: region_r[:, (t % 3) * 1024:(t % 3) * 1024 + 1024] if t % 3 < 2 else shared[:, :]
        t_bd = lambda t: region_r[:, 2048 + (t % 2) * 1024:2048 + (t % 2) * 1024 + 1024]
        u_bd = lambda t: region_t[:, (t % 2) * 1024:(t % 2) * 1024 + 1024]
        raw_dn = region_t
        dn_part = [region_x.bitcast(BF16), region_a[:, 12288:16384].bitcast(BF16),
                   region_r.bitcast(BF16)]
        wd_bd = a_bd = region_a[:, 0:8192]
        b_nat = region_a[:, 8192:12288]

        H = region_h
        f_ln = lambda k: step_buf(H, 0, 2, k)
        f_lnT = lambda k: step_buf(H, 13824, 3, k)
        h1_s = H[:, 2048:4096]
        h2_s = H[:, 4096:6144]
        lora_T = lambda k: H[0:96, 6144 + (k % 2) * 512:6656 + (k % 2) * 512].bitcast(BF16)
        wi_s = H[:, 8192:8704]
        wo_s = H[:, 8704:9216]
        wga_s = H[:, 9216:9236]
        lb_raw = H[0:96, 9728:10240]
        lb_hi = H[0:96, 10240:10496].bitcast(BF16)
        lb_mid = H[0:96, 10496:10752].bitcast(BF16)
        lb_part = H[0:96, 10752:11008].bitcast(BF16)
        proj = lambda k: H[:, 11008 + (k % 2) * 80:11008 + (k % 2) * 80 + 80]
        T0 = 11264
        r_max = H[:, T0:T0 + 4]
        r_sh = H[:, T0 + 16:T0 + 32]
        r_exp = H[:, T0 + 32:T0 + 48]
        r_gt = H[:, T0 + 64:T0 + 128]
        r_eq = H[:, T0 + 128:T0 + 192]
        r_rank = H[:, T0 + 192:T0 + 208]
        r_mask = H[:, T0 + 256:T0 + 288]
        r_pick = H[:, T0 + 288:T0 + 304]
        r_sum = H[:, T0 + 320:T0 + 324]
        r_inv = H[:, T0 + 328:T0 + 332]
        r_ratio = H[:, T0 + 344:T0 + 348]
        r_w0 = lambda k: H[:, T0 + 352 + 4 * (k % 3):T0 + 356 + 4 * (k % 3)]
        l_low = H[:, T0 + 384:T0 + 512]
        l_rest = H[:, T0 + 512:T0 + 640]
        l_parts = H[:, T0 + 640:T0 + 1024].bitcast(BF16)
        h_s = lambda k: A[:, 10240 + (k % 2) * 2048:12288 + (k % 2) * 2048]
        ratio_T = H[:, 12800:13312]

        consts_in, weights_in, small_in = sem("consts_in"), sem("weights_in"), sem("small_in")
        up_raw_in, down_raw_in, router_in = sem("up_raw_in"), sem("down_raw_in"), sem("router_in")
        lora_in, wd_in = sem("lora_in"), sem("wd_in")
        x_in_sem = [sem(f"x_in_{k}") for k in range(CHUNKS)]
        ctx_in_sem = [sem(f"ctx_in_{i}") for i in range(4)]
        names = ("stats ln xb ctxT_pe lnT_pe ctxT lnT k_pe q_pe k q s_pe s_ev sm prob pt_pe pt u_pe u "
                 "o_pe x").split()
        att = [{n: sem(f"att{L}_{n}") for n in names} for L in range(2)]
        gates_ready, ident_b_ready = sem("gates_ready"), sem("ident_b_ready")
        vff_pe, vff_ready, bv_ready, bias_ready = (sem("vff_pe"), sem("vff_ready"), sem("bv_ready"),
                                                   sem("bias_ready"))
        tables_up = sem("tables_up")
        m_stats, m_ln, m_lnT_pe, m_lnT, m_xt = (sem("m_stats"), sem("m_ln"), sem("m_lnT_pe"),
                                                sem("m_lnT"), sem("m_xt"))
        ru = {n: sem(f"ru_{n}") for n in "log_pe log lgT_pe gap egap oh oh_pe ohT_a ohT_d prb pb_pe pb".split()}
        rd = {n: sem(f"rd_{n}") for n in "log_pe log lgT_pe gap egap oh oh_pe ohT_a ohT_d prb pb_pe pb".split()}
        g_pe, g_act, g_dve = sem("g_pe"), sem("g_act"), sem("g_dve")
        xbd_ready, s1_pe, tbd_ready, s2_pe, hb_ready, h_ready = (
            sem("xbd_ready"), sem("s1_pe"), sem("tbd_ready"), sem("s2_pe"), sem("hb_ready"), sem("h_ready"))
        wd_zero, split_act, split_dve, split_pool, split_zero = (
            sem("wd_zero"), sem("split_act"), sem("split_dve"), sem("split_pool"), sem("split_zero"))
        mv_ready = sem("mv_ready")
        xbd_pool, down_bias = sem("xbd_pool"), sem("down_bias")
        da_pe, da_act, da_dve, db_pe, db_act, db_dve = (sem("da_pe"), sem("da_act"), sem("da_dve"),
                                                        sem("db_pe"), sem("db_act"), sem("db_dve"))
        d1_pe, ubd_ready, d2_pe = sem("d1_pe"), sem("ubd_ready"), sem("d2_pe")
        y_rows, x2 = sem("y_rows"), sem("x2")
        fnames = ("hi mid rest stats ln lnT_pe lnT proj_pe proj low parts lora_pe lora exp_in exp lb z1_pe z2_pe h1 h2 "
                  "o_pe y ratio_w ratio_pe ratio h").split()
        ff = {n: sem(f"ff_{n}") for n in fnames}
        stored = sem("stored")
        dve_step, pool_step = sem("dve_step"), sem("pool_step")

        block = ctx.enter_context(nc.Block())

        def here(k):
            return 0 <= k < CHUNKS

        ATT_STEPS = [range(CHUNKS + 5), range(CHUNKS + 3)]
        FF_STEPS = range(CHUNKS + 3)
        UP_CASTS = {2: (0,), 3: (1,), 5: (2,), 8: (3,), 9: (4,), 10: (5,), 11: (6,), 12: (7,)}
        UP_RESTS = {3: (0,), 5: (1,), 9: (2,), 11: (3,)}
        ATT1_EARLY = {3: 0, 6: 1}

        SPLIT = 8

        def split_cast(act, n, raw, hm, lo):
            tb, stage = ((0, 0), (1, 0), (0, 1), (0, 2), (1, 1), (1, 2), (0, 3), (1, 3))[n]
            src = raw[:, tb * 2048:(tb + 1) * 2048]
            if stage == 1:
                act.wait_ge(split_pool, tb + 1)
            if stage == 3:
                act.wait_ge(split_pool, tb + 3)
            dst, part = ((hm[tb], slice(0, 128)), (hm[tb], slice(64, 128)), (lo[tb], slice(0, 64)),
                         (lo[tb], slice(0, 64)))[stage]
            act.activation(dst[part, :], src[part, :], ACT.Copy).then_inc(split_act, 1)

        def split_rest(pool, n, raw, hm, lo):
            tb, part = n % 2, slice(0, 128) if n < 2 else slice(0, 64)
            src = raw[part, tb * 2048:(tb + 1) * 2048]
            pool.wait_ge(split_act, (1, 2, 4, 6)[n])
            pool.tensor_tensor(src, src, (hm if n < 2 else lo)[tb][part, :], ALU.subtract
                               ).then_inc(split_pool, 1)

        def x_blocks(t):
            return (x_bd(t).rearrange("p (n x g i) -> p n x g i", n=4, x=2, g=4),
                    xT[:, t * 128:(t + 1) * 128].rearrange("p (n i) -> p n i", n=4))

        def inverse_std(eng, link, scratch, n, ks, home, done, used):
            w = CHUNK * len(ks)
            m = mv[:, 16 * (n % 2):16 * (n % 2) + 2 * w].rearrange("p (t c) -> p t c", c=2)
            var, half = scratch[:, 0:w], scratch[:, 2 * CHUNK:2 * CHUNK + w]
            y = rstd[:, home:home + w]
            if used:
                eng.wait_ge(*used)
            link(eng.tensor_scalar(var, m[:, :, 1], EPS, None, ALU.add))
            link(eng.tensor_scalar(y.bitcast(I32), var.bitcast(I32), -0.5, float(0x5F3759DF), ALU.mult, ALU.add))
            for i in range(NEWTON):
                link(eng.tensor_tensor(half, y, y, ALU.mult))
                link(eng.tensor_tensor(half, half, var, ALU.mult))
                link(eng.tensor_scalar(half, half, -0.5, 1.5, ALU.mult, ALU.add))
                link(eng.tensor_tensor(y, half, y, ALU.mult))
            link(eng.tensor_tensor(half, m[:, :, 0], y, ALU.mult))
            link(eng.tensor_scalar(shift[:, home:home + w], half, -1.0, None, ALU.mult))
            eng.nop().then_inc(done, 1)

        M_ON_VECTOR = (6, 7)

        def q_out(L, k, eng):
            S = att[L]
            eng.wait_ge(S["q_pe"], k + 1)
            if k >= 2:
                eng.wait_ge(S["s_pe"], k - 1)
            if L == 0:
                eng.tensor_scalar(qT_s(L, k), banks[:, 3, :], bq[L], None, ALU.add).then_inc(S["q"], 1)
            else:
                eng.activation(qT_s(L, k), banks[:, 3, :], ACT.Identity, bias=bq[L]).then_inc(S["q"], 1)

        def linker(eng, step_sem):
            count = [0]

            def link(ins):
                count[0] += 1
                ins.then_inc(step_sem, 1)
                eng.wait_ge(step_sem, count[0])
            return link

        @block.sync
        def _(sp):
            def rows_in(k):
                sp.dma_start(x_res[:, k * W:(k + 1) * W].rearrange("p (t d) -> p t d", t=CHUNK),
                             x_in[k * CHUNK:(k + 1) * CHUNK].rearrange("t p d -> p t d")).then_inc(x_in_sem[k], 16)

            rows_in(0)
            rows_in(1)
            sp.dma_start(const[:, :], consts).then_inc(consts_in, 16)
            sp.dma_start(ctx_ring(0, 0).rearrange("p (t d) -> p t d", t=CHUNK),
                         ctx_in[0:CHUNK].rearrange("t p d -> p t d")).then_inc(ctx_in_sem[0], 16)
            sp.dma_start(gate[:, :], gates.broadcast_to([128, 6])).then_inc(small_in, 16)
            sp.dma_start(row_c[:, :], rows.broadcast_to([128, 260])).then_inc(small_in, 16)
            sp.dma_start(col_c[:, :], cols).then_inc(small_in, 16)
            sp.dma_start(w_att[:, :], attn_w).then_inc(weights_in, 16)
            rows_in(2)
            rows_in(3)
            for k in range(1, CHUNKS):
                if k == 3:
                    for i in range(4, CHUNKS):
                        rows_in(i)
                if k >= 4:
                    sp.wait_ge(att[0]["u_pe"], k - 3)
                sp.dma_start(ctx_ring(0, k).rearrange("p (t d) -> p t d", t=CHUNK),
                             ctx_in[k * CHUNK:(k + 1) * CHUNK].rearrange("t p d -> p t d")
                             ).then_inc(ctx_in_sem[k % 4], 16)
                if k == 2:
                    for tb, table in enumerate((b_up, a_up)):
                        for half in range(2):
                            sp.dma_start(raw_up[64 * half:64 * half + 64, tb * 2048:tb * 2048 + 2048],
                                         table).then_inc(up_raw_in, 16)
                if k == 3:
                    sp.dma_start(wu, w_up_router).then_inc(router_in, 16)
                    for half in range(2):
                        sp.dma_start(bup[64 * half:64 * half + 64, :], bias_up).then_inc(router_in, 16)
                    sp.dma_start(bias_rows[:, :], bias_down).then_inc(router_in, 16)
            sp.wait_ge(g_pe, 32)
            for tb, table in enumerate((a_down, b_down)):
                for half in range(2):
                    sp.dma_start(raw_dn[64 * half:64 * half + 64, tb * 2048:tb * 2048 + 2048],
                                 table).then_inc(down_raw_in, 16)
            sp.wait_ge(s2_pe, TILES // 2)
            for half in range(2):
                sp.dma_start(wd_bd[64 * half:64 * half + 64, :].rearrange("p (j x e) -> p j x e", j=64, x=2)[:, :, half, :],
                             w_down_router).then_inc(wd_in, 16)
            sp.wait_ge(split_act, SPLIT + 6)
            for k in range(CHUNKS):
                if k >= 4:
                    sp.wait_ge(att[1]["u_pe"], k - 3)
                sp.dma_start(ctx_ring(1, k).rearrange("p (t d) -> p t d", t=CHUNK),
                             ctx_in[k * CHUNK:(k + 1) * CHUNK].rearrange("t p d -> p t d")
                             ).then_inc(ctx_in_sem[k % 4], 16)
                if k == 3:
                    sp.wait_ge(d1_pe, TILES)
                    sp.dma_start(wi_s, wi_t).then_inc(lora_in, 16)
                    sp.dma_start(wo_s, wo_t).then_inc(lora_in, 16)
                    sp.dma_start(wga_s, wg_a).then_inc(lora_in, 16)
                    for i in range(6):
                        sp.dma_start(lb_raw[i * LR:(i + 1) * LR, :], lora_b).then_inc(lora_in, 16)
            for k in range(CHUNKS):
                sp.wait_ge(ff["y"], k + 1)
                sp.dma_start(out[k * CHUNK:(k + 1) * CHUNK].rearrange("t p d -> p t d"),
                             x_res[:, k * W:(k + 1) * W].rearrange("p (t d) -> p t d", t=CHUNK)
                             ).then_inc(stored, 16)
            sp.wait_ge(stored, 16 * CHUNKS)

        @block.gpsimd
        def _(pool):
            link = linker(pool, pool_step)

            chains = [0]

            def rstd_chain(ks, home, done, used):
                chains[0] += 1
                pool.wait_ge(mv_ready, chains[0])
                inverse_std(pool, link, newton[:, 0:4 * CHUNK], chains[0] - 1, ks, home, done, used)

            def pair_chain(p, S, before):
                used = (S["ln"], 2 * p - 2) if p >= 2 else (before["ln"], 2 * p + 6) if before else None
                rstd_chain((2 * p, 2 * p + 1), 2 * CHUNK * (p % 2), S["stats"], used)

            def lora_factors(n):
                pick = lambda c: sel[:, c:c + 1].broadcast_to([96, HIDDEN])
                if n == 0:
                    pool.wait_ge(lora_in, 16 * 9)
                    link(pool.tensor_copy(lb_hi, lb_raw))
                elif n == 1:
                    link(pool.tensor_tensor(lb_raw, lb_raw, lb_hi, ALU.subtract))
                elif n == 2:
                    link(pool.tensor_copy(lb_mid, lb_raw))
                elif n == 3:
                    link(pool.tensor_tensor(lb_raw, lb_raw, lb_mid, ALU.subtract))
                    link(pool.tensor_tensor(lb_hi, lb_hi, pick(0), ALU.mult))
                elif n == 4:
                    link(pool.tensor_tensor(lb_mid, lb_mid, pick(1), ALU.mult))
                    link(pool.tensor_tensor(lb_part, lb_raw, pick(2), ALU.mult))
                elif n == 5:
                    link(pool.tensor_tensor(lb_part, lb_part, lb_mid, ALU.add))
                    pool.tensor_tensor(lb_part, lb_part, lb_hi, ALU.add).then_inc(ff["lb"], 1)
                    pool.wait_ge(ff["lb"], 1)

            def attention_step(L, j):
                S, before = att[L], att[0] if L else None
                if L == 0 and j == 0:
                    chains[0] += 1
                if j in (2, 4) or (L, j) == (0, 0):
                    pair_chain(j // 2 + 1, S, before)
                if L == 0 and j == 0:
                    pool.wait_ge(bias_ready, 2)
                k = j
                if here(k):
                    pool.wait_ge(S["ln"], k + 1)
                    xk = x_res[:, k * W:(k + 1) * W].rearrange("p (t d) -> p t d", t=CHUNK)
                    pool.tensor_tensor(xk, xk, spread(bias_x[:, L * 128:(L + 1) * 128], 1, CHUNK),
                                       ALU.add).then_inc(S["xb"], 1)
                    pool.wait_ge(S["xb"], k + 1)
                k = j - 3
                if k in M_ON_VECTOR and L == 0:
                    chains[0] += 1
                elif here(k) and L == 0:
                    rstd_chain((k,), CHUNK * (4 + k % 2), m_stats, (m_ln, k - 1) if k >= 2 else None)
                elif L == 1 and j in (5, 6):
                    pair_chain(j - 5, ff, att[1])
                if L == 1 and 3 <= j < 9:
                    lora_factors(j - 3)
                for n in UP_RESTS.get(j, ()) if L == 0 else ():
                    split_rest(pool, n, raw_up, up_hm, up_lo)
                    pool.wait_ge(split_pool, n + 1)

            for tb in range(2):
                link(pool.memset(up_lo[tb][64:128, :], 0.0))
            pool.memset(region_r[:, :], 0.0).then_inc(tables_up, 1)
            pool.wait_ge(tables_up, 1)
            for j in ATT_STEPS[0]:
                attention_step(0, j)
            pool.wait_ge(router_in, 16 * 4)
            link(pool.tensor_scalar(bias_rows[:, :], bias_rows[:, :], tgate[:, 2:3], None, ALU.mult))
            for k in range(CHUNKS):
                pool.wait_ge(m_ln, k + 1)
                xk = x_res[:, k * W:(k + 1) * W].rearrange("p (t d) -> p t d", t=CHUNK)
                pool.tensor_tensor(xk, xk, spread(bias_rows[:, :], 1, CHUNK), ALU.add).then_inc(down_bias, 1)
                pool.wait_ge(down_bias, k + 1)
            pool.wait_ge(m_xt, CHUNKS)
            wd_off = wd_bd.rearrange("p (k j x e) -> p k j x e", k=4, j=16, x=2)
            for t in range(TILES):
                if t == 2:
                    pool.wait_ge(g_pe, 32)
                    pool.memset(shared[:, :], 0.0).then_inc(tables_up, 1)
                    pool.wait_ge(tables_up, 2)
                if t >= 3:
                    pool.wait_ge(s1_pe, t - 2)
                dst, src = x_blocks(t)
                link(pool.tensor_copy(dst[96:128, :, 0, 3, :], src[64:96, :, :]))
                pool.tensor_copy(dst[96:128, :, 1, 3, :], src[96:128, :, :]).then_inc(xbd_pool, 1)
                pool.wait_ge(xbd_pool, t + 1)
                if 20 <= t < 28:
                    if t == 20:
                        pool.wait_ge(s2_pe, TILES // 2)
                    x = t % 2
                    pool.memset(wd_off[64 * x:64 * x + 64, (t - 20) // 2, :, 1 - x, :], 0.0).then_inc(wd_zero, 1)
                    pool.wait_ge(wd_zero, t - 19)
            for part in range(3):
                pool.wait_ge(xbd_ready if part == 0 else s2_pe, TILES)
                v = dn_part[part].rearrange("p (m x i) -> p m x i", m=64, x=2)
                link(pool.memset(v[0:64, :, 1, :], 0.0))
                pool.memset(v[64:128, :, 0, :], 0.0).then_inc(split_zero, 1)
                pool.wait_ge(split_zero, part + 1)
            pool.wait_ge(split_act, SPLIT + 6)
            pool.memset(region_t[:, 0:2048], 0.0).then_inc(split_zero, 1)

            def ff_step(j):
                k = j - 2
                if here(k):
                    for fc in range(FC):
                        part = slice(fc * W, (fc + 1) * W)
                        pool.wait_ge(ff["h2"], FC * k + fc + 1)
                        pool.wait_ge(ff["h1"], FC * k + fc + 1)
                        if k >= 2 and fc == 0:
                            pool.wait_ge(ff["o_pe"], k - 1)
                        pool.tensor_tensor(h_s(k)[:, part], h1_s[:, part], h2_s[:, part], ALU.add).then_inc(ff["h"], 1)
                if j in (1, 2):
                    pair_chain(j + 1, ff, att[1])

            for t in range(TILES):
                if t in (16, 24):
                    pair_chain((t - 16) // 8, att[1], att[0])
                pool.wait_ge(y_rows, t + 1)
                xt = x_res[:, t * 128:(t + 1) * 128]
                pool.tensor_tensor(xt, xt, y_r(t), ALU.add).then_inc(x2, 1)
                if t - 24 in ATT1_EARLY:
                    attention_step(1, ATT1_EARLY[t - 24])
            for j in ATT_STEPS[1]:
                if j >= len(ATT1_EARLY):
                    attention_step(1, j)
                if j == CHUNKS - 1:
                    ff_step(0)
                if j == CHUNKS + 2:
                    ff_step(1)
            for j in FF_STEPS[2:]:
                ff_step(j)

        @block.scalar
        def _(act):
            def copy(dst, src):
                return act.activation(dst, src, ACT.Copy)

            act.wait_ge(small_in, 48)
            act.activation(tgate[:, :], gate[:, 0:4], ACT.Tanh).then_inc(gates_ready, 1)

            def normalise(dst, k, pairs, stats_sem, done_sem):
                act.wait_ge(stats_sem, k // 2 + 1 if pairs else k + 1)
                for i in range(CHUNK):
                    j = CHUNK * (k % 4 if pairs else 4 + k % 2) + i
                    ins = act.activation(dst[:, i * D:(i + 1) * D], x_res[:, k * W + i * D:k * W + (i + 1) * D],
                                         ACT.Identity, bias=shift[:, j:j + 1], scale=rstd[:, j:j + 1])
                ins.then_inc(done_sem, 1)

            def attention_step(L, j):
                S = att[L]
                if j == 0:
                    if L == 1:
                        act.wait_ge(db_pe, 32)
                    normalise(ln_s(L, 0), 0, True, S["stats"], S["ln"])
                k = j - 3
                if here(k):
                    act.wait_ge(S["pt_pe"], k + 1)
                    if k >= 2:
                        act.wait_ge(S["u_pe"], k - 1)
                    copy(pT_s(L, k), banks[:, 5, :]).then_inc(S["pt"], 1)
                k = j
                if here(k):
                    act.wait_ge(S["ctxT_pe"], k + 1)
                    if k >= 2:
                        act.wait_ge(S["k_pe"], k - 1)
                    copy(ctxT_s(L, k), banks[:, 0, :]).then_inc(S["ctxT"], 1)
                k = j - 2
                if here(k):
                    act.wait_ge(S["sm"], k + 1)
                    if k >= 2:
                        act.wait_ge(S["pt_pe"], k - 1)
                        act.wait_ge(S["x"], k - 1)
                    for i in range(CHUNK):
                        j2 = (k % 2) * CHUNK + i
                        ins = act.activation(prob_s(L, k)[:, i * D:(i + 1) * D], sm_s(L, k)[:, i * D:(i + 1) * D],
                                             ACT.Exp, bias=negm[:, j2:j2 + 1], scale=SCALE,
                                             accum_out=rsum[:, j2:j2 + 1])
                    ins.then_inc(S["prob"], 1)
                k = j - 1
                if here(k):
                    act.wait_ge(S["k_pe"], k + 1)
                    if k >= 2:
                        act.wait_ge(S["s_pe"], k - 1)
                    act.activation(kT_s(L, k), banks[:, 2, :], ACT.Identity, bias=bk[L]).then_inc(S["k"], 1)
                    if L == 1:
                        q_out(L, k, act)
                k = j - 5
                if L == 0 and here(k):
                    act.wait_ge(m_lnT_pe, k + 1)
                    copy(lnT_all[:, k * W:(k + 1) * W], banks[:, 0, :]).then_inc(m_lnT, 1)
                k = j + 1
                if here(k):
                    if k >= 2:
                        act.wait_ge(S["lnT_pe"], k - 1)
                    normalise(ln_s(L, k), k, True, S["stats"], S["ln"])
                k = j - 4
                if L == 0 and here(k):
                    if k >= 2:
                        act.wait_ge(m_lnT_pe, k - 1)
                        act.wait_ge(m_xt, k - 1)
                    normalise(mln_s(k), k, False, m_stats, m_ln)
                if L == 1 and j == CHUNKS - 2:
                    normalise(f_ln(0), 0, True, ff["stats"], ff["ln"])
                for n in UP_CASTS.get(j, ()) if L == 0 else ():
                    if n == 0:
                        act.wait_ge(up_raw_in, 64)
                    split_cast(act, n, raw_up, up_hm, up_lo)

            for j in ATT_STEPS[0]:
                attention_step(0, j)

            act.wait_ge(ru["log_pe"], 4)
            copy(logT_up.rearrange("p (q t n) -> p t q n", q=4, n=4),
                 banks[0:64, 2, :].rearrange("p (t q n) -> p t q n", q=4, n=4)).then_inc(ru["log"], 1)
            act.wait_ge(ru["gap"], 1)
            act.activation(egap[:, :], gap[:, :], ACT.Exp).then_inc(ru["egap"], 1)
            act.wait_ge(ru["oh_pe"], 1)
            copy(oh_up_T[:, 0:512].rearrange("p (s P x) -> p s x P", s=2, x=2),
                 banks[:, 4, :].rearrange("p (s x P) -> p s x P", s=2, x=2)).then_inc(ru["ohT_a"], 1)
            def x_blocks_out(t):
                if t >= 3:
                    act.wait_ge(s1_pe, t - 2)
                if t == 2:
                    act.wait_ge(tables_up, 2)
                dst, src = x_blocks(t)
                for g in range(3):
                    for x in range(2):
                        q = (g // 2) * 2 + x
                        ins = copy(dst[32 * g:32 * g + 32, :, x, g, :], src[32 * q:32 * q + 32, :, :])
                ins.then_inc(xbd_ready, 1)

            act.wait_ge(m_xt, CHUNKS)
            act.wait_ge(tables_up, 1)
            x_blocks_out(0)
            x_blocks_out(1)
            for u in range(0, 32, 2):
                act.wait_ge(g_pe, u + 1)
                if u == 16:
                    act.wait_ge(down_bias, CHUNKS)
                dst = (g_b if u < 16 else g_a)[:, :].rearrange("p (m c) -> p c m", c=64)
                copy(dst[:, 4 * (u % 16):4 * (u % 16) + 4, :],
                     banks[:, 2 * (u % 4):2 * (u % 4) + 2, :].rearrange("p b (c m) -> p (b c) m", c=2)
                     ).then_inc(g_act, 1)
            for j in range(TILES + 4):
                t = j
                if 2 <= t < TILES:
                    x_blocks_out(t)
                t = j - 4
                if t >= 0:
                    act.wait_ge(hb_ready, t + 1)
                    ht = h_all[:, t * 512:(t + 1) * 512]
                    act.activation(ht, ht, ACT.Gelu).then_inc(h_ready, 1)
            act.wait_ge(down_raw_in, 64)
            for part in range(3):
                if part == 0:
                    act.wait_ge(xbd_ready, TILES)
                    act.wait_ge(xbd_pool, TILES)
                else:
                    act.wait_ge(s2_pe, TILES)
                for x in range(2):
                    if part:
                        act.wait_ge(split_dve, 2 * part - 1 + x)
                    raw = raw_dn[64 * x:64 * x + 64, :].rearrange("p (m i) -> p m i", m=64)
                    v = dn_part[part].rearrange("p (m x i) -> p m x i", m=64, x=2)
                    copy(v[64 * x:64 * x + 64, :, x, :], raw).then_inc(split_act, 1)
            act.wait_ge(rd["log_pe"], 1)
            copy(logT_dn, banks[:, 6, 0:256]).then_inc(rd["log"], 1)
            act.wait_ge(rd["gap"], 1)
            act.activation(egap[:, :], gap[:, :], ACT.Exp).then_inc(rd["egap"], 1)
            act.wait_ge(rd["oh_pe"], 1)
            copy(oh_a_T.rearrange("p (s P k) -> p k s P", s=2, k=2),
                 banks[:, 0, :].rearrange("p (k s P) -> p k s P", k=2, s=2)).then_inc(rd["ohT_a"], 1)
            for k in range(4):
                for v in range(8):
                    act.wait_ge(da_pe, 8 * k + v + 1)
                    dst = a_bd.rearrange("p (m x s o) -> p o s m x", m=64, x=2, s=2)
                    src = banks[:, v % 4, :].rearrange("p (o s m) -> p o s m", o=4, s=2)
                    copy(dst[0:64, 4 * v:4 * v + 4, :, :, 0], src[0:64]).then_inc(da_act, 1)
                for v in range(0, 8, 2):
                    act.wait_ge(db_pe, 8 * k + v + 1)
                    dst = b_nat.rearrange("p (m s o) -> p o s m", m=64, s=2)
                    src = banks[:, v % 4, :].rearrange("p (o s m) -> p o s m", o=4, s=2)
                    copy(dst[:, 4 * v:4 * v + 4, :, :], src).then_inc(db_act, 1)

            def ff_front(j):
                k = j
                if here(k):
                    act.wait_ge(ff["lnT_pe"], k + 1)
                    if k >= 3:
                        act.wait_ge(ff["z2_pe"], FC * (k - 2))
                    copy(f_lnT(k), banks[:, 0, :]).then_inc(ff["lnT"], 1)
                k = j - 1
                if here(k):
                    act.wait_ge(ff["exp_in"], k + 1)
                    act.activation(r_exp, r_sh, ACT.Exp).then_inc(ff["exp"], 1)
                k = j + 1
                if here(k):
                    if k >= 2:
                        act.wait_ge(ff["lnT_pe"], k - 1)
                    normalise(f_ln(k), k, True, ff["stats"], ff["ln"])

            def ff_back(j):
                rest = l_rest.rearrange("p (m c) -> p m c", c=LR)
                parts = l_parts.rearrange("p (m six c) -> p m six c", m=2 * CHUNK, six=6)
                k = j - 1
                if here(k):
                    low = l_low.rearrange("p (m c) -> p m c", c=LR)
                    act.wait_ge(ff["low"], k + 1)
                    if k >= 1:
                        act.wait_ge(ff["lora_pe"], k)
                    copy(parts[:, :, 0, :], low).then_inc(ff["hi"], 1)
                    copy(parts[:, :, 2, :], low)
                    copy(parts[:, :, 4, :], low)
                    act.wait_ge(ff["rest"], 2 * k + 1)
                    copy(parts[:, :, 1, :], rest)
                    copy(parts[:, :, 3, :], rest).then_inc(ff["mid"], 1)
                k = j - 2
                if here(k):
                    for fc in range(FC):
                        act.wait_ge(ff["z1_pe"], FC * k + fc + 1)
                        if k >= 1 and fc == 0:
                            act.wait_ge(ff["h"], FC * k)
                        act.activation(h1_s[:, fc * W:(fc + 1) * W], banks[:, 4 + (FC * k + fc) % 3, :],
                                       ACT.Relu).then_inc(ff["h1"], 1)
                k = j - 1
                if here(k):
                    act.wait_ge(ff["rest"], 2 * k + 2)
                    copy(parts[:, :, 5, :], rest).then_inc(ff["parts"], 1)
                    act.wait_ge(ff["ratio_pe"], k + 1)
                    if k >= 1:
                        act.wait_ge(ff["h2"], FC * k)
                    copy(ratio_T, banks[:, 3, :]).then_inc(ff["ratio"], 1)
                    act.wait_ge(ff["lora_pe"], k + 1)
                    if k >= 2:
                        act.wait_ge(ff["z2_pe"], FC * (k - 1))
                    copy(lora_T(k), banks[0:96, 2, :].bitcast(BF16)).then_inc(ff["lora"], 1)

            for j in ATT_STEPS[1]:
                attention_step(1, j)
                if j == CHUNKS - 1:
                    ff_front(0)
                    ff_back(0)
                if j == CHUNKS:
                    ff_front(1)
                if j == CHUNKS + 2:
                    ff_back(1)
            for j in FF_STEPS[2:]:
                ff_front(j)
                ff_back(j)

        @block.vector
        def _(dve):
            link = linker(dve, dve_step)

            handed = [0]
            stats_of = []

            def half_statistics(k, place):
                for i in range(CHUNK):
                    at = 6 * (CHUNK * place + i)
                    ins = dve.bn_stats(stat[:, at:at + 6], x_res[:, k * W + i * D:k * W + (i + 1) * D])
                link(ins)

            def statistics(ks, done, count, half_done=False):
                n = handed[0]
                handed[0] += 1
                stats_of.append((done, count))
                if not half_done:
                    for place, k in enumerate(ks):
                        half_statistics(k, place)
                if n >= 2:
                    dve.wait_ge(*stats_of[n - 2])
                for i in range(CHUNK * len(ks)):
                    at = 16 * (n % 2) + 2 * i
                    ins = dve.bn_aggr(mv[:, at:at + 2], stat[:, 6 * i:6 * i + 6])
                ins.then_inc(mv_ready, 1)
                dve.wait_ge(mv_ready, n + 1)

            def stats(L, p):
                for k in (2 * p, 2 * p + 1):
                    if L == 0:
                        dve.wait_ge(x_in_sem[k], 16)
                    else:
                        dve.wait_ge(x2, CHUNK * (k + 1))
                statistics((2 * p, 2 * p + 1), att[L]["stats"], p + 1)

            def attention_step(L, j):
                S = att[L]
                k = j - 5
                if L == 0 and here(k):
                    dve.wait_ge(m_ln, k + 1)
                    for i in range(CHUNK):
                        t = k * CHUNK + i
                        ins = dve.transpose(
                            xT[:, t * 128:(t + 1) * 128].rearrange("p (n b r) -> p b n r", n=4, b=4),
                            mln_s(k)[:, i * 128:(i + 1) * 128])
                    ins.then_inc(m_xt, 1)
                k = j - 2
                if here(k):
                    dve.wait_ge(S["s_pe"], k + 1)
                    if k >= 2:
                        dve.wait_ge(S["prob"], k - 1)
                    dve.tensor_tensor(sm_s(L, k).rearrange("p (t m) -> p t m", t=CHUNK),
                                      banks[:, 4, :].rearrange("p (t m) -> p t m", t=CHUNK),
                                      spread(masks[L], 1, CHUNK), ALU.add).then_inc(S["s_ev"], 1)
                    dve.wait_ge(S["s_ev"], k + 1)
                    if k >= 1:
                        dve.wait_ge(S["sm"], k)
                    link(dve.tensor_reduce(mx[:, :], sm_s(L, k).rearrange("p (t m) -> p t m", t=CHUNK),
                                           AX_X, ALU.max))
                    dve.tensor_scalar(negm[:, CHUNK * (k % 2):CHUNK * (k % 2 + 1)], mx[:, :], -SCALE, None,
                                      ALU.mult).then_inc(S["sm"], 1)
                k = j
                if here(k):
                    dve.wait_ge(S["lnT_pe"], k + 1)
                    if k >= 2:
                        dve.wait_ge(S["q_pe"], k - 1)
                    dve.tensor_copy(lnT_s(L, k), banks[:, 1, :]).then_inc(S["lnT"], 1)
                k = j - 3
                if here(k):
                    dve.wait_ge(S["u_pe"], k + 1)
                    if k >= 2:
                        dve.wait_ge(S["o_pe"], k - 1)
                    dve.tensor_copy(uT_s(L, k), banks[:, 6, :]).then_inc(S["u"], 1)
                k = j - 1
                if here(k) and L == 0:
                    q_out(L, k, dve)
                if j in (2, 4):
                    stats(L, j // 2 + 1)
                if L == 0 and j == 0:
                    dve.wait_ge(gates_ready, 1)
                    dve.wait_ge(vff_pe, 1)
                    link(dve.tensor_tensor(bias_x[:, 0:128], banks[:, 7, 128:256], row_c[:, 0:128], ALU.add))
                    dve.tensor_scalar(w_vff[:, :], banks[:, 7, 0:128], tgate[:, 0:1], None, ALU.mult)
                    dve.tensor_scalar(wout[1], wout[1], tgate[:, 1:2], None, ALU.mult).then_inc(vff_ready, 1)
                    dve.tensor_scalar(bias_x[:, 0:128], bias_x[:, 0:128], tgate[:, 0:1], None,
                                      ALU.mult).then_inc(bias_ready, 1)
                    dve.tensor_scalar(bias_x[:, 128:256], row_c[:, 128:256], tgate[:, 1:2], None,
                                      ALU.mult).then_inc(bias_ready, 1)
                k = j - 3
                if here(k):
                    dve.wait_ge(S["prob"], k + 1)
                    if k >= 1:
                        dve.wait_ge(S["x"], k)
                    link(dve.reciprocal(rinv[:, :], rsum[:, CHUNK * (k % 2):CHUNK * (k % 2 + 1)]))
                    dve.wait_ge(S["o_pe"], k + 1)
                    dve.wait_ge(S["xb"], k + 1)
                    for i in range(CHUNK):
                        xt = x_res[:, k * W + i * D:k * W + (i + 1) * D]
                        ins = dve.scalar_tensor_tensor(xt, banks[:, 7, i * D:(i + 1) * D], rinv[:, i:i + 1],
                                                       xt, ALU.mult, ALU.add)
                    ins.then_inc(S["x"], 1)
                    if L == 0:
                        dve.wait_ge(S["x"], k + 1)
                        statistics((k,), m_stats, k + 1)
                        if k in M_ON_VECTOR:
                            inverse_std(dve, link, newton[:, 4 * CHUNK:8 * CHUNK], handed[0] - 1, (k,),
                                        CHUNK * (4 + k % 2), m_stats, (m_ln, 6))
                    elif j in (5, 6):
                        dve.wait_ge(S["x"], 2 * (j - 5) + 2)
                        statistics((2 * (j - 5), 2 * (j - 5) + 1), ff["stats"], j - 4)

            stats(0, 0)
            inverse_std(dve, link, newton[:, 4 * CHUNK:8 * CHUNK], 0, (0, 1), 0, att[0]["stats"], None)
            stats(0, 1)
            dve.wait_ge(small_in, 48)
            dve.tensor_copy(vff_tmp[:, 0:128], spread(bv0[:, 0], 1, 128)).then_inc(bv_ready, 1)
            dve.wait_ge(consts_in, 16)
            dve.tensor_copy(ident_b[:, :], ident).then_inc(ident_b_ready, 1)
            for j in ATT_STEPS[0]:
                attention_step(0, j)

            def route(S, lg, log_bank, oh, copies):
                dve.wait_ge(S["lgT_pe"], 1)
                link(dve.tensor_copy(lg, banks[:, log_bank, 0:256]))
                for q in range(4):
                    ins = dve.max(v8[:, 8 * q:8 * q + 8], lg[:, 64 * q:64 * q + 64])
                link(ins)
                for q in range(4):
                    ins = dve.max_index(ix8[:, 8 * q:8 * q + 8], v8[:, 8 * q:8 * q + 8], lg[:, 64 * q:64 * q + 64])
                v = v8[:, :].rearrange("p (q k) -> p q k", k=8)
                dve.tensor_tensor(gap[:, :], v[:, :, 1], v[:, :, 0], ALU.subtract).then_inc(S["gap"], 1)
                dve.wait_ge(S["gap"], 1)
                link(dve.tensor_copy(idx[:, :].rearrange("p (q s) -> p q s", s=2),
                                     ix8[:, :].rearrange("p (q k) -> p q k", k=8)[:, :, 0:2]))
                for i in range(copies):
                    ins = dve.tensor_tensor(oh.rearrange("p (m i e) -> p m i e", i=copies, e=64)[:, :, i, :],
                                            spread(iota, 1, 8), spread(idx[:, :], 2, 64), ALU.is_equal)
                ins.then_inc(S["oh"], 1)
                dve.wait_ge(S["egap"], 1)
                link(dve.tensor_scalar(den[:, :], egap[:, :], 1.0, None, ALU.add))
                p2 = pr[:, :].rearrange("p (q s) -> p q s", s=2)
                link(dve.reciprocal(p2[:, :, 0], den[:, :]))
                link(dve.tensor_tensor(p2[:, :, 1], p2[:, :, 0], egap[:, :], ALU.mult))

            route(ru, lg_up, 3, oh_up, 2)
            prq = pr[:, :].rearrange("p (k x s) -> p k x s", k=2, x=2)
            for x in range(2):
                ins = dve.tensor_copy(prb_up[:, x * 128:(x + 1) * 128].rearrange("p (k s i) -> p k s i", k=2, s=2),
                                      spread(prq[:, :, x, :], 3, 32))
            ins.then_inc(ru["prb"], 1)
            dve.wait_ge(ru["oh_pe"], 1)
            dve.tensor_copy(oh_up_T[:, 512:1024].rearrange("p (s P x) -> p s x P", s=2, x=2),
                            banks[:, 5, :].rearrange("p (s x P) -> p s x P", s=2, x=2)).then_inc(ru["ohT_d"], 1)
            dve.wait_ge(ru["pb_pe"], 1)
            dve.tensor_copy(prob[:, 0:256].rearrange("p (P x) -> p x P", x=2),
                            banks[:, 6, 0:256].rearrange("p (x P) -> p x P", x=2)).then_inc(ru["pb"], 1)
            for u in range(1, 32, 2):
                dve.wait_ge(g_pe, u + 1)
                if u == 17:
                    dve.wait_ge(down_bias, CHUNKS)
                dst = (g_b if u < 16 else g_a)[:, :].rearrange("p (m c) -> p c m", c=64)
                dve.tensor_copy(dst[:, 4 * (u % 16):4 * (u % 16) + 4, :],
                                banks[:, 2 * (u % 4):2 * (u % 4) + 2, :].rearrange("p b (c m) -> p (b c) m", c=2)
                                ).then_inc(g_dve, 1)

            dve.wait_ge(ru["pb"], 1)
            dve.wait_ge(router_in, 16 * 4)
            for j in range(TILES + 1):
                t = j
                if t < TILES:
                    dve.wait_ge(s1_pe, t + 1)
                    if t >= 2:
                        dve.wait_ge(s2_pe, t - 1)
                    for k in range(2):
                        part = slice(64 * k, 64 * k + 64)
                        ins = dve.tensor_tensor(
                            t_bd(t).rearrange("p (m k c) -> p m k c", m=8, k=2)[part, :, k, :],
                            banks[part, t % 3, :].rearrange("p (m c) -> p m c", m=8),
                            spread(prob[part, t * 8:(t + 1) * 8], 2, 64), ALU.mult)
                    ins.then_inc(tbd_ready, 1)
                t = j - 1
                if t >= 0:
                    dve.wait_ge(s2_pe, t + 1)
                    dve.scalar_tensor_tensor(
                        h_all[:, t * 512:(t + 1) * 512].rearrange("p (m c) -> p m c", c=64),
                        banks[:, 3 + t % 3, :].rearrange("p (m c) -> p m c", c=64), gate[:, 4:5],
                        spread(bup[:, :], 1, 8), ALU.mult, ALU.add).then_inc(hb_ready, 1)

            for part in range(2):
                for x in range(2):
                    dve.wait_ge(split_act, SPLIT + 2 * part + x + 1)
                    raw = raw_dn[64 * x:64 * x + 64, :].rearrange("p (m i) -> p m i", m=64)
                    v = dn_part[part].rearrange("p (m x i) -> p m x i", m=64, x=2)
                    dve.tensor_tensor(raw, raw, v[64 * x:64 * x + 64, :, x, :], ALU.subtract
                                      ).then_inc(split_dve, 1)

            route(rd, lg_dn, 7, oh_dn, 1)
            link(dve.tensor_scalar(pr[:, :], pr[:, :], gate[:, 5:6], tgate[:, 2:3], ALU.mult, ALU.mult))
            dve.tensor_copy(prb_dn.rearrange("p (m c) -> p m c", c=64), spread(pr[:, :], 2, 64)).then_inc(rd["prb"], 1)
            dve.wait_ge(rd["oh_pe"], 2)
            dve.tensor_copy(oh_b_T.rearrange("p (s m q) -> p q s m", s=2, q=4),
                            banks[:, 1, :].rearrange("p (q s m) -> p q s m", q=4, s=2)).then_inc(rd["ohT_d"], 1)
            dve.wait_ge(rd["pb_pe"], 1)
            dve.tensor_copy(prob[:, :].rearrange("p (m g) -> p g m", g=8),
                            banks[:, 2, :].rearrange("p (g m) -> p g m", g=8)).then_inc(rd["pb"], 1)
            dve.wait_ge(split_zero, 4)
            dve.wait_ge(rd["pb"], 1)
            for k in range(4):
                for v in range(8):
                    dve.wait_ge(da_pe, 8 * k + v + 1)
                    dst = a_bd.rearrange("p (m x s o) -> p o s m x", m=64, x=2, s=2)
                    src = banks[:, v % 4, :].rearrange("p (o s m) -> p o s m", o=4, s=2)
                    dve.tensor_copy(dst[64:128, 4 * v:4 * v + 4, :, :, 1], src[64:128]).then_inc(da_dve, 1)
                for v in range(1, 8, 2):
                    dve.wait_ge(db_pe, 8 * k + v + 1)
                    dst = b_nat.rearrange("p (m s o) -> p o s m", m=64, s=2)
                    src = banks[:, v % 4, :].rearrange("p (o s m) -> p o s m", o=4, s=2)
                    dve.tensor_copy(dst[:, 4 * v:4 * v + 4, :, :], src).then_inc(db_dve, 1)
                    if k >= 2:
                        pair = (2 * (k - 2), 2 * (k - 2) + 1)
                        if v < 5:
                            dve.wait_ge(x2, CHUNK * (pair[v // 2] + 1))
                            half_statistics(pair[v // 2], v // 2)
                        elif v == 5:
                            statistics(pair, att[1]["stats"], k - 1, half_done=True)
                for j in range(9):
                    t = 8 * k + j
                    if j < 8:
                        dve.wait_ge(d1_pe, t + 1)
                        if t >= 2:
                            dve.wait_ge(d2_pe, t - 1)
                        for c in range(2):
                            part = slice(64 * c, 64 * c + 64)
                            ins = dve.tensor_tensor(
                                u_bd(t).rearrange("p (m c o) -> p m c o", m=16, c=2)[part, :, c, :],
                                banks[part, 4 + t % 2, :].rearrange("p (m o) -> p m o", m=16),
                                spread(prob[part, t * 16:(t + 1) * 16], 2, 32), ALU.mult)
                        ins.then_inc(ubd_ready, 1)
                    t = 8 * k + j - 1
                    if j >= 1:
                        dve.wait_ge(d2_pe, t + 1)
                        if t >= 4:
                            dve.wait_ge(x2, t - 3)
                        dve.transpose(y_r(t), banks[:, 6 + t % 2, 0:128].rearrange(
                            "p (n r b) -> p b n r", n=4, b=4)).then_inc(y_rows, 1)
                    if k == 3 and j in ATT1_EARLY:
                        attention_step(1, ATT1_EARLY[j])

            m16 = lambda ap: ap.rearrange("p (m c) -> p m c", c=LR)
            parts = lambda i: l_parts.rearrange("p (m six c) -> p m six c", m=2 * CHUNK, six=6)[:, :, i, :]

            def ff_front(j):
                k = j - 1
                if here(k):
                    dve.wait_ge(ff["proj_pe"], k + 1)
                    pk = proj(k).rearrange("p (t c) -> p t c", c=PROJ)
                    pp = banks[:, 1, 0:CHUNK * PROJ].rearrange("p (t c) -> p t c", c=PROJ)
                    dve.tensor_tensor(pk[:, :, 0:LORA_E], pp[:, :, 0:LORA_E],
                                      spread(row_c[:, 256:260], 1, CHUNK), ALU.add)
                    dve.tensor_copy(pk[:, :, LORA_E:PROJ], pp[:, :, LORA_E:PROJ]).then_inc(ff["proj"], 1)
                    dve.wait_ge(ff["proj"], k + 1)
                    lg = pk[:, :, 0:LORA_E]
                    low = pk[:, :, LORA_E:PROJ].rearrange("p t (e r) -> p t e r", e=LORA_E)
                    e3 = lambda ap: ap.rearrange("p (t e) -> p t e", e=LORA_E)
                    pair = lambda ap: ap.rearrange("p (t e f) -> p t e f", e=LORA_E, f=LORA_E)
                    link(dve.tensor_reduce(r_max, lg, AX_X, ALU.max))
                    dve.tensor_tensor(e3(r_sh), lg, spread(r_max, 2, LORA_E), ALU.subtract).then_inc(ff["exp_in"], 1)
                    other, own = spread(lg, 2, LORA_E), spread(lg, 3, LORA_E)
                    dve.tensor_tensor(pair(r_gt), other, own, ALU.is_gt)
                    link(dve.tensor_tensor(pair(r_eq), other, own, ALU.is_equal))
                    link(dve.tensor_tensor(pair(r_eq), pair(r_eq),
                                           spread(tri.rearrange("p (e f) -> p e f", f=LORA_E), 1, CHUNK), ALU.mult))
                    link(dve.tensor_tensor(r_gt, r_gt, r_eq, ALU.add))
                    link(dve.tensor_reduce(e3(r_rank), pair(r_gt), AX_X, ALU.add))
                    mask = r_mask.rearrange("p (t s e) -> p t s e", s=2, e=LORA_E)
                    link(dve.tensor_tensor(mask, spread(e3(r_rank), 2, 2),
                                           spread(spread(slot_id, 1, CHUNK), 3, LORA_E), ALU.is_equal))
                    if k >= 1:
                        dve.wait_ge(ff["parts"], k)
                    lo4 = l_low.rearrange("p (v t e r) -> p v t e r", v=2, t=CHUNK, e=LORA_E)
                    for s in range(2):
                        ins = dve.tensor_tensor(lo4[:, s], low, spread(mask[:, :, s, :], 3, LORA_R), ALU.mult)
                    link(ins)
                    dve.tensor_tensor(l_low[:, 64:128], l_low[:, 64:128], l_low[:, 0:64],
                                      ALU.subtract).then_inc(ff["low"], 1)
                    dve.wait_ge(ff["exp"], k + 1)
                    link(dve.tensor_tensor(e3(r_pick), mask[:, :, 1, :], e3(r_exp), ALU.mult))
                    if k >= 1:
                        dve.wait_ge(ff["ratio_pe"], k)
                    dve.tensor_reduce(r_ratio, e3(r_pick), AX_X, ALU.add).then_inc(ff["ratio_w"], 1)
                    link(dve.tensor_reduce(r_sum, e3(r_exp), AX_X, ALU.add))
                    link(dve.reciprocal(r_inv, r_sum))
                    link(dve.tensor_scalar(r_w0(k), r_inv, tgate[:, 3:4], None, ALU.mult))

            def ff_back(j):
                k = j - 1
                if here(k):
                    dve.wait_ge(ff["hi"], k + 1)
                    dve.tensor_tensor(m16(l_rest), m16(l_low), parts(0), ALU.subtract).then_inc(ff["rest"], 1)
                k = j - 3
                if here(k):
                    dve.wait_ge(ff["o_pe"], k + 1)
                    for i in range(CHUNK):
                        xt = x_res[:, k * W + i * D:k * W + (i + 1) * D]
                        ins = dve.scalar_tensor_tensor(xt, banks[:, 7, i * D:(i + 1) * D], r_w0(k)[:, i:i + 1], xt,
                                                       ALU.mult, ALU.add)
                    ins.then_inc(ff["y"], 1)
                k = j - 2
                if here(k):
                    dve.wait_ge(ff["ratio"], k + 1)
                    for fc in range(FC):
                        dve.wait_ge(ff["z2_pe"], FC * k + fc + 1)
                        if k >= 1 and fc == 0:
                            dve.wait_ge(ff["h"], FC * k)
                        dve.scalar_tensor_tensor(h2_s[:, fc * W:(fc + 1) * W], banks[:, 4 + (FC * k + fc) % 3, :],
                                                 0.0, ratio_T, ALU.max, ALU.mult).then_inc(ff["h2"], 1)
                        if here(k + 1) and fc == 0:
                            dve.wait_ge(ff["mid"], k + 2)
                            dve.tensor_tensor(m16(l_rest), m16(l_rest), parts(1), ALU.subtract
                                              ).then_inc(ff["rest"], 1)
                elif k == -1:
                    dve.wait_ge(ff["mid"], 1)
                    dve.tensor_tensor(m16(l_rest), m16(l_rest), parts(1), ALU.subtract).then_inc(ff["rest"], 1)
                if j in (1, 2):
                    dve.wait_ge(att[1]["x"], 2 * j + 4)
                    statistics((2 * j + 2, 2 * j + 3), ff["stats"], j + 2)

            for j in ATT_STEPS[1]:
                if j >= len(ATT1_EARLY):
                    attention_step(1, j)
                if j == CHUNKS - 1:
                    ff_front(0)
                    ff_back(0)
                if j == CHUNKS:
                    ff_front(1)
                if j == CHUNKS + 2:
                    ff_back(1)
            for j in FF_STEPS[2:]:
                ff_front(j)
                ff_back(j)

        @block.tensor
        def _(pe):
            def tiles4(fn):
                for i in range(CHUNK):
                    ins = fn(slice(i * D, (i + 1) * D))
                return ins

            def keep_clock(n, bank=7):
                for i in range(n):
                    pe.matmul(banks[:, bank, 0:128], ident_b[:, :], ident_b[:, :], start=True, stop=True)

            def transpose4(bank, src):
                return tiles4(lambda c: pe.transpose(banks[:, bank, c], src[:, c], ident))

            def router_up(k0, k1):
                if k0 == 0:
                    pe.wait_ge(router_in, 16 * 4)
                    pe.wait_ge(att[0]["k"], CHUNKS)
                pe.wait_ge(m_lnT, k1)
                tok = lnT_all.rearrange("p (n r) -> p n r", r=8)
                n = slice(k0 * 64, k1 * 64)
                for r in range(8):
                    ins = pe.matmul(banks[0:64, 2, n], wu[:, r * 64:(r + 1) * 64], tok[:, n, r],
                                    start=(r == 0), stop=(r == 7))
                ins.then_inc(ru["log_pe"], 1)

            def attention_step(L, j):
                S = att[L]
                k = j - 2
                if here(k):
                    pe.wait_ge(S["k"], k + 1)
                    pe.wait_ge(S["q"], k + 1)
                    if k >= 1:
                        pe.wait_ge(S["s_ev"], k)
                    tiles4(lambda c: pe.matmul(banks[:, 4, c], qT_s(L, k)[:, c], kT_s(L, k)[:, c],
                                               start=True, stop=True)).then_inc(S["s_pe"], 1)
                k = j - 3
                if here(k):
                    pe.wait_ge(S["prob"], k + 1)
                    if k >= 1:
                        pe.wait_ge(S["pt"], k)
                    transpose4(5, prob_s(L, k)).then_inc(S["pt_pe"], 1)
                k = j
                if here(k):
                    pe.wait_ge(ctx_in_sem[k % 4], 16 * (2 * L + k // 4 + 1))
                    if k == 0:
                        pe.wait_ge(consts_in, 16)
                    if k >= 1:
                        pe.wait_ge(S["ctxT"], k)
                    if L == 0 and here(k - 6):
                        pe.wait_ge(m_lnT, k - 5)
                    transpose4(0, ctx_ring(L, k)).then_inc(S["ctxT_pe"], 1)
                    pe.wait_ge(S["ln"], k + 1)
                    if k >= 1:
                        pe.wait_ge(S["lnT"], k)
                    transpose4(1, ln_s(L, k)).then_inc(S["lnT_pe"], 1)
                if L == 0 and j == 0:
                    pe.wait_ge(weights_in, 16)
                    pe.wait_ge(bv_ready, 1)
                    pe.matmul(banks[:, 7, 0:128], wv0, wff_t, start=True, stop=True)
                    pe.matmul(banks[:, 7, 128:256], vff_tmp[:, 0:128], wff_t, start=True,
                              stop=True).then_inc(vff_pe, 1)
                k = j - 3
                if here(k):
                    pe.wait_ge(S["pt"], k + 1)
                    if k >= 1:
                        pe.wait_ge(S["u"], k)
                    tiles4(lambda c: pe.matmul(banks[:, 6, c], ctx_ring(L, k)[:, c], pT_s(L, k)[:, c],
                                               start=True, stop=True)).then_inc(S["u_pe"], 1)
                k = j - 1
                if here(k):
                    pe.wait_ge(S["ctxT"], k + 1)
                    if k >= 1:
                        pe.wait_ge(S["k"], k)
                    pe.matmul(banks[:, 2, :], wk[L], ctxT_s(L, k), start=True, stop=True).then_inc(S["k_pe"], 1)
                    pe.wait_ge(S["lnT"], k + 1)
                    if k >= 1:
                        pe.wait_ge(S["q"], k)
                    pe.matmul(banks[:, 3, :], wq[L], lnT_s(L, k), start=True, stop=True).then_inc(S["q_pe"], 1)
                k = j - 5
                if L == 0 and here(k):
                    pe.wait_ge(m_ln, k + 1)
                    pe.wait_ge(S["ctxT"], min(j + 1, CHUNKS))
                    if k >= 1:
                        pe.wait_ge(m_lnT, k)
                    transpose4(0, mln_s(k)).then_inc(m_lnT_pe, 1)
                k = j - 3
                if here(k):
                    pe.wait_ge(S["u"], k + 1)
                    if L == 0 and k == 0:
                        pe.wait_ge(vff_ready, 1)
                        pe.wait_ge(bias_ready, 2)
                    if k >= 1:
                        pe.wait_ge(S["x"], k)
                    tiles4(lambda c: pe.matmul(banks[:, 7, c], uT_s(L, k)[:, c], wout[L],
                                               start=True, stop=True)).then_inc(S["o_pe"], 1)
                if L == 0 and j == CHUNKS + 1:
                    router_up(0, 4)
                if L == 0 and j == CHUNKS + 3:
                    router_up(4, 6)
                if L == 0 and j == CHUNKS + 4:
                    keep_clock(KEEP_TAIL, 3)
                    router_up(6, 7)
                    keep_clock(KEEP_TAIL, 3)

            for j in ATT_STEPS[0]:
                attention_step(0, j)

            router_up(7, 8)
            pe.wait_ge(ru["log"], 1)
            for q in range(4):
                ins = pe.transpose(banks[:, 3, q * 64:(q + 1) * 64], logT_up[:, q * 128:(q + 1) * 128], ident[0:64, 0:64])
            ins.then_inc(ru["lgT_pe"], 1)
            pe.wait_ge(att[0]["x"], CHUNKS)
            pe.wait_ge(ident_b_ready, 1)
            keep_clock(KEEP_UP)
            pe.wait_ge(ru["oh"], 1)
            pe.wait_ge(ident_b_ready, 1)
            oh = oh_up.rearrange("p (k x s e) -> p k x s e", k=2, x=2, s=2)
            for k in range(2):
                for s in range(2):
                    for x in range(2):
                        c = (s * 2 + x) * 128
                        ins = pe.matmul(banks[:, 4 + k, c:c + 128], oh[:, k, x, s, :],
                                        ident_b[:, :], start=True, stop=True)
            ins.then_inc(ru["oh_pe"], 1)
            pe.wait_ge(ru["prb"], 1)
            for x in range(2):
                ins = pe.matmul(banks[:, 6, x * 128:(x + 1) * 128], prb_up[:, x * 128:(x + 1) * 128], ident,
                                start=True, stop=True)
            ins.then_inc(ru["pb_pe"], 1)
            keep_clock(KEEP_UP2)
            pe.wait_ge(ru["ohT_a"], 1)
            pe.wait_ge(ru["ohT_d"], 1)
            pe.wait_ge(ru["pb"], 1)
            pe.wait_ge(tables_up, 1)
            pe.wait_ge(split_act, SPLIT)
            for u in range(32):
                if u >= 4:
                    pe.wait_ge(g_act if u % 2 == 0 else g_dve, (u - 4) // 2 + 1)
                tb = u // 16
                for ci in range(4):
                    col = 4 * (u % 16) + ci
                    for g in range(4):
                        o = banks[32 * g:32 * g + 32, 2 * (u % 4) + ci // 2, (ci % 2) * 256:(ci % 2) * 256 + 256]
                        rhs = oh_up_T[:, g * 256:(g + 1) * 256]
                        pe.matmul(o, up_hm[tb][:, col * 32:(col + 1) * 32], rhs, start=True, stop=False)
                        ins = pe.matmul(o, up_lo[tb][:, col * 32:(col + 1) * 32], rhs, start=False, stop=True)
                ins.then_inc(g_pe, 1)
            for j in range(TILES + 1):
                t = j
                if t == 0:
                    pe.wait_ge(g_act, 15)
                if t == 2:
                    pe.wait_ge(g_dve, 15)
                if t < TILES:
                    pe.wait_ge(xbd_ready, t + 1)
                    pe.wait_ge(xbd_pool, t + 1)
                    if t >= 3:
                        pe.wait_ge(tbd_ready, t - 2)
                    for k in range(2):
                        for m in range(8):
                            ins = pe.matmul(banks[64 * k:64 * k + 64, t % 3, m * 64:(m + 1) * 64],
                                            x_bd(t)[:, m * 128 + k * 64:m * 128 + k * 64 + 64],
                                            g_b[:, t * 512 + m * 64:t * 512 + (m + 1) * 64], start=True, stop=True)
                    ins.then_inc(s1_pe, 1)
                t = j - 1
                if t >= 0:
                    pe.wait_ge(tbd_ready, t + 1)
                    if t == 0:
                        pe.wait_ge(g_act, 16)
                        pe.wait_ge(g_dve, 16)
                    if t >= 3:
                        pe.wait_ge(hb_ready, t - 2)
                    for m in range(8):
                        n, x = m // 2, m % 2
                        ins = pe.matmul(banks[64 * x:64 * x + 64, 3 + t % 3, n * 128:(n + 1) * 128],
                                        g_a[:, t * 512 + m * 64:t * 512 + (m + 1) * 64],
                                        t_bd(t)[:, m * 128:(m + 1) * 128], start=True, stop=True)
                    ins.then_inc(s2_pe, 1)

            pe.wait_ge(h_ready, TILES)
            pe.wait_ge(wd_in, 32)
            pe.wait_ge(wd_zero, 8)
            hp = h_all[:, :].rearrange("p (m c) -> p m c", c=64)
            for c in range(64):
                ins = pe.matmul(banks[:, 6, 0:256], wd_bd[:, c * 128:(c + 1) * 128], hp[:, :, c],
                                start=(c == 0), stop=(c == 63))
            ins.then_inc(rd["log_pe"], 1)
            pe.wait_ge(rd["log"], 1)
            lt2 = logT_dn.rearrange("p (P k) -> p P k", k=2)
            for k in range(2):
                ins = pe.transpose(banks[:, 7, k * 128:(k + 1) * 128], lt2[:, :, k], ident)
            ins.then_inc(rd["lgT_pe"], 1)
            keep_clock(KEEP_DOWN, 5)
            pe.wait_ge(rd["oh"], 1)
            oh = oh_dn.rearrange("p (k x s e) -> p k x s e", k=2, x=2, s=2)
            for k in range(2):
                for s in range(2):
                    for x in range(2):
                        c = (k * 2 + s) * 128
                        ins = pe.matmul(banks[64 * x:64 * x + 64, 0, c:c + 128], oh[:, k, x, s, :], ident_b[:, :],
                                        start=True, stop=True)
            ins.then_inc(rd["oh_pe"], 1)
            ohq = oh_dn.rearrange("p (m e) -> p m e", e=64)
            par = lambda ap, c: ap.rearrange("p (m c) -> p m c", c=2)[:, :, c]
            for m in range(8):
                for c in range(2):
                    ins = pe.matmul(banks[64 * c:64 * c + 64, 1, m * 64:(m + 1) * 64], ohq[:, m, :],
                                    par(ident_b[:, :], c), start=True, stop=True)
            ins.then_inc(rd["oh_pe"], 1)
            pe.wait_ge(rd["prb"], 1)
            for m in range(8):
                for c in range(2):
                    ins = pe.matmul(banks[64 * c:64 * c + 64, 2, m * 64:(m + 1) * 64],
                                    prb_dn[:, m * 64:(m + 1) * 64], par(ident, c), start=True, stop=True)
            ins.then_inc(rd["pb_pe"], 1)
            keep_clock(KEEP_DOWN2)
            pe.wait_ge(rd["ohT_a"], 1)
            pe.wait_ge(rd["ohT_d"], 1)
            pe.wait_ge(rd["pb"], 1)
            pe.wait_ge(split_act, SPLIT + 6)
            pe.wait_ge(split_zero, 4)
            part = [v.rearrange("p (tb o c) -> p tb o c", tb=2, o=32) for v in dn_part]

            def gather(k, units):
                for tb, v in units:
                    ohT = (oh_a_T if tb == 0 else oh_b_T).rearrange("p (s m) -> p s m", s=2)[:, :, 64 * k:64 * k + 64]
                    if tb == 1 and v >= 4:
                        pe.wait_ge(db_act if v % 2 == 0 else db_dve, 4 * k + (v - 4) // 2 + 1)
                    elif tb == 1 or v >= 4:
                        n = 8 * k + (v - 4) % 8 + 1
                        pe.wait_ge(da_act, n)
                        pe.wait_ge(da_dve, n)
                    elif k >= 1:
                        pe.wait_ge(db_act if v % 2 == 0 else db_dve, 4 * (k - 1) + (v + 4) // 2 + 1)
                    for oi in range(4):
                        for i in range(3):
                            ins = pe.matmul(banks[:, v % 4, oi * 128:(oi + 1) * 128],
                                            part[i][:, tb, 4 * v + oi, :], ohT, start=(i == 0), stop=(i == 2))
                    ins.then_inc(da_pe if tb == 0 else db_pe, 1)

            early = [(0, v) for v in range(4)]
            later = [(0, v) for v in range(4, 8)] + [(1, v) for v in range(8)]
            gather(0, early)
            for k in range(4):
                gather(k, later)
                pe.wait_ge(da_act, 8 * k + 8)
                pe.wait_ge(da_dve, 8 * k + 8)
                for j in range(9):
                    t = 8 * k + j
                    if j < 8:
                        if t >= 2:
                            pe.wait_ge(ubd_ready, t - 1)
                        for n4h in range(2):
                            for k2 in range(2):
                                for c in range(2):
                                    m = (n4h * 2 + c) * 2 + k2
                                    o = (n4h * 2 + k2) * 128
                                    ins = pe.matmul(banks[64 * c:64 * c + 64, 4 + t % 2, o:o + 128],
                                                    h_all[:, t * 512 + m * 64:t * 512 + (m + 1) * 64],
                                                    a_bd[:, (j * 8 + m) * 128:(j * 8 + m + 1) * 128],
                                                    start=True, stop=True)
                        ins.then_inc(d1_pe, 1)
                    elif k < 3:
                        gather(k + 1, early)
                    t = 8 * k + j - 1
                    if j >= 1:
                        if j == 1:
                            pe.wait_ge(db_act, 4 * k + 4)
                            pe.wait_ge(db_dve, 4 * k + 4)
                        pe.wait_ge(ubd_ready, t + 1)
                        if t >= 2:
                            pe.wait_ge(y_rows, t - 1)
                        for n4h in range(2):
                            for q in range(4):
                                for s in range(2):
                                    m = n4h * 4 + q
                                    at = (((j - 1) * 8 + m) * 2 + s) * 32
                                    ins = pe.matmul(banks[32 * q:32 * q + 32, 6 + t % 2, n4h * 64:(n4h + 1) * 64],
                                                    b_nat[:, at:at + 32],
                                                    u_bd(t)[:, (m * 2 + s) * 64:(m * 2 + s + 1) * 64],
                                                    start=(s == 0), stop=(s == 1))
                        ins.then_inc(d2_pe, 1)
                    if k == 3 and j in ATT1_EARLY:
                        attention_step(1, ATT1_EARLY[j])

            def ff_front(j):
                if j == 0:
                    pe.wait_ge(lora_in, 16 * 9)
                    pe.wait_ge(att[1]["ctxT"], CHUNKS)
                    pe.wait_ge(att[1]["lnT"], CHUNKS)
                k = j
                if here(k):
                    pe.wait_ge(ff["ln"], k + 1)
                    if k >= 1:
                        pe.wait_ge(ff["lnT"], k)
                    transpose4(0, f_ln(k)).then_inc(ff["lnT_pe"], 1)
                k = j - 3
                if here(k):
                    if k >= 1:
                        pe.wait_ge(ff["y"], k)
                    for i in range(CHUNK):
                        for fc in range(FC):
                            if i == 0:
                                pe.wait_ge(ff["h"], FC * k + fc + 1)
                            ins = pe.matmul(banks[:, 7, i * D:(i + 1) * D],
                                            h_s(k)[:, fc * W + i * D:fc * W + (i + 1) * D],
                                            wo_s[:, fc * 128:(fc + 1) * 128], start=(fc == 0), stop=(fc == FC - 1))
                    ins.then_inc(ff["o_pe"], 1)
                k = j - 2
                if here(k):
                    pe.wait_ge(ff["lora"], k + 1)
                    lv = lora_T(k).rearrange("p (v m) -> p v m", v=2)

                    def slot0(fc, k=k, lv=lv):
                        n = FC * k + fc
                        f = slice(fc * 128, (fc + 1) * 128)
                        if n >= 3:
                            pe.wait_ge(ff["h2"], n - 2)
                        pe.matmul(banks[:, 4 + n % 3, :], wi_s[:, f], f_lnT(k), start=True, stop=False)
                        pe.matmul(banks[:, 4 + n % 3, :], lb_part[:, f], lv[:, 0, :], start=False, stop=True,
                                  ).then_inc(ff["z1_pe"], 1)

                    def slot1(fc, k=k, lv=lv):
                        n = FC * k + fc
                        f = slice(fc * 128, (fc + 1) * 128)
                        pe.wait_ge(ff["h1"], n + 1)
                        pe.matmul(banks[:, 4 + n % 3, :], lb_part[:, f], lv[:, 1, :], start=False, stop=True,
                                  skip_group_check=True).then_inc(ff["z2_pe"], 1)

                    slot0(0)
                    slot0(1)
                    slot1(0)
                    slot0(2)
                    slot1(1)
                    slot0(3)
                    slot1(2)
                k = j
                if here(k):
                    pe.wait_ge(ff["lnT"], k + 1)
                    if k >= 1:
                        pe.wait_ge(ff["proj"], k)
                    for i in range(CHUNK):
                        ins = pe.matmul(banks[:, 1, i * PROJ:(i + 1) * PROJ], f_lnT(k)[:, i * D:(i + 1) * D],
                                        wga_s, start=True, stop=True)
                    ins.then_inc(ff["proj_pe"], 1)
                if here(j - 2):
                    slot1(3)

            def ff_back(j):
                k = j - 1
                if here(k):
                    pe.wait_ge(ff["ratio_w"], k + 1)
                    if k >= 1:
                        pe.wait_ge(ff["ratio"], k)
                    for i in range(CHUNK):
                        ins = pe.matmul(banks[:, 3, i * D:(i + 1) * D],
                                        r_ratio[:, i:i + 1].broadcast_to([128, 128]), ident, start=True, stop=True)
                    ins.then_inc(ff["ratio_pe"], 1)
                    pe.wait_ge(ff["parts"], k + 1)
                    if k >= 1:
                        pe.wait_ge(ff["lora"], k)
                    lp = l_parts.rearrange("p (m c) -> p m c", m=2 * CHUNK)
                    lb = banks[0:96, 2, :].bitcast(BF16).rearrange("p (m c) -> p m c", m=2 * CHUNK)
                    for m in range(2 * CHUNK):
                        ins = pe.transpose(lb[:, m, :], lp[:, m, :], ident_b[:, :])
                    ins.then_inc(ff["lora_pe"], 1)

            for j in ATT_STEPS[1]:
                if j >= len(ATT1_EARLY):
                    attention_step(1, j)
                if j == CHUNKS - 1:
                    ff_front(0)
                    ff_back(0)
                if j == CHUNKS:
                    ff_front(1)
                if j == CHUNKS + 2:
                    ff_back(1)
            pe.wait_ge(ff["lb"], 1)
            for n in ("s_ev", "pt", "u", "x"):
                pe.wait_ge(att[1][n], CHUNKS)
            for j in FF_STEPS[2:]:
                ff_front(j)
                ff_back(j)


def kernel(**inputs):
    import numpy as np
    import concourse.bacc as bacc
    from concourse import mybir as _mybir
    from concourse.bass_utils import run_bass_kernel_spmd

    v = {k: np.asarray(a) for k, a in inputs.items()}
    f32 = np.float32
    r = np.arange(128)
    same = (r[:, None] // 64) == (r[None, :] // 64)
    e4 = np.arange(4)
    consts = np.zeros((128, 472), f32)
    consts[:, 0:128] = np.eye(128, dtype=f32)
    consts[:, 128:256] = np.where(same & (r[None, :] <= r[:, None]), 0.0, -1e30)
    consts[:, 256:384] = np.where(same, 0.0, -1e30)
    consts[:, 384:448] = np.arange(64)
    consts[:, 448:464] = (e4[None, :] < e4[:, None]).reshape(-1)
    consts[:, 464:466] = np.arange(2)
    place = r[:96] // 16
    for c, places in enumerate(((0, 1, 5), (2, 3), (4,))):
        consts[:96, 466 + c] = np.isin(place, places)

    def t(name):
        return v[name].T

    arrays = {
        "x": v["x"].reshape(TILES, 128, D),
        "ctx": v["ctx_1024"].reshape(TILES, 128, D),
        "consts": consts,
        "gates": np.concatenate([v["g_xattn"], v["g_ffn"], v["L0_ffn_scale_up"], v["L0_ffn_scale_down"]])[None, :],
        "rows": np.concatenate([v["L0_xattn_bff"], v["L1_xattn_bv"], v["L1_ffn_bg"]])[None, :],
        "cols": np.stack([v["L0_xattn_bq"], v["L0_xattn_bk"], v["L0_xattn_bv"], v["L1_xattn_bq"],
                          v["L1_xattn_bk"]], axis=1),
        "attn_w": np.concatenate([t("L0_xattn_Wq"), t("L0_xattn_Wk"), t("L0_xattn_Wff"), v["L0_xattn_Wv"],
                                  t("L1_xattn_Wq"), t("L1_xattn_Wk"), t("L1_xattn_Wv")], axis=1),
        "w_up_router": v["L0_ffn_W_up"].reshape(64, 8, 128).transpose(2, 1, 0).reshape(128, 512),
        "w_down_router": v["L0_ffn_W_down"].reshape(64, 64, 64).transpose(1, 2, 0),
        "a_up": v["L0_ffn_A_up"].reshape(64, 64, 8, 4).transpose(0, 1, 3, 2).reshape(64, 2048),
        "b_up": v["L0_ffn_B_up"].reshape(64, 2048),
        "a_down": v["L0_ffn_A_down"].reshape(64, 2048),
        "b_down": v["L0_ffn_B_down"].reshape(64, 2048),
        "bias_up": v["L0_ffn_bias_up"].reshape(64, 64),
        "bias_down": np.tile(v["L0_ffn_bias_down"].reshape(8, 128), (16, 1)),
        "wi_t": t("L1_ffn_Wi"),
        "wo_t": v["L1_ffn_Wo"].T.reshape(FC, 128, D).transpose(1, 0, 2).reshape(128, FC * D),
        "wg_a": np.concatenate([t("L1_ffn_Wg"), v["L1_ffn_A"].reshape(LR, D).T], axis=1),
        "lora_b": v["L1_ffn_B"].transpose(0, 2, 1).reshape(LR, HIDDEN),
    }
    nc = bacc.Bacc("TRN2", target_bir_lowering=False, num_devices=1)
    feed, args = {}, []
    for name, a in arrays.items():
        a = np.ascontiguousarray(a)
        feed[f"in_{name}"] = a
        args.append(nc.dram_tensor(f"in_{name}", a.shape, _mybir.dt.from_np(a.dtype), kind="ExternalInput").ap())
    res = nc.dram_tensor("out_x", (TILES, 128, D), _mybir.dt.float32, kind="ExternalOutput").ap()
    flamingo_kernel(nc, *args, res)
    got = run_bass_kernel_spmd(nc, [feed], core_ids=[0])
    return got.results[0]["out_x"].reshape(64, 64, D)
```
